# Optimizing a Trainium2 kernel written in Bass

```python
import numpy as np
import jax
import jax.numpy as jnp

def _softmax(x, axis=-1):
    return jax.nn.softmax(x, axis=axis)

def _gelu(x):
    return jax.nn.gelu(x, approximate=True)

def _silu(x):
    return jax.nn.silu(x)

def _sigmoid(x):
    return jax.nn.sigmoid(x)

def _layernorm(x, axis=-1, eps=1e-05):
    m = jnp.mean(x, axis=axis, keepdims=True)
    v = jnp.var(x, axis=axis, keepdims=True)
    return (x - m) / jnp.sqrt(v + eps)

def _scatter_add(tgt, idx, src, axis=0):
    return tgt.at[idx].add(src)

def _segment_sum(src, seg, n):
    return jax.ops.segment_sum(src, seg, n)
kernel_name = 'mk_seq_postln_d2_jaxref_r4_e4bc2f'

def setup_inputs(seed: int=0):
    np.random.seed(seed)
    _w = jnp.asarray

    def _L0_attn_setup():
        import jax, jax.numpy as jnp
        import numpy as np
        SEQ_LEN = 512
        DIM_EMB = 256
        DIM_K = 256
        DIM_V = 256
        BATCH = 4
        key = jax.random.key(seed)
        kx, kq, kk, kv, ko = jax.random.split(key, 5)
        s = DIM_EMB ** (-0.5)
        return {'x': jax.random.normal(kx, (BATCH, SEQ_LEN, DIM_EMB), dtype=jnp.float32), 'Wq': jax.random.normal(kq, (DIM_EMB, DIM_K), dtype=jnp.float32) * s, 'Wk': jax.random.normal(kk, (DIM_EMB, DIM_K), dtype=jnp.float32) * s, 'Wv': jax.random.normal(kv, (DIM_EMB, DIM_V), dtype=jnp.float32) * s, 'Wo': jax.random.normal(ko, (DIM_V, DIM_V), dtype=jnp.float32) * DIM_V ** (-0.5)}
    _L0_attn_in = _L0_attn_setup()

    def _L0_ffn_setup():
        import jax, jax.numpy as jnp
        import numpy as np
        N_EMBD = 256
        NUM_EXPERTS = 8
        TOP_K = 2
        D_FF = 4 * N_EMBD
        B, S = (4, 512)
        key = jax.random.key(seed)
        ks = jax.random.split(key, 7)
        scale = lambda fan_in: 1.0 / np.sqrt(fan_in)
        x = jax.random.normal(ks[0], (B, S, N_EMBD), dtype=jnp.float32)
        W_router = jax.random.normal(ks[1], (N_EMBD, NUM_EXPERTS), dtype=jnp.float32) * scale(N_EMBD)
        b_router = jnp.zeros((NUM_EXPERTS,), dtype=jnp.float32)
        W1 = jax.random.normal(ks[2], (NUM_EXPERTS, N_EMBD, D_FF), dtype=jnp.float32) * scale(N_EMBD)
        b1 = jnp.zeros((NUM_EXPERTS, D_FF), dtype=jnp.float32)
        W2 = jax.random.normal(ks[3], (NUM_EXPERTS, D_FF, N_EMBD), dtype=jnp.float32) * scale(D_FF)
        b2 = jnpp = jnp.zeros((NUM_EXPERTS, N_EMBD), dtype=jnp.float32)
        return {'x': x, 'W_router': W_router, 'b_router': b_router, 'W1': W1, 'b1': b1, 'W2': W2, 'b2': b2}
    _L0_ffn_in = _L0_ffn_setup()

    def _L1_attn_setup():
        import jax, jax.numpy as jnp
        import numpy as np
        B, T, C = (4, 512, 256)
        NQ, D = (8, C // 8)
        key = jax.random.key(seed)
        ks = jax.random.split(key, 6)
        s = 0.02
        return {'x': jax.random.normal(ks[0], (B, T, C), dtype=jnp.float32), 'Wk': jax.random.normal(ks[1], (C, D), dtype=jnp.float32) * s, 'Wv': jax.random.normal(ks[2], (C, D), dtype=jnp.float32) * s, 'Wq': jax.random.normal(ks[3], (NQ, C, D), dtype=jnp.float32) * s, 'Wp': jax.random.normal(ks[4], (NQ * D, C), dtype=jnp.float32) * s, 'bp': jnp.zeros((C,), dtype=jnp.float32)}
    _L1_attn_in = _L1_attn_setup()

    def _L1_ffn_setup():
        import jax, jax.numpy as jnp
        import numpy as np
        D_IN, D_HID = (256, 1024)

        def _ternary(key, shape):
            return jax.random.randint(key, shape, -1, 2).astype(jnp.float32)

        def _tlin(x, w, s):
            return jnp.einsum('bsi,oi->bso', x, w) * s
        key = jax.random.key(seed)
        ks = jax.random.split(key, 12)
        inv = lambda fan: 1.0 / np.sqrt(fan).astype(np.float32)
        return {'x': jax.random.normal(ks[0], (4, 512, D_IN), dtype=jnp.float32), 'w1_w': _ternary(ks[1], (D_HID, D_IN)), 'w1_s': jax.random.uniform(ks[2], (D_HID,), dtype=jnp.float32) * inv(D_IN), 'w2_w': _ternary(ks[3], (D_HID, D_IN)), 'w2_s': jax.random.uniform(ks[4], (D_HID,), dtype=jnp.float32) * inv(D_IN), 'h1_w': _ternary(ks[5], (D_HID, D_HID)), 'h1_s': jax.random.uniform(ks[6], (D_HID,), dtype=jnp.float32) * inv(D_HID), 'h2_w': _ternary(ks[7], (D_HID, D_HID)), 'h2_s': jax.random.uniform(ks[8], (D_HID,), dtype=jnp.float32) * inv(D_HID), 'w3_w': _ternary(ks[9], (D_IN, D_HID)), 'w3_s': jax.random.uniform(ks[10], (D_IN,), dtype=jnp.float32) * inv(D_HID)}
    _L1_ffn_in = _L1_ffn_setup()
    _d = {'L0_attn_x': _L0_attn_in['x'], 'L0_attn_Wq': _L0_attn_in['Wq'], 'L0_attn_Wk': _L0_attn_in['Wk'], 'L0_attn_Wv': _L0_attn_in['Wv'], 'L0_attn_Wo': _L0_attn_in['Wo'], 'L0_ffn_W_router': _L0_ffn_in['W_router'], 'L0_ffn_b_router': _L0_ffn_in['b_router'], 'L0_ffn_W1': _L0_ffn_in['W1'], 'L0_ffn_b1': _L0_ffn_in['b1'], 'L0_ffn_W2': _L0_ffn_in['W2'], 'L0_ffn_b2': _L0_ffn_in['b2'], 'L1_attn_Wk': _L1_attn_in['Wk'], 'L1_attn_Wv': _L1_attn_in['Wv'], 'L1_attn_Wq': _L1_attn_in['Wq'], 'L1_attn_Wp': _L1_attn_in['Wp'], 'L1_attn_bp': _L1_attn_in['bp'], 'L1_ffn_w1_w': _L1_ffn_in['w1_w'], 'L1_ffn_w1_s': _L1_ffn_in['w1_s'], 'L1_ffn_w2_w': _L1_ffn_in['w2_w'], 'L1_ffn_w2_s': _L1_ffn_in['w2_s'], 'L1_ffn_h1_w': _L1_ffn_in['h1_w'], 'L1_ffn_h1_s': _L1_ffn_in['h1_s'], 'L1_ffn_h2_w': _L1_ffn_in['h2_w'], 'L1_ffn_h2_s': _L1_ffn_in['h2_s'], 'L1_ffn_w3_w': _L1_ffn_in['w3_w'], 'L1_ffn_w3_s': _L1_ffn_in['w3_s']}
    _x0 = _d['L0_attn_x']
    _d['L0_attn_x'] = jax.random.normal(jax.random.fold_in(jax.random.key(seed), 1), (4, 1024, 256), dtype=_x0.dtype)
    del _x0
    return _d

def reference(L0_attn_x, L0_attn_Wq, L0_attn_Wk, L0_attn_Wv, L0_attn_Wo, L0_ffn_W_router, L0_ffn_b_router, L0_ffn_W1, L0_ffn_b1, L0_ffn_W2, L0_ffn_b2, L1_attn_Wk, L1_attn_Wv, L1_attn_Wq, L1_attn_Wp, L1_attn_bp, L1_ffn_w1_w, L1_ffn_w1_s, L1_ffn_w2_w, L1_ffn_w2_s, L1_ffn_h1_w, L1_ffn_h1_s, L1_ffn_h2_w, L1_ffn_h2_s, L1_ffn_w3_w, L1_ffn_w3_s):

    def _L0_attn_ref(x, Wq, Wk, Wv, Wo):
        import jax, jax.numpy as jnp
        import numpy as np
        SEQ_LEN = 512
        DIM_EMB = 256
        DIM_K = 256
        DIM_V = 256
        BATCH = 4
        q = jnp.einsum('bse,ek->bsk', x, Wq)
        k = jnp.einsum('bse,ek->bsk', x, Wk)
        v = jnp.einsum('bse,ev->bsv', x, Wv)
        scores = jnp.einsum('bqk,bsk->bqs', q, k)
        S = scores.shape[-1]
        causal_mask = jnp.triu(jnp.ones((S, S), dtype=bool), k=1)
        scores = jnp.where(causal_mask[None], -jnp.inf, scores)
        attn = jax.nn.softmax(scores * Wq.shape[1] ** (-0.5), axis=-1)
        out = jnp.einsum('bqs,bsv->bqv', attn, v)
        return jnp.einsum('bqv,vo->bqo', out, Wo)

    def _L0_ffn_ref(x, W_router, b_router, W1, b1, W2, b2):
        import jax, jax.numpy as jnp
        import numpy as np
        N_EMBD = 256
        NUM_EXPERTS = 8
        TOP_K = 2
        D_FF = 4 * N_EMBD
        B, S = (4, 512)
        Bv, Sv, D = x.shape
        flat_x = x.reshape(-1, D)
        T = flat_x.shape[0]
        logits = flat_x @ W_router + b_router
        top_vals, top_idx = jax.lax.top_k(logits, TOP_K)
        neg_inf = jnp.full_like(logits, -jnp.inf)
        sparse_logits = neg_inf.at[jnp.arange(T)[:, None], top_idx].set(top_vals)
        router_weights = jax.nn.softmax(sparse_logits, axis=-1)
        final_output = jnp.zeros_like(flat_x)
        for e in range(NUM_EXPERTS):
            expert_mask = jnp.any(top_idx == e, axis=-1)
            h = jax.nn.relu(flat_x @ W1[e] + b1[e])
            y = h @ W2[e] + b2[e]
            w = router_weights[:, e] * expert_mask.astype(x.dtype)
            final_output = final_output + y * w[:, None]
        return final_output.reshape(Bv, Sv, D)

    def _L1_attn_ref(x, Wk, Wv, Wq, Wp, bp):
        import jax, jax.numpy as jnp
        import numpy as np
        B, T, C = (4, 512, 256)
        NQ, D = (8, C // 8)
        b, t, c = x.shape
        scale = c ** (-0.5)
        k = x @ Wk
        v = x @ Wv
        q = jnp.einsum('btc,qcd->bqtd', x, Wq)
        wei = jnp.einsum('bqtd,bsd->bqts', q, k) * scale
        causal = jnp.tril(jnp.ones((t, t), dtype=bool))
        wei = jnp.where(causal, wei, -jnp.inf)
        wei = jax.nn.softmax(wei, axis=-1)
        out = jnp.einsum('bqts,bsd->btqd', wei, v)
        out = out.reshape(b, t, -1)
        return out @ Wp + bp

    def _L1_ffn_ref(x, w1_w, w1_s, w2_w, w2_s, h1_w, h1_s, h2_w, h2_s, w3_w, w3_s):
        import jax, jax.numpy as jnp
        import numpy as np
        D_IN, D_HID = (256, 1024)

        def _ternary(key, shape):
            return jax.random.randint(key, shape, -1, 2).astype(jnp.float32)

        def _tlin(x, w, s):
            return jnp.einsum('bsi,oi->bso', x, w) * s
        h = jax.nn.silu(_tlin(x, w1_w, w1_s)) * _tlin(x, w2_w, w2_s)
        h = jax.nn.gelu(_tlin(h, h1_w, h1_s), approximate=False)
        h = jax.nn.gelu(_tlin(h, h2_w, h2_s), approximate=False)
        return _tlin(h, w3_w, w3_s)
    x = L0_attn_x
    x = _layernorm(x + _L0_attn_ref(x, L0_attn_Wq, L0_attn_Wk, L0_attn_Wv, L0_attn_Wo), axis=-1)
    x = _layernorm(x + _L0_ffn_ref(x, L0_ffn_W_router, L0_ffn_b_router, L0_ffn_W1, L0_ffn_b1, L0_ffn_W2, L0_ffn_b2), axis=-1)
    x = _layernorm(x + _L1_attn_ref(x, L1_attn_Wk, L1_attn_Wv, L1_attn_Wq, L1_attn_Wp, L1_attn_bp), axis=-1)
    x = _layernorm(x + _L1_ffn_ref(x, L1_ffn_w1_w, L1_ffn_w1_s, L1_ffn_w2_w, L1_ffn_w2_s, L1_ffn_h1_w, L1_ffn_h1_s, L1_ffn_h2_w, L1_ffn_h2_s, L1_ffn_w3_w, L1_ffn_w3_s), axis=-1)
    return x

_drawn_inputs = setup_inputs


def setup_inputs(seed=0):
    import zlib

    import numpy as np

    out = dict(_drawn_inputs(seed))
    spreads = {'L0_ffn_b_router': (0.0, 0.1),
     'L0_ffn_b1': (0.0, 0.1),
     'L0_ffn_b2': (0.0, 0.1),
     'L1_attn_bp': (0.0, 0.1)}
    factors = {'L1_attn_Wk': 8.0,
     'L1_attn_Wv': 3.481,
     'L1_attn_Wq': 8.0,
     'L1_attn_Wp': 3.486,
     'L1_ffn_w1_w': 8.0,
     'L1_ffn_w1_s': 8.0,
     'L1_ffn_w2_w': 8.0,
     'L1_ffn_w2_s': 8.0,
     'L1_ffn_h1_w': 8.0,
     'L1_ffn_h1_s': 8.0,
     'L1_ffn_h2_w': 8.0,
     'L1_ffn_h2_s': 8.0,
     'L1_ffn_w3_w': 8.0,
     'L1_ffn_w3_s': 8.0}
    for name, (base, spread) in spreads.items():
        noise = np.random.default_rng([zlib.crc32(name.encode()), seed]).standard_normal(out[name].shape)
        drawn = base * np.exp(spread * noise) if base else spread * noise
        out[name] = jnp.asarray(drawn.astype(out[name].dtype))
    for name, factor in factors.items():
        out[name] = (out[name] * factor).astype(out[name].dtype)
    return out
```

```python
from contextlib import ExitStack

import concourse.bass as bass
from concourse import mybir
from concourse.alu_op_type import AluOpType as ALU

F32 = mybir.dt.float32
F32R = mybir.dt.float32r
BF16 = mybir.dt.bfloat16
I32 = mybir.dt.int32
U32 = mybir.dt.uint32
ACT = mybir.ActivationFunctionType
X = mybir.AxisListType.X
P = 128
EPS = 1e-5
PRIMED = 1
UNIT = 256


def prime(nc, semaphores):
    with nc.Block() as block:
        @block.gpsimd
        def _(pool):
            for semaphore in semaphores:
                pool.sem_inc(semaphore, PRIMED)


RSQRT_STEPS = 3
RSQRT_LINKS = 3 + 3 * RSQRT_STEPS


def rsqrt_guess(engine, link, y, v, shifted):
    link(engine.tensor_scalar(v, v, EPS, None, ALU.add))
    link(engine.tensor_scalar(shifted, v.bitcast(I32), 1, None, ALU.logical_shift_right))
    link(engine.tensor_scalar(y.bitcast(I32), shifted, -1, 0x5F3759DF, ALU.mult, ALU.add))


def rsqrt_newton(engine, link, y, v, t):
    for _ in range(RSQRT_STEPS):
        link(engine.tensor_tensor(t, y, v, ALU.mult))
        link(engine.tensor_tensor(t, t, y, ALU.mult))
        link(engine.tensor_scalar(t, t, -0.5, 1.5, ALU.mult, ALU.add))
        link(engine.tensor_tensor(y, t, y, ALU.mult))


def rsqrt(nc, link, y, v, t, shifted):
    rsqrt_guess(nc.vector, link, y, v, shifted)
    for _ in range(RSQRT_STEPS):
        link(nc.vector.scalar_tensor_tensor(t, y, -0.5, v, ALU.mult, ALU.mult))
        link(nc.vector.tensor_tensor(t, t, y, ALU.mult))
        link(nc.vector.scalar_tensor_tensor(y, t, 1.5, y, ALU.add, ALU.mult))


def ffn_phase(nc, flag, x_in, w1, w2, h1, h2, w3, s_cols, s3_row, out, ident_dram, split):
    T, D = x_in.shape
    KD = D // P
    FH = w1.shape[2]
    KF = FH // P
    CH = 512
    NT = CH // P
    PAIRS = T // CH // 2
    WDT = F32R if split else F32
    name = "f" if split else "g"
    with ExitStack() as ctx:
        def sb(n, s, d=F32):
            return ctx.enter_context(nc.sbuf_tensor(name + n, s, d))

        primed = []
        ctx.callback(nc.clear_and_free_semaphores, primed)

        def sem(n):
            primed.append(nc.alloc_semaphore(name + n))
            return primed[-1]

        parts = 2 if split else 1
        w1_sb = sb("w1", [P, KD, FH], WDT)
        w2_sb = sb("w2", [P, KD, FH], WDT)
        h1_sb = sb("h1", [P, KF, FH], WDT)
        h2_sb = sb("h2", [P, KF, FH], WDT)
        w3_sb = sb("w3", [P, KF, D], WDT)
        ident = sb("ident", [P, P])
        scl = sb("scl", [P, 4, KF])
        half = sb("half", [P, 2, KF])
        s3 = sb("s3", [P, D])
        x = sb("x", [P, 2, NT, D])
        xT = [sb(f"xT{q}", [P, KD, CH], WDT) for q in range(parts)]
        ha = [sb(f"ha{q}", [P, KF, CH], WDT) for q in range(parts)]
        hb = [sb(f"hb{q}", [P, KF, CH], WDT) for q in range(parts)]
        t = sb("t", [P, 2, CH])
        a = sb("a", [P, 2, CH])
        g = sb("g", [P, 2, CH])
        z = sb("z", [P, NT, D])
        st = sb("st", [P, NT, 6])
        mv = sb("mv", [P, NT, 2])
        rstd = sb("rstd", [P, NT])
        var = sb("var", [P, NT])
        tmp = sb("tmp", [P, NT])
        shifted = sb("shifted", [P, NT], I32)
        o = sb("o", [P, 2, NT, D])
        mm = [ctx.enter_context(nc.psum_tensor(f"{name}mm{b}", [P, CH], F32)) for b in range(4)]
        psT = [ctx.enter_context(nc.psum_tensor(f"{name}psT{k}", [P, CH], F32)) for k in range(KD)]
        psY = [ctx.enter_context(nc.psum_tensor(f"{name}psY{k}", [P, D], F32)) for k in range(2)]

        wsem = sem("w_loaded")
        half_done = sem("half_done")
        x_loaded = [sem(f"x_loaded{j}") for j in range(2)]
        xT_ps = [sem(f"xT_ps{k}") for k in range(KD)]
        xT_ev = [sem(f"xT_ev{k}") for k in range(KD)]
        up_ps = sem("up_ps")
        t_ready = sem("t_ready")
        a_done = [sem(f"a_done{p}") for p in range(2)]
        h0_done = [sem(f"h0_done{p}") for p in range(2)]
        hid_ps = [sem("h1_ps"), sem("h2_ps")]
        gelu_done = [sem("gelu1_done"), sem("gelu2_done")]
        split_done = [sem("split1_done"), sem("split2_done")]
        y_ps = sem("y_ps")
        y_used = [sem(f"y_used{p}") for p in range(2)]
        z_done = sem("z_done")
        chain = sem("chain")
        o_ready = sem("o_ready")
        o_out = [sem(f"o_out{j}") for j in range(2)]
        WD = 16 * (3 if split else 8)

        st_done = sem("st_done")
        mv_done = sem("mv_done")

        dst_src = [(w1_sb, w1), (w2_sb, w2), (h1_sb, h1), (h2_sb, h2), (w3_sb, w3)]
        PIECE = 1024
        pieces = [(d.rearrange("p k n -> p (k n)")[:, q:q + PIECE], s.rearrange("p k n -> p (k n)")[:, q:q + PIECE])
                  for d, s in ((d[:], s) for d, s in dst_src) for q in range(0, d.shape[1] * d.shape[2], PIECE)]
        if split:
            stage = sb("stage", [P, 2, PIECE])
            miss = sb("miss", [P, len(pieces)])
            ones = sb("ones", [P, 1])
            misses = sb("misses", [P, 1])
            stage_in = [sem(f"stage_in{b}") for b in range(2)]
            rounded = sem("rounded")
            compared = sem("compared")
            missed = sem("missed")
            miss_ps = sem("miss_ps")
            flag_done = sem("flag_done")
        prime(nc, primed)
        block = ctx.enter_context(nc.Block())

        def guarded(eng):
            if split:
                eng.wait_ge(flag_done, PRIMED + 1)
            value = eng.value_load(flag[0:1, 0:1], min_val=0, max_val=1)
            return eng.If(1 - value if split else value)

        def chunk_dram(ap, c):
            return ap.rearrange("(c t p) d -> c p t d", t=NT, p=P)[c]

        @block.sync
        def _(sp):
            def load_first():
                sp.dma_start(ident[:], ident_dram).then_inc(wsem, 16)
                for j in range(2):
                    sp.dma_start(x[:, j], chunk_dram(x_in, j)).then_inc(x_loaded[j], 16)
                sp.dma_start(scl[:], s_cols).then_inc(wsem, 16)
                sp.dma_start(s3[:], s3_row).then_inc(wsem, 16)

            def store(c, j):
                sp.wait_ge(o_ready, PRIMED + NT * (c + 1))
                sp.dma_start(chunk_dram(out, c), o[:, j]).then_inc(o_out[j], 16)

            if split:
                load_first()
                for n, (_, src) in enumerate(pieces):
                    if n >= 2:
                        sp.wait_ge(compared, PRIMED + n - 1)
                    sp.dma_start(stage[:, n % 2], src).then_inc(stage_in[n % 2], 16)
                sp.wait_ge(wsem, PRIMED + WD)
                for j in range(2):
                    sp.wait_ge(x_loaded[j], PRIMED + 16)
            with guarded(sp):
                if not split:
                    load_first()
                    for d, src in dst_src:
                        sp.dma_start(d[:], src).then_inc(wsem, 16)
                with sp.Fori(0, PAIRS - 1) as i:
                    for j in range(2):
                        store(2 * i + j, j)
                        sp.wait_ge(z_done, PRIMED + NT * (2 * i + j + 1))
                        sp.dma_start(x[:, j], chunk_dram(x_in, 2 * i + j + 2)).then_inc(x_loaded[j], 16)
                for j in range(2):
                    store(2 * (PAIRS - 1) + j, j)
                for j in range(2):
                    sp.wait_ge(o_out[j], PRIMED + 16 * PAIRS)

        @block.tensor
        def _(pe):
            def product(ps, w, rhs, k, K):
                for q in range(parts):
                    last = nc.tensor.matmul(ps, w, rhs[q][:, k, :], start=(k == 0 and q == 0),
                                            stop=(k == K - 1 and q == parts - 1))
                return last

            def chunk(i, j):
                c = 2 * i + j
                pe.wait_ge(x_loaded[j], PRIMED + 16 * (i + 1))
                for k in range(KD):
                    pe.wait_ge(xT_ev[k], PRIMED + c)
                    for n in range(NT):
                        last = nc.tensor.transpose(psT[k][:, n * P:(n + 1) * P], x[:, j, n, k * P:(k + 1) * P], ident[:])
                    last.then_inc(xT_ps[k], 1)
                for k in range(KD):
                    pe.wait_ge(xT_ev[k], PRIMED + c + 1)
                for m in range(KF):
                    p = m % 2
                    if m < 2:
                        pe.wait_ge(gelu_done[1], PRIMED + KF * c)
                    else:
                        pe.wait_ge(a_done[p], PRIMED + KF // 2 * c + m // 2)
                        pe.wait_ge(h0_done[p], PRIMED + KF // 2 * c + m // 2)
                    cols = slice(m * P, (m + 1) * P)
                    for k in range(KD):
                        product(mm[2 * p][:], w1_sb[:, k, cols], xT, k, KD)
                    for k in range(KD):
                        last = product(mm[2 * p + 1][:], w2_sb[:, k, cols], xT, k, KD)
                    last.then_inc(up_ps, 1)
                for layer, w in enumerate((h1_sb, h2_sb)):
                    src = (ha, hb)[layer]
                    for m in range(KF):
                        if layer == 0 and m == 0:
                            pe.wait_ge(a_done[0], PRIMED + KF // 2 * (c + 1))
                        if layer == 0 and m == 2:
                            pe.wait_ge(a_done[1], PRIMED + KF // 2 * (c + 1))
                        if m >= 4:
                            pe.wait_ge(gelu_done[layer], PRIMED + KF * c + m - 3)
                        if m < 4 and layer == 1:
                            pe.wait_ge(gelu_done[0], PRIMED + KF * c + m + 5)
                        for k in range(KF):
                            if m == 0 and layer == 0:
                                pe.wait_ge(h0_done[k % 2], PRIMED + KF // 2 * c + k // 2 + 1)
                            if m == 0 and layer == 1:
                                pe.wait_ge((split_done if split else gelu_done)[0], PRIMED + KF * c + k + 1)
                            last = product(mm[m % 4][:], w[:, k, m * P:(m + 1) * P], src, k, KF)
                        last.then_inc(hid_ps[layer], 1)
                for n in range(NT):
                    pe.wait_ge(y_used[n % 2], PRIMED + NT // 2 * c + n // 2)
                    for k in range(KF):
                        if n == 0:
                            pe.wait_ge((split_done if split else gelu_done)[1], PRIMED + KF * c + k + 1)
                        for q in range(parts):
                            last = nc.tensor.matmul(psY[n % 2][:], ha[q][:, k, n * P:(n + 1) * P], w3_sb[:, k, :],
                                                    start=(k == 0 and q == 0), stop=(k == KF - 1 and q == parts - 1))
                    last.then_inc(y_ps, 1)

            if split:
                pe.wait_ge(missed, PRIMED + 1)
                nc.tensor.matmul(psY[0][0:1, 0:1], misses[:], ones[:], start=True, stop=True).then_inc(miss_ps, 1)
            with guarded(pe):
                pe.wait_ge(wsem, PRIMED + WD)
                with pe.Fori(0, PAIRS) as i:
                    for j in range(2):
                        chunk(i, j)

        @block.scalar
        def _(act):
            if split:
                for n, (dst, _) in enumerate(pieces):
                    act.wait_ge(stage_in[n % 2], PRIMED + 16 * (n // 2 + 1))
                    nc.scalar.activation(dst, stage[:, n % 2], ACT.Copy).then_inc(rounded, 1)
            with guarded(act):
                act.wait_ge(half_done, PRIMED + 2)
                with act.Fori(0, PAIRS) as i:
                    for j in range(2):
                        c = 2 * i + j
                        for m in range(KF):
                            act.wait_ge(up_ps, PRIMED + KF * c + m + 1)
                            act.wait_ge(a_done[m % 2], PRIMED + KF // 2 * c + m // 2)
                            nc.scalar.activation(t[:, m % 2], mm[2 * (m % 2)][:], ACT.Tanh,
                                                 scale=half[:, 0, m:m + 1]).then_inc(t_ready, 1)
                        for layer in range(2):
                            dst = (hb, ha)[layer]
                            for m in range(KF):
                                act.wait_ge(hid_ps[layer], PRIMED + KF * c + m + 1)
                                if split:
                                    if m >= 2:
                                        act.wait_ge(split_done[layer], PRIMED + KF * c + m - 1)
                                    elif layer == 1:
                                        act.wait_ge(split_done[0], PRIMED + KF * c + KF - 1 + m)
                                    out_m = g[:, m % 2]
                                else:
                                    out_m = dst[0][:, m, :]
                                nc.scalar.activation(out_m, mm[m % 4][:], ACT.Gelu,
                                                     scale=scl[:, 2 + layer, m:m + 1]).then_inc(gelu_done[layer], 1)

        @block.vector
        def _(dve):
            LINKS = KD * split + 2 * KF * split + 2 * KF * split + 1 + RSQRT_LINKS
            if split:
                nc.vector.memset(ones[:], 1.0)
                for n, (dst, _) in enumerate(pieces):
                    dve.wait_ge(rounded, PRIMED + n + 1)
                    if n:
                        dve.wait_ge(compared, PRIMED + n)
                    nc.vector.scalar_tensor_tensor(a[:].rearrange("p j n -> p (j n)"), stage[:, n % 2], 1.0, dst, ALU.mult,
                                                   ALU.not_equal, accum_out=miss[:, n:n + 1]).then_inc(compared, 1)
                dve.wait_ge(compared, PRIMED + len(pieces))
                nc.vector.reduce_sum(misses[:], miss[:], X).then_inc(missed, 1)
                dve.wait_ge(miss_ps, PRIMED + 1)
                nc.vector.tensor_scalar(flag[0:1, 0:1], psY[0][0:1, 0:1], 0.0, None, ALU.is_gt).then_inc(flag_done, 1)
            with guarded(dve):
                dve.wait_ge(wsem, PRIMED + WD)
                nc.vector.tensor_scalar(half[:, 0], scl[:, 0], 0.5, None, ALU.mult).then_inc(half_done, 1)
                dve.wait_ge(half_done, PRIMED + 1)
                nc.vector.tensor_tensor(half[:, 1], half[:, 0], scl[:, 1], ALU.mult).then_inc(half_done, 1)
                dve.wait_ge(half_done, PRIMED + 2)
                with dve.Fori(0, PAIRS) as i:
                    for j in range(2):
                        c = 2 * i + j
                        n_link = [0]

                        def link(ins):
                            n_link[0] += 1
                            ins.then_inc(chain, 1)
                            dve.wait_ge(chain, PRIMED + LINKS * c + n_link[0])

                        for k in range(KD):
                            dve.wait_ge(xT_ps[k], PRIMED + c + 1)
                            if split:
                                link(nc.vector.tensor_copy(xT[0][:, k], psT[k][:]))
                                nc.vector.tensor_tensor(xT[1][:, k], psT[k][:], xT[0][:, k],
                                                        ALU.subtract).then_inc(xT_ev[k], 1)
                            else:
                                nc.vector.tensor_copy(xT[0][:, k], psT[k][:]).then_inc(xT_ev[k], 1)
                        for m in range(KF):
                            p = m % 2
                            dve.wait_ge(t_ready, PRIMED + KF * c + m + 1)
                            nc.vector.scalar_tensor_tensor(a[:, p], t[:, p], 1.0, mm[2 * p][:], ALU.add,
                                                           ALU.mult).then_inc(a_done[p], 1)
                            dve.wait_ge(a_done[p], PRIMED + KF // 2 * c + m // 2 + 1)
                            if split:
                                link(nc.vector.scalar_tensor_tensor(g[:, p], mm[2 * p + 1][:], half[:, 1, m:m + 1], a[:, p],
                                                                    ALU.mult, ALU.mult))
                                link(nc.vector.tensor_copy(ha[0][:, m], g[:, p]))
                                nc.vector.tensor_tensor(ha[1][:, m], g[:, p], ha[0][:, m],
                                                        ALU.subtract).then_inc(h0_done[p], 1)
                                continue
                            nc.vector.scalar_tensor_tensor(ha[0][:, m], mm[2 * p + 1][:], half[:, 1, m:m + 1], a[:, p],
                                                           ALU.mult, ALU.mult).then_inc(h0_done[p], 1)
                        for layer in range(2 * split):
                            dst = (hb, ha)[layer]
                            for m in range(KF):
                                dve.wait_ge(gelu_done[layer], PRIMED + KF * c + m + 1)
                                link(nc.vector.tensor_copy(dst[0][:, m], g[:, m % 2]))
                                nc.vector.tensor_tensor(dst[1][:, m], g[:, m % 2], dst[0][:, m],
                                                        ALU.subtract).then_inc(split_done[layer], 1)
                        for n in range(NT):
                            p = n % 2
                            dve.wait_ge(y_ps, PRIMED + NT * c + n + 1)
                            nc.vector.tensor_tensor(z[:, n], psY[p][:], s3[:], ALU.mult).then_inc(y_used[p], 1)
                            dve.wait_ge(y_used[p], PRIMED + NT // 2 * c + n // 2 + 1)
                            nc.vector.tensor_tensor(z[:, n], z[:, n], x[:, j, n, :], ALU.add).then_inc(z_done, 1)
                            dve.wait_ge(z_done, PRIMED + NT * c + n + 1)
                            nc.vector.bn_stats(st[:, n], z[:, n]).then_inc(st_done, 1)
                            dve.wait_ge(half_done, PRIMED + 2)
                            dve.wait_ge(st_done, PRIMED + NT * c + n + 1)
                            nc.vector.bn_aggr(mv[:, n], st[:, n]).then_inc(mv_done, 1)
                        dve.wait_ge(mv_done, PRIMED + NT * c + NT)
                        link(nc.vector.tensor_copy(var[:], mv[:, :, 1]))
                        rsqrt(nc, link, rstd[:], var[:], tmp[:], shifted[:])
                        dve.wait_ge(o_out[j], PRIMED + 16 * i)
                        for n in range(NT):
                            nc.vector.tensor_scalar(o[:, j, n], z[:, n], mv[:, n, 0:1], rstd[:, n:n + 1], ALU.subtract,
                                                    ALU.mult).then_inc(o_ready, 1)
                        assert n_link[0] == LINKS, n_link


def attend_and_route_phase(nc, x_in, xT_in, wqT, wkT, wvT, wo, w_router, b_router, consts, route, x1_out, slots,
                           batches, capacity):
    T, D = x_in.shape
    KD = D // P
    SEQ = T // batches
    NT = SEQ // P
    HALF = SEQ // 2
    E = w_router.shape[2]
    GROUP = 4
    groups = [[(n, min(n + GROUP, i + 1)) for n in range(0, i + 1, GROUP)] for i in range(NT)]
    first_group = [sum(len(g) for g in groups[:i]) for i in range(NT + 1)]
    NG = first_group[NT]
    ROWS_AT = {0: 0, 1: 1, 2: 2, 3: 3}
    LOGITS_AT, COUNTS_AT = 4, 5
    SCALE = float(D) ** -0.5
    with ExitStack() as ctx:
        def sb(n, s, d=F32):
            return ctx.enter_context(nc.sbuf_tensor("a" + n, s, d))

        def psum(n, s):
            return ctx.enter_context(nc.psum_tensor("a" + n, s, F32))

        primed = []
        ctx.callback(nc.clear_and_free_semaphores, primed)

        def sem(n):
            primed.append(nc.alloc_semaphore("a" + n))
            return primed[-1]

        ident, ident_bf, mask_bf, before_me, all_ones = (sb(n, [P, P], d) for n, d in (
            ("ident", F32), ("ident_bf", BF16), ("mask_bf", BF16), ("before_me", F32), ("all_ones", F32)))
        iota_e = sb("iota_e", [P, E])
        br = sb("br", [P, E])
        wr = sb("wr", [P, KD, E])
        raw = [sb(f"raw{n}", [P, KD, D]) for n in range(4)]
        score_hi, score_lo, value_hi, value_lo = (sb(n, [P, KD, D], F32R) for n in ("sc_hi", "sc_lo", "va_hi", "va_lo"))
        xs = sb("xs", [P, KD, SEQ])
        xT_hi, xT_lo, qT_hi, qT_lo = (sb(n, [P, KD, SEQ], F32R) for n in ("xT_hi", "xT_lo", "qT_hi", "qT_lo"))
        v_hi, v_lo = (sb(n, [P, NT, D], F32R) for n in ("v_hi", "v_lo"))
        xin = sb("xin", [P, NT, D])
        prob = sb("prob", [P, 2, SEQ])
        pT_hi, pT_lo = (sb(n, [P, 4, GROUP, P], F32R) for n in ("pT_hi", "pT_lo"))
        nmax, rowsum, recip, var, rstd, tmp = (sb(n, [P, NT]) for n in ("nmax", "rowsum", "recip", "var", "rstd", "tmp"))
        shifted = sb("shifted", [P, NT], I32)
        z = sb("z", [P, NT, D])
        st = sb("st", [P, NT, 6])
        mv = sb("mv", [P, NT, 2])
        xn = sb("xn", [P, NT, D])
        x1T = sb("x1T", [P, KD, SEQ])
        lg, top, both, pos, prod = (sb(n, [P, NT, E]) for n in ("lg", "top", "both", "pos", "prod"))
        top_i = sb("top_i", [P, NT, E], U32)
        top_f = sb("top_f", [P, NT, 2])
        oh = [sb(f"oh{c}", [P, NT, E]) for c in range(2)]
        cum = sb("cum", [P, NT + 1, E])
        gap = sb("gap", [P, NT])
        egap = sb("egap", [P, NT])
        slot_f = sb("slot_f", [P, NT])
        slot_i = [sb(f"slot_i{c}", [P, NT], I32) for c in range(2)]
        S = [psum(f"S{n}", [P, SEQ]) for n in range(2)]
        PT = psum("PT", [P, 2, GROUP, P])
        O = psum("O", [P, D])
        misc = psum("misc", [P, 512])
        PTf = PT[:].rearrange("p a b c -> p (a b c)")

        names = ("const_in xs_in xin_in ab_ps ab_hi ab_lo x_hi x_lo q_ps q_hi q_lo v_ps v_hi v_lo s_ps mx ex pt_ps pt_hi "
                 "pt_lo o_ps z_done chain ln_chain xn_done t_ps t_ev lg_ps both_done px_ps gap_done e_done slot_done sc_out scattered x1_st "
                 "st_done recip_done top_done mv_done").split()
        (const_in, xs_in, xin_in, ab_ps, ab_hi, ab_lo, x_hi, x_lo, q_ps, q_hi, q_lo, v_ps, v_hi_done, v_lo_done, s_ps, mx,
         ex, pt_ps, pt_hi, pt_lo, o_ps, z_done, chain, ln_chain, xn_done, t_ps, t_ev, lg_ps, both_done, px_ps, gap_done, e_done,
         slot_done, sc_out, scattered, x1_st, st_done, recip_done, top_done, mv_done) = (sem(n) for n in names)
        unwatched = {n.engine: sem(f"unwatched{q}") for q, n in
                     enumerate((nc.sync, nc.gpsimd, nc.tensor, nc.scalar, nc.vector))}
        loads = [(ident[:], consts["ident"]), (z[:, 0, :P], consts["mask"]),
                 (before_me[:], consts["before_me"]), (all_ones[:], consts["all_ones"]), (iota_e[:], consts["iota_e"]),
                 (br[:], b_router), (wr[:], w_router)]
        raws = list(zip(raw, (wqT, wkT, wvT, wo)))
        N_CONST = 16 * (len(loads) + len(raws))

        by_gpsimd = [sc_out]
        prime(nc, [s for s in primed if s not in by_gpsimd])
        block = ctx.enter_context(nc.Block())

        def wait_alone(eng, semaphore, value):
            eng.wait_ge(semaphore, value)
            eng.sem_inc(unwatched[eng.engine], 1)

        def tokens(ap, b):
            return ap.rearrange("(b t p) d -> b p t d", t=NT, p=P)[b]

        TRANSPOSES = NT // 2

        def each_sequence(eng, attention, tail):
            attention(0, False, True)
            with eng.Fori(1, batches - 1) as b:
                attention(b, True, True)
            attention(batches - 1, True, False)
            tail(batches - 1)

        @block.sync
        def _(sp):
            for d, s in raws:
                sp.dma_start(d[:], s).then_inc(const_in, 16)
            for d, s in loads:
                sp.dma_start(d, s).then_inc(const_in, 16)
            sp.wait_ge(const_in, PRIMED + N_CONST)

            def attention(b, earlier, later):
                sp.wait_ge(x_lo, PRIMED + b)
                sp.dma_start(xs[:], xT_in[b]).then_inc(xs_in, 16)
                sp.wait_ge(z_done, PRIMED + NT * b)
                sp.dma_start(xin[:], tokens(x_in, b)).then_inc(xin_in, 16)
                if earlier:
                    tail(b - 1)

            def tail(b):
                sp.wait_ge(xn_done, PRIMED + b + 1)
                sp.dma_start(tokens(x1_out, b), xn[:]).then_inc(x1_st, 16)

            each_sequence(sp, attention, tail)
            sp.wait_ge(x1_st, PRIMED + 16 * batches)

        @block.gpsimd
        def _(pool):
            def tail(b):
                wait_alone(pool, slot_done, PRIMED + 2 * b + 2)
                for c in range(2):
                    for t in range(NT):
                        pool.indirect_dma_start(
                            out=slots, out_offset=bass.IndirectOffsetOnAxis(ap=slot_i[c][:, t:t + 1], axis=0),
                            in_=xn[:, t, :], in_offset=None).then_inc(sc_out, 16)
                pool.wait_ge(sc_out, 16 * 2 * NT * (b + 1))
                pool.sem_inc(scattered, 1)

            each_sequence(pool, lambda b, earlier, later: tail(b - 1) if earlier else None, tail)

        @block.tensor
        def _(pe):
            def three(ps, left, right, first, last):
                (lh, ll), (rh, rl) = left, right
                nc.tensor.matmul(ps, lh, rh, start=first, stop=False)
                nc.tensor.matmul(ps, lh, rl, start=False, stop=False)
                return nc.tensor.matmul(ps, ll, rh, start=False, stop=last)

            pe.wait_ge(const_in, PRIMED + N_CONST)
            for pair in range(2):
                if pair:
                    pe.wait_ge(ab_lo, PRIMED + 1)
                for m in range(KD):
                    for k in range(KD):
                        last = nc.tensor.matmul(misc[:, m * D:(m + 1) * D], raw[2 * pair][:, k, m * P:(m + 1) * P],
                                                raw[2 * pair + 1][:, k, :], start=(k == 0), stop=(k == KD - 1))
                last.then_inc(ab_ps, 1)
            pe.wait_ge(ab_lo, PRIMED + 2)

            def scores(b, i):
                s = S[i % 2]
                if i == 0:
                    pe.wait_ge(v_lo_done, PRIMED + 2 * b + 2)
                    pe.wait_ge(q_lo, PRIMED + 2 * b + 2)
                elif i >= 2:
                    pe.wait_ge(ex, PRIMED + NT * b + i - 1)
                width = (i + 1) * P
                for c0 in range(0, width, HALF):
                    c1 = min(width, c0 + HALF)
                    for k in range(KD):
                        three(s[:, c0:c1], (qT_hi[:, k, i * P:(i + 1) * P], qT_lo[:, k, i * P:(i + 1) * P]),
                              (xT_hi[:, k, c0:c1], xT_lo[:, k, c0:c1]), k == 0, k == KD - 1)
                    if c1 == width:
                        last = nc.tensor.matmul(s[:, i * P:width], ident_bf[:], mask_bf[:], start=False, stop=True,
                                                skip_group_check=True)
                last.then_inc(s_ps, 1)

            def transpose_probs(b, i):
                pe.wait_ge(ex, PRIMED + NT * b + i + 1)
                for g, (n0, n1) in enumerate(groups[i]):
                    g += first_group[i]
                    if g >= 2:
                        pe.wait_ge(pt_lo, PRIMED + NG * b + g - 1)
                    for n in range(n0, n1):
                        last = nc.tensor.transpose(PT[:, g % 2, n - n0, :], prob[:, i % 2, n * P:(n + 1) * P], ident[:])
                    last.then_inc(pt_ps, 1)

            def weigh(b, i):
                pe.wait_ge(z_done, PRIMED + NT * b + i)
                for g, (n0, n1) in enumerate(groups[i]):
                    g += first_group[i]
                    pe.wait_ge(pt_lo, PRIMED + NG * b + g + 1)
                    for n in range(n0, n1):
                        last = three(O[:], (pT_hi[:, g % 4, n - n0, :], pT_lo[:, g % 4, n - n0, :]),
                                     (v_hi[:, n, :], v_lo[:, n, :]), n == 0, n == i)
                last.then_inc(o_ps, 1)

            def transpose_rows(b, j):
                if j == 0:
                    pe.wait_ge(xn_done, PRIMED + b + 1)
                    pe.wait_ge(slot_done, PRIMED + 2 * b)
                else:
                    pe.wait_ge(t_ev, PRIMED + TRANSPOSES * b + j)
                for k in range(KD):
                    for n in range(2):
                        last = nc.tensor.transpose(misc[:, (2 * k + n) * P:(2 * k + n + 1) * P],
                                                   xn[:, 2 * j + n, k * P:(k + 1) * P], ident[:])
                last.then_inc(t_ps, 1)

            def logits(b):
                pe.wait_ge(t_ev, PRIMED + TRANSPOSES * (b + 1))
                for t in range(NT):
                    for k in range(KD):
                        last = nc.tensor.matmul(misc[:, t * E:(t + 1) * E], x1T[:, k, t * P:(t + 1) * P], wr[:, k, :],
                                                start=(k == 0), stop=(k == KD - 1))
                last.then_inc(lg_ps, 1)

            def counts(b):
                pe.wait_ge(both_done, PRIMED + b + 1)
                flat = both[:].rearrange("p t e -> p (t e)")
                nc.tensor.matmul(misc[:, NT * E:2 * NT * E], before_me[:], flat, start=True, stop=True)
                nc.tensor.matmul(misc[:, 2 * NT * E:3 * NT * E], all_ones[:], flat, start=True, stop=True).then_inc(px_ps, 1)

            def attention(b, earlier, later):
                pe.wait_ge(x_lo, PRIMED + b + 1)
                pe.wait_ge(ex, PRIMED + NT * b)
                for m in range(KD):
                    for c in range(2):
                        cs = slice(c * HALF, (c + 1) * HALF)
                        for k in range(KD):
                            last = three(S[m][:, cs], (score_hi[:, k, m * P:(m + 1) * P], score_lo[:, k, m * P:(m + 1) * P]),
                                         (xT_hi[:, k, cs], xT_lo[:, k, cs]), k == 0, k == KD - 1)
                    last.then_inc(q_ps, 1)
                for half in range(2):
                    dst = (PTf, S[0][:])[half]
                    if half == 0:
                        pe.wait_ge(pt_lo, PRIMED + NG * b)
                    else:
                        pe.wait_ge(q_lo, PRIMED + 2 * b + 1)
                    for n in range(NT // 2):
                        t = half * NT // 2 + n
                        for k in range(KD):
                            last = three(dst[:, n * D:(n + 1) * D],
                                         (xT_hi[:, k, t * P:(t + 1) * P], xT_lo[:, k, t * P:(t + 1) * P]),
                                         (value_hi[:, k, :], value_lo[:, k, :]), k == 0, k == KD - 1)
                    last.then_inc(v_ps, 1)
                scores(b, 0)
                for i in range(NT):
                    if i + 1 < NT:
                        scores(b, i + 1)
                    if earlier and i in ROWS_AT:
                        transpose_rows(b - 1, ROWS_AT[i])
                    if earlier and i == COUNTS_AT:
                        counts(b - 1)
                    transpose_probs(b, i)
                    if i:
                        weigh(b, i - 1)
                    if earlier and i == LOGITS_AT:
                        logits(b - 1)
                weigh(b, NT - 1)

            def tail(b):
                for j in range(TRANSPOSES):
                    transpose_rows(b, j)
                logits(b)
                counts(b)

            each_sequence(pe, attention, tail)

        @block.scalar
        def _(act):
            for pair, hi in enumerate((score_hi, value_hi)):
                act.wait_ge(ab_ps, PRIMED + pair + 1)
                nc.scalar.activation(hi[:].rearrange("p k d -> p (k d)"), misc[:], ACT.Copy,
                                     scale=SCALE if pair == 0 else 1.0).then_inc(ab_hi, 1)

            def rows_out(b, j):
                act.wait_ge(t_ps, PRIMED + TRANSPOSES * b + j + 1)
                nc.scalar.activation(x1T[:, :, 2 * j * P:(2 * j + 2) * P], misc[:].rearrange("p (k t) -> p k t", k=KD),
                                     ACT.Copy).then_inc(t_ev, 1)

            def weights(b):
                act.wait_ge(gap_done, PRIMED + b + 1)
                nc.scalar.activation(egap[:], gap[:], ACT.Exp).then_inc(e_done, 1)

            def x_high(b):
                act.wait_ge(xs_in, PRIMED + 16 * b + 16)
                act.wait_ge(s_ps, PRIMED + NT * b)
                nc.scalar.activation(xT_hi[:], xs[:], ACT.Copy).then_inc(x_hi, 1)

            def attention(b, earlier, later):
                for m in range(KD):
                    act.wait_ge(q_ps, PRIMED + 2 * b + m + 1)
                    nc.scalar.activation(qT_hi[:, m, :], S[m][:], ACT.Copy).then_inc(q_hi, 1)
                for half in range(2):
                    src = (PTf, S[0][:])[half]
                    act.wait_ge(v_ps, PRIMED + 2 * b + half + 1)
                    nc.scalar.activation(v_hi[:, half * NT // 2:(half + 1) * NT // 2, :].rearrange("p t d -> p (t d)"), src,
                                         ACT.Copy).then_inc(v_hi_done, 1)

                def exp(i):
                    act.wait_ge(mx, PRIMED + NT * b + i + 1)
                    if i >= 2:
                        act.wait_ge(pt_ps, PRIMED + NG * b + first_group[i - 1])
                    width = (i + 1) * P
                    nc.scalar.activation(prob[:, i % 2, :width], S[i % 2][:, :width], ACT.Exp, bias=nmax[:, i:i + 1],
                                         accum_out=rowsum[:, i:i + 1]).then_inc(ex, 1)

                exp(0)
                for i in range(NT):
                    if i + 1 < NT:
                        exp(i + 1)
                    if earlier and i in ROWS_AT:
                        rows_out(b - 1, ROWS_AT[i])
                    for g, (n0, n1) in enumerate(groups[i]):
                        g += first_group[i]
                        act.wait_ge(pt_ps, PRIMED + NG * b + g + 1)
                        if i >= 2:
                            act.wait_ge(o_ps, PRIMED + NT * b + i - 1)
                        nc.scalar.activation(pT_hi[:, g % 4, :n1 - n0, :], PT[:, g % 2, :n1 - n0, :],
                                             ACT.Copy).then_inc(pt_hi, 1)
                    if earlier and i == COUNTS_AT:
                        weights(b - 1)
                if later:
                    x_high(b + 1)

            def tail(b):
                for j in range(TRANSPOSES):
                    rows_out(b, j)
                weights(b)

            x_high(0)
            each_sequence(act, attention, tail)

        @block.vector
        def _(dve):
            LINKS = 1 + 1 + 1 + 1 + 2 + 1 + NT + 1 + 2 * 4 + 1
            dve.wait_ge(const_in, PRIMED + N_CONST)
            nc.vector.tensor_copy(ident_bf[:], ident[:])
            nc.vector.tensor_copy(mask_bf[:], z[:, 0, :P])
            for pair, (hi, lo) in enumerate(((score_hi, score_lo), (value_hi, value_lo))):
                dve.wait_ge(ab_hi, PRIMED + pair + 1)
                nc.vector.scalar_tensor_tensor(lo[:].rearrange("p k d -> p (k d)"), misc[:], SCALE if pair == 0 else 1.0,
                                               hi[:].rearrange("p k d -> p (k d)"), ALU.mult, ALU.subtract).then_inc(ab_lo, 1)
            nc.vector.memset(cum[:, NT, :], 0.0).then_inc(chain, 1)

            def make_tail(b):
                n_link = [0]

                def link(ins, alone=False):
                    n_link[0] += 1
                    ins.then_inc(chain, 1)
                    (wait_alone if alone else lambda e, s, v: e.wait_ge(s, v))(dve, chain, PRIMED + LINKS * b + n_link[0] + 1)

                def choose():
                    wait_alone(dve, lg_ps, PRIMED + b + 1)
                    link(nc.vector.tensor_tensor(lg[:], misc[:, :NT * E].rearrange("p (t e) -> p t e", e=E),
                                                 br[:].unsqueeze(1).to_broadcast([P, NT, E]), ALU.add), alone=True)
                    for t in range(NT):
                        ins = nc.vector.max(top[:, t], lg[:, t])
                    link(ins, alone=True)
                    for t in range(NT):
                        ins = nc.vector.max_index(top_i[:, t], top[:, t], lg[:, t])
                    link(ins)
                    nc.vector.tensor_tensor(gap[:], top[:, :, 1], top[:, :, 0], ALU.subtract).then_inc(gap_done, 1)
                    link(nc.vector.tensor_copy(top_f[:], top_i[:, :, 0:2]))
                    for c in range(2):
                        ins = nc.vector.tensor_tensor(oh[c][:], iota_e[:].unsqueeze(1).to_broadcast([P, NT, E]),
                                                      top_f[:, :, c:c + 1].to_broadcast([P, NT, E]), ALU.is_equal)
                    ins.then_inc(top_done, 1)
                    dve.wait_ge(top_done, PRIMED + b + 1)
                    nc.vector.tensor_tensor(both[:], oh[0][:], oh[1][:], ALU.add).then_inc(both_done, 1)

                def place():
                    dve.wait_ge(e_done, PRIMED + b + 1)
                    link(nc.vector.tensor_scalar(gap[:], egap[:], 1.0, None, ALU.add))
                    w0 = route["weight"][0][:, bass.ds(b * NT, NT)]
                    w1 = route["weight"][1][:, bass.ds(b * NT, NT)]
                    link(nc.vector.reciprocal(w0, gap[:]))
                    nc.vector.tensor_tensor(w1, egap[:], w0, ALU.mult)
                    dve.wait_ge(px_ps, PRIMED + b + 1)
                    link(nc.vector.tensor_copy(cum[:, 0, :], cum[:, NT, :]))
                    for t in range(NT):
                        link(nc.vector.tensor_tensor(cum[:, t + 1, :], misc[:, (2 * NT + t) * E:(2 * NT + t + 1) * E],
                                                     cum[:, t, :], ALU.add))
                    link(nc.vector.tensor_tensor(pos[:], misc[:, NT * E:2 * NT * E].rearrange("p (t e) -> p t e", e=E),
                                                 cum[:, :NT, :], ALU.add))
                    for c in range(2):
                        rank = route["rank"][c][:, bass.ds(b * NT, NT)]
                        keep = route["onehot"][c][:, bass.ds(b * NT, NT), :]
                        nc.vector.tensor_copy(keep, oh[c][:]).then_inc(chain, 1)
                        n_link[0] += 1
                        link(nc.vector.tensor_tensor(prod[:], oh[c][:], pos[:], ALU.mult))
                        link(nc.vector.tensor_reduce(rank, prod[:], X, ALU.add))
                        link(nc.vector.scalar_tensor_tensor(slot_f[:], top_f[:, :, c], float(capacity), rank, ALU.mult,
                                                            ALU.add))
                        nc.vector.tensor_copy(slot_i[c][:], slot_f[:]).then_inc(slot_done, 1)
                    dve.wait_ge(slot_done, PRIMED + 2 * b + 2)
                    link(nc.vector.tensor_copy(route["count"][:], cum[:, NT, :]))
                    assert n_link[0] == LINKS, (n_link[0], LINKS)

                return choose, place

            def x_low(b):
                dve.wait_ge(x_hi, PRIMED + b + 1)
                nc.vector.tensor_tensor(xT_lo[:], xs[:], xT_hi[:], ALU.subtract).then_inc(x_lo, 1)

            def normalised():
                for i in range(NT):
                    ins = nc.vector.tensor_scalar(xn[:, i], z[:, i], mv[:, i, 0:1], rstd[:, i:i + 1], ALU.subtract, ALU.mult)
                ins.then_inc(xn_done, 1)

            def attention(b, earlier, later):
                if earlier:
                    choose, place = make_tail(b - 1)
                for m in range(KD):
                    dve.wait_ge(q_hi, PRIMED + 2 * b + m + 1)
                    nc.vector.tensor_tensor(qT_lo[:, m, :], S[m][:], qT_hi[:, m, :], ALU.subtract).then_inc(q_lo, 1)
                for half in range(2):
                    src = (PTf, S[0][:])[half]
                    rows = slice(half * NT // 2, (half + 1) * NT // 2)
                    dve.wait_ge(v_hi_done, PRIMED + 2 * b + half + 1)
                    nc.vector.tensor_tensor(v_lo[:, rows, :].rearrange("p t d -> p (t d)"), src,
                                            v_hi[:, rows, :].rearrange("p t d -> p (t d)"), ALU.subtract).then_inc(v_lo_done, 1)

                if earlier:
                    dve.wait_ge(x1_st, PRIMED + 16 * (b - 1))
                    dve.wait_ge(scattered, PRIMED + b - 1)
                    normalised()

                def row_max(i):
                    dve.wait_ge(s_ps, PRIMED + NT * b + i + 1)
                    nc.vector.tensor_reduce(nmax[:, i:i + 1], S[i % 2][:, :(i + 1) * P], X, ALU.max, negate=True).then_inc(mx, 1)

                def residual(i):
                    dve.wait_ge(ex, PRIMED + NT * b + i + 1)
                    nc.vector.reciprocal(recip[:, i:i + 1], rowsum[:, i:i + 1]).then_inc(recip_done, 1)
                    dve.wait_ge(o_ps, PRIMED + NT * b + i + 1)
                    dve.wait_ge(xin_in, PRIMED + 16 * b + 16)
                    if i == 0 and earlier:
                        dve.wait_ge(xn_done, PRIMED + b)
                    dve.wait_ge(recip_done, PRIMED + NT * b + i + 1)
                    nc.vector.scalar_tensor_tensor(z[:, i], O[:], recip[:, i:i + 1], xin[:, i], ALU.mult,
                                                   ALU.add).then_inc(z_done, 1)
                    dve.wait_ge(z_done, PRIMED + NT * b + i + 1)
                    nc.vector.bn_stats(st[:, i], z[:, i]).then_inc(st_done, 1)

                row_max(0)
                for i in range(NT):
                    if i + 1 < NT:
                        row_max(i + 1)
                    for g, (n0, n1) in enumerate(groups[i]):
                        g += first_group[i]
                        dve.wait_ge(pt_hi, PRIMED + NG * b + g + 1)
                        nc.vector.tensor_tensor(pT_lo[:, g % 4, :n1 - n0, :], PT[:, g % 2, :n1 - n0, :],
                                                pT_hi[:, g % 4, :n1 - n0, :], ALU.subtract).then_inc(pt_lo, 1)
                    if i:
                        residual(i - 1)
                    if earlier and i == LOGITS_AT:
                        choose()
                    if earlier and i == COUNTS_AT:
                        place()
                if later:
                    x_low(b + 1)
                residual(NT - 1)
                wait_alone(dve, st_done, PRIMED + NT * b + NT)
                for i in range(NT):
                    ins = nc.vector.bn_aggr(mv[:, i], st[:, i])

                def link(ins):
                    n_link[0] += 1
                    ins.then_inc(mv_done, 1)
                    dve.wait_ge(mv_done, PRIMED + (2 + RSQRT_LINKS) * b + n_link[0])

                n_link = [0]
                link(ins)
                link(nc.vector.tensor_copy(var[:], mv[:, :, 1]))
                rsqrt(nc, link, rstd[:], var[:], tmp[:], shifted[:])

            def tail(b):
                dve.wait_ge(x1_st, PRIMED + 16 * b)
                dve.wait_ge(scattered, PRIMED + b)
                normalised()
                choose, place = make_tail(b)
                choose()
                place()

            x_low(0)
            each_sequence(dve, attention, tail)


def plan_phase(nc, route, units, starts_dram, slots, results, capacity, unit):
    E = route["count"].shape[1]
    D = slots.shape[1]
    TILES = route["rank"][0].shape[1]
    STARTS = starts_dram.shape[1]
    with ExitStack() as ctx:
        def sb(n, s, d=F32):
            return ctx.enter_context(nc.sbuf_tensor("p" + n, s, d))

        def sem(n):
            return ctx.enter_context(nc.semaphore("p" + n))

        starts = sb("starts", [P, STARTS])
        begun = sb("begun", [P, E, STARTS])
        taken = sb("taken", [P, E])
        before = sb("before", [P, E + 2])
        first_row = sb("first_row", [P, E])
        count_i = sb("count_i", [1, E], I32)
        zeros = sb("zeros", [P, unit // P, D])
        by_expert = sb("by_expert", [P, TILES, E])
        row_f = sb("row_f", [P, TILES])
        starts_in, zeros_done, counted, zeros_out, unreached_out, step = (sem(n) for n in ("starts_in", "zeros_done", "counted",
                                                                            "zeros_out",
                                                                                           "unreached_out", "step"))
        prime(nc, [])
        block = ctx.enter_context(nc.Block())

        @block.sync
        def _(sp):
            sp.dma_start(starts[:], starts_dram).then_inc(starts_in, 16)
            sp.wait_ge(counted, 1)
            sp.wait_ge(zeros_done, 1)
            for e in range(E):
                n = sp.value_load(count_i[0:1, e:e + 1], min_val=0, max_val=TILES * P)
                sp.dma_start(slots[bass.ds(e * capacity + n, unit), :].rearrange("(n p) d -> p n d", p=P), zeros[:]
                             ).then_inc(zeros_out, 16)
            sp.wait_ge(zeros_out, 16 * E)

        sure_units = 2 * TILES * P // unit
        most_units = results.shape[0] // unit - 1

        @block.scalar
        def _(act):
            act.wait_ge(zeros_done, 1)
            for n in range(sure_units + 1, most_units + 1):
                act.dma_start(results[n * unit:(n + 1) * unit, :].rearrange("(n p) d -> p n d", p=P), zeros[:]
                              ).then_inc(unreached_out, 16)
            act.wait_ge(unreached_out, 16 * (most_units - sure_units))

        @block.gpsimd
        def _(pool):
            nc.gpsimd.memset(zeros[:], 0.0).then_inc(zeros_done, 1)

        @block.vector
        def _(dve):
            steps = [0]

            def then(ins):
                steps[0] += 1
                ins.then_inc(step, 1)
                dve.wait_ge(step, steps[0])

            nc.vector.tensor_copy(count_i[:], route["count"][0:1, :]).then_inc(counted, 1)
            dve.wait_ge(starts_in, 16)
            then(nc.vector.tensor_tensor(begun[:], route["count"][:].unsqueeze(2).to_broadcast([P, E, STARTS]),
                                         starts[:].unsqueeze(1).to_broadcast([P, E, STARTS]), ALU.is_gt))
            then(nc.vector.tensor_reduce(taken[:], begun[:], X, ALU.add))
            then(nc.vector.memset(before[:], 0.0))
            for e in range(E):
                then(nc.vector.tensor_tensor(before[:, e + 2:e + 3], before[:, e + 1:e + 2], taken[:, e:e + 1], ALU.add))
            then(nc.vector.tensor_copy(units[:], before[0:1, :]))
            then(nc.vector.tensor_scalar(first_row[:], before[:, 1:E + 1], float(unit), float(unit), ALU.mult, ALU.add))
            for c in range(2):
                then(nc.vector.tensor_tensor(by_expert[:], route["onehot"][c][:],
                                             first_row[:].unsqueeze(1).to_broadcast([P, TILES, E]), ALU.mult))
                then(nc.vector.tensor_reduce(row_f[:], by_expert[:], X, ALU.add))
                then(nc.vector.tensor_tensor(row_f[:], row_f[:], route["rank"][c][:], ALU.add))
                then(nc.vector.tensor_copy(route["row"][c][:], row_f[:]))


def moe_phase(nc, units, slots, w_pack, b_pack, results, ident_dram, capacity, most_tokens):
    D = slots.shape[1]
    KD = D // P
    E, _, WN = w_pack.shape
    F = WN // (2 * KD)
    KF = F // P
    U = 256
    NH = U // P
    MAX_UNITS = most_tokens // U
    GROUP = 4
    MOST = results.shape[0] // U - 1
    with ExitStack() as ctx:
        def sb(n, s, d=F32):
            return ctx.enter_context(nc.sbuf_tensor("e" + n, s, d))

        def psum(n, s):
            return ctx.enter_context(nc.psum_tensor("e" + n, s, F32))

        primed = []
        ctx.callback(nc.clear_and_free_semaphores, primed)

        def sem(n):
            primed.append(nc.alloc_semaphore("e" + n))
            return primed[-1]

        ident = sb("ident", [P, P])
        stage = sb("stage", [P, WN])
        w_hi = [sb(f"w_hi{b}", [P, WN], F32R) for b in range(2)]
        w_lo = [sb(f"w_lo{b}", [P, WN], F32R) for b in range(2)]
        bias = sb("bias", [P, 2, KF + D])
        x = sb("x", [P, NH, D])
        xT_hi = sb("xT_hi", [P, KD, U], F32R)
        xT_lo = sb("xT_lo", [P, KD, U], F32R)
        h = sb("h", [P, 4, U])
        h_hi = sb("h_hi", [P, KF, U], F32R)
        h_lo = sb("h_lo", [P, KF, U], F32R)
        y = sb("y", [P, NH, D])
        psH = [psum(f"psH{b}", [P, U]) for b in range(4)]
        psT = psum("psT", [P, KD, U])
        psY = [psum(f"psY{n}", [P, D]) for n in range(NH)]

        ident_in = sem("ident_in")
        staged = sem("staged")
        bias_in = [sem(f"bias_in{b}") for b in range(2)]
        hi_done = sem("hi_done")
        lo_done = sem("lo_done")
        x_in = sem("x_in")
        xT_ps = sem("xT_ps")
        xT_hi_done = sem("xT_hi_done")
        xT_done = sem("xT_done")
        h_ps = sem("h_ps")
        h_act = sem("h_act")
        h_hi_done = sem("h_hi_done")
        h_done = sem("h_done")
        y_ps = sem("y_ps")
        y_done = sem("y_done")
        y_out = sem("y_out")

        unwatched = {n.engine: sem(f"unwatched{q}") for q, n in
                     enumerate((nc.sync, nc.gpsimd, nc.tensor, nc.scalar, nc.vector))}

        by_gpsimd = [staged, *bias_in]
        prime(nc, [s for s in primed if s not in by_gpsimd])
        block = ctx.enter_context(nc.Block())

        def w1(buf, k, m):
            return buf[:, k * F + m * P:k * F + (m + 1) * P]

        def w2(buf, k):
            return buf[:, KD * F + k * D:KD * F + (k + 1) * D]

        def wait_alone(eng, semaphore, value):
            eng.wait_ge(semaphore, value)
            eng.sem_inc(unwatched[eng.engine], 1)

        def for_units(eng, per_expert, per_unit):
            with eng.Fori(0, E // 2) as pair:
                for b in range(2):
                    e = 2 * pair + b
                    before = eng.value_load(units[0:1, bass.ds(e + 1, 1)], min_val=0, max_val=MOST)
                    upto = eng.value_load(units[0:1, bass.ds(e + 2, 1)], min_val=0, max_val=MOST)
                    per_expert(e, b, before, upto)
                    with eng.Fori(before, before + MAX_UNITS, GROUP) as g0:
                        with eng.If(g0 < upto):
                            with eng.Fori(g0, g0 + GROUP) as g:
                                with eng.If(g < upto):
                                    per_unit(e, b, g - before, g)

        @block.sync
        def _(sp):
            sp.dma_start(ident[:], ident_dram).then_inc(ident_in, 16)
            def per_unit(e, b, t, g):
                sp.wait_ge(xT_ps, PRIMED + g)
                row = nc.s_assert_within(e * capacity + t * U, 0, E * capacity - U, skip_runtime_bounds_check_because="g stays within the units counted")
                sp.dma_start(x[:], slots[bass.ds(row, U), :].rearrange("(n p) d -> p n d", p=P)).then_inc(x_in, 16)

            for_units(sp, lambda *_: None, per_unit)
            total = sp.value_load(units[0:1, E + 1:E + 2], min_val=0, max_val=MOST)
            sp.wait_ge(xT_ps, PRIMED + total)
            sp.dma_start(x[:], slots[0:U, :].rearrange("(n p) d -> p n d", p=P)).then_inc(x_in, 16)
            wait_alone(sp, x_in, PRIMED + 16 * total + 16)

        @block.gpsimd
        def _(pool):
            pool.dma_start(stage[:], w_pack[0]).then_inc(staged, 16)
            with pool.Fori(0, E // 2) as pair:
                for b in range(2):
                    e = 2 * pair + b
                    held = pool.value_load(units[0:1, bass.ds(e, 1)], min_val=0, max_val=MOST)
                    wait_alone(pool, y_ps, PRIMED + held)
                    pool.wait_ge(y_done, PRIMED + NH * held + 1)
                    pool.dma_start(bias[:, b], b_pack[e]).then_inc(bias_in[b], 16)
                    wait_alone(pool, staged, 16 * (e + 1))
                    nc.gpsimd.tensor_copy(w_hi[b][:], stage[:]).then_inc(hi_done, 1)
                    pool.wait_ge(hi_done, PRIMED + e + 1)
                    nc.gpsimd.tensor_tensor(w_lo[b][:], stage[:], w_hi[b][:], ALU.subtract).then_inc(lo_done, 1)
                    pool.wait_ge(lo_done, PRIMED + e + 1)
                    pool.dma_start(stage[:], w_pack[(e + 1) % E]).then_inc(staged, 16)
            pool.wait_ge(staged, 16 * (E + 1))

        @block.tensor
        def _(pe):
            def transposes():
                for k in range(KD):
                    for n in range(NH):
                        last = nc.tensor.transpose(psT[:, k, n * P:(n + 1) * P], x[:, n, k * P:(k + 1) * P], ident[:])
                last.then_inc(xT_ps, 1)

            def per_expert(e, b, before, upto):
                wait_alone(pe, lo_done, PRIMED + e + 1)

            def per_unit(e, b, t, g):
                pe.wait_ge(xT_done, PRIMED + g + 1)
                for m in range(KF):
                    if m < 4:
                        pe.wait_ge(h_done, PRIMED + KF * g)
                    else:
                        pe.wait_ge(h_act, PRIMED + KF * g + m - 3)
                    for k in range(KD):
                        for n, (w, v) in enumerate(((w_hi, xT_hi), (w_hi, xT_lo), (w_lo, xT_hi))):
                            last = nc.tensor.matmul(psH[m % 4][:], w1(w[b], k, m), v[:, k, :], start=(k == 0 and n == 0),
                                                    stop=(k == KD - 1 and n == 2))
                    last.then_inc(h_ps, 1)
                pe.wait_ge(x_in, PRIMED + 16 * g + 32)
                transposes()
                pe.wait_ge(y_done, PRIMED + NH * g + 1)
                for n in range(NH):
                    for k in range(KF):
                        if n == 0:
                            pe.wait_ge(h_done, PRIMED + KF * g + k + 1)
                        for q, (v, w) in enumerate(((h_hi, w_hi), (h_lo, w_hi), (h_hi, w_lo))):
                            last = nc.tensor.matmul(psY[n][:], v[:, k, n * P:(n + 1) * P], w2(w[b], k),
                                                    start=(k == 0 and q == 0), stop=(k == KF - 1 and q == 2))
                last.then_inc(y_ps, 1)

            pe.wait_ge(ident_in, PRIMED + 16)
            pe.wait_ge(x_in, PRIMED + 16)
            transposes()
            for_units(pe, per_expert, per_unit)

        @block.scalar
        def _(act):
            def store(g):
                act.wait_ge(y_done, PRIMED + NH * g + 1)
                act.dma_start(results[bass.ds(nc.s_assert_within(g * U, 0, MOST * U, skip_runtime_bounds_check_because="g stays within the units counted"), U), :].rearrange("(n p) d -> p n d", p=P), y[:]).then_inc(y_out, 16)

            def per_expert(e, b, before, upto):
                wait_alone(act, bias_in[b], 8 * (e - b) + 16)

            def per_unit(e, b, t, g):
                for m in range(KF):
                    act.wait_ge(h_ps, PRIMED + KF * g + m + 1)
                    if m >= 4:
                        act.wait_ge(h_done, PRIMED + KF * g + m - 3)
                    nc.scalar.activation(h[:, m % 4], psH[m % 4][:], ACT.Relu, bias=bias[:, b, m:m + 1]).then_inc(h_act, 1)
                    if m == 3:
                        store(g)

            for_units(act, per_expert, per_unit)
            total = act.value_load(units[0:1, E + 1:E + 2], min_val=0, max_val=MOST)
            store(total)
            wait_alone(act, y_out, PRIMED + 16 * total + 16)

        @block.vector
        def _(dve):
            def transposed(g):
                dve.wait_ge(xT_ps, PRIMED + g + 1)
                nc.vector.tensor_copy(xT_hi[:], psT[:]).then_inc(xT_hi_done, 1)
                dve.wait_ge(xT_hi_done, PRIMED + g + 1)
                nc.vector.tensor_tensor(xT_lo[:], psT[:], xT_hi[:], ALU.subtract).then_inc(xT_done, 1)

            def per_expert(e, b, before, upto):
                wait_alone(dve, bias_in[b], 8 * (e - b) + 16)

            def per_unit(e, b, t, g):
                for m in range(KF):
                    dve.wait_ge(h_act, PRIMED + KF * g + m + 1)
                    nc.vector.tensor_copy(h_hi[:, m], h[:, m % 4]).then_inc(h_hi_done, 1)
                    dve.wait_ge(h_hi_done, PRIMED + KF * g + m + 1)
                    nc.vector.tensor_tensor(h_lo[:, m], h[:, m % 4], h_hi[:, m], ALU.subtract).then_inc(h_done, 1)
                transposed(g + 1)
                dve.wait_ge(y_ps, PRIMED + g + 1)
                dve.wait_ge(y_out, PRIMED + 16 * g + 16)
                for n in range(NH):
                    nc.vector.tensor_tensor(y[:, n], psY[n][:], bias[:, b, KF:], ALU.add).then_inc(y_done, 1)

            nc.vector.memset(y[:], 0.0).then_inc(y_done, 1)
            dve.wait_ge(ident_in, PRIMED + 16)
            transposed(0)
            for_units(dve, per_expert, per_unit)


def heads_phase(nc, x1_in, results, route, wkv3, wq3, wp, bp_row, ident_dram, mask_dram, maskT_dram,
                x3_out, batches):
    T, D = x1_in.shape
    KD = D // P
    SEQ = T // batches
    NT = SEQ // P
    BANK = 512
    HALVES = SEQ // BANK
    PER = BANK // P
    HEADS = wq3.shape[2]
    HD = wq3.shape[3] // 3
    SCALE = float(D) ** -0.5
    with ExitStack() as ctx:
        def sb(n, s, d=F32):
            return ctx.enter_context(nc.sbuf_tensor("m" + n, s, d))

        def psum(n, s):
            return ctx.enter_context(nc.psum_tensor("m" + n, s, F32))

        primed = []
        ctx.callback(nc.clear_and_free_semaphores, primed)

        def sem(n):
            primed.append(nc.alloc_semaphore("m" + n))
            return primed[-1]

        ident, ident_bf, mask_bf, maskT_bf = (sb(n, [P, P], d) for n, d in (
            ("ident", F32), ("ident_bf", BF16), ("mask_bf", BF16), ("maskT_bf", BF16)))
        wkv_raw = sb("wkv_raw", [P, KD, P])
        wkv_hi, wkv_lo = (sb(n, [P, KD, P], F32R) for n in ("wkv_hi", "wkv_lo"))
        wq_raw = sb("wq_raw", [P, KD, HEADS, 3 * HD])
        wq_hi, wq_lo = (sb(n, [P, KD, HEADS, 3 * HD], F32R) for n in ("wq_hi", "wq_lo"))
        wp_sb = sb("wp", [P, KD, D])
        bp = sb("bp", [P, D])
        x1 = sb("x1", [P, NT, D])
        y = [sb(f"y{c}", [P, NT, D]) for c in range(2)]
        x2 = sb("x2", [P, NT, D])
        res = sb("res", [P, NT, D])
        x2T_hi, x2T_lo = (sb(n, [P, KD, SEQ], F32R) for n in ("x2T_hi", "x2T_lo"))
        kvT = sb("kvT", [P, SEQ])
        k_rows = sb("k_rows", [P, SEQ], F32R)
        q_rows = [sb(f"q_rows{n}", [P, SEQ], F32R) for n in range(2)]
        v1 = sb("v1", [P, NT, 2 * HD])
        prob = [sb(f"prob{n}", [P, BANK]) for n in range(3)]
        nmax = sb("nmax", [P, NT])
        nmT_hi, nmT_lo = (sb(n, [NT, P], F32R) for n in ("nmT_hi", "nmT_lo"))
        sums = sb("sums", [P, KD, SEQ])
        att = sb("att", [P, KD, SEQ])
        z = sb("z", [P, NT, D])
        st, stA = (sb(n, [P, NT, 6]) for n in ("st", "stA"))
        mv, mvA = (sb(n, [P, NT, 2]) for n in ("mv", "mvA"))
        rstd, var, tmp = (sb(n, [P, NT]) for n in ("rstd", "var", "tmp"))
        shifted = sb("shifted", [P, NT], I32)
        rows_now = [sb(f"rows_now{c}", [P, NT], I32) for c in range(2)]
        weight_now = sb("weight_now", [P, 2, NT])
        unread = sb("unread", [1, 1])
        out_row = sb("out_row", [P, NT, D])
        S = [psum(f"S{n}", [P, SEQ]) for n in range(2)]
        ST = [psum(f"ST{n}", [P, BANK]) for n in range(2)]
        O = [psum(f"O{n}", [P, BANK]) for n in range(HALVES)]

        names = ("const_in setup x1_in y_in rows_ready x2_done res_done t_ps t_hi t_lo kv_ps kv_sb k_hi k_lo v_ps "
                 "v_done q_ps q_hi q_lo s_ps mx nm_ps nm_hi nm_lo st_ps ex pv_ps o_used att_done pr_ps z_done chain x3_done "
                 "x3_st st_done stA_done").split()
        (const_in, setup, x1_ld, y_in, rows_ready, x2_done, res_done, t_ps, t_hi, t_lo, kv_ps, kv_sb, k_hi, k_lo, v_ps,
         v_done, q_ps, q_hi, q_lo, s_ps, mx, nm_ps, nm_hi, nm_lo, st_ps, ex, pv_ps, o_used, att_done, pr_ps, z_done, chain,
         x3_done, x3_st, st_done, stA_done) = (sem(n) for n in names)
        nm_in = [sem(f"nm_in{n}") for n in range(2)]
        unwatched = {n.engine: sem(f"unwatched{q}") for q, n in
                     enumerate((nc.sync, nc.gpsimd, nc.tensor, nc.scalar, nc.vector))}
        loads = [(ident[:], ident_dram), (z[:, 0, :P], mask_dram), (z[:, 1, :P], maskT_dram), (wkv_raw[:], wkv3), (wq_raw[:], wq3), (wp_sb[:], wp), (bp[:], bp_row)]
        N_CONST = 16 * len(loads)
        SETUP = 2 + 5 + 2 * HALVES

        chunks = [(half, t) for half in range(HALVES) for t in range(PER * (half + 1))]
        NCH = len(chunks)
        TILES_AT = {4: (0, 1, 2), 5: (3, 4, 5), 6: (6, 7)}
        PIECE = SEQ // 4
        assert HEADS == 8 and NT == 8

        by_gpsimd = [y_in, *nm_in]
        prime(nc, [s for s in primed if s not in by_gpsimd])
        block = ctx.enter_context(nc.Block())

        def wait_alone(eng, semaphore, value):
            eng.wait_ge(semaphore, value)
            eng.sem_inc(unwatched[eng.engine], 1)

        def tokens(ap, b):
            return ap.rearrange("(b t p) d -> b p t d", t=NT, p=P)[b]

        def each_sequence(eng, body):
            with eng.Fori(0, batches - 1) as b:
                body(b, True)
            body(batches - 1, False)

        @block.sync
        def _(sp):
            for d, s in loads:
                sp.dma_start(d, s).then_inc(const_in, 16)
            sp.dma_start(x1[:], tokens(x1_in, 0)).then_inc(x1_ld, 16)

            def sequence(b, more):
                if more:
                    sp.wait_ge(x2_done, PRIMED + b + 1)
                    sp.dma_start(x1[:], tokens(x1_in, b + 1)).then_inc(x1_ld, 16)
                sp.wait_ge(x3_done, PRIMED + b + 1)
                sp.dma_start(tokens(x3_out, b), out_row[:]).then_inc(x3_st, 16)

            each_sequence(sp, sequence)
            sp.wait_ge(x3_st, PRIMED + 16 * batches)

        @block.gpsimd
        def _(pool):
            def gather(t):
                for c in range(2):
                    pool.indirect_dma_start(out=y[c][:, t, :], out_offset=None, in_=results,
                                            in_offset=bass.IndirectOffsetOnAxis(ap=rows_now[c][:, t:t + 1], axis=0)
                                            ).then_inc(y_in, 16)

            pool.wait_ge(const_in, PRIMED + N_CONST)
            pool.wait_ge(rows_ready, PRIMED + 1)
            for t in range(NT):
                gather(t)

            def sequence(b, more):
                pool.wait_ge(z_done, PRIMED + NT * b)
                pool.wait_ge(x2_done, PRIMED + b + 1)
                nc.gpsimd.tensor_tensor(res[:], x2[:], bp[:].unsqueeze(1).to_broadcast([P, NT, D]), ALU.add).then_inc(res_done, 1)
                for h in range(HEADS):
                    n = HEADS * b + h
                    for r, (row, ready) in enumerate(((nmT_hi, nm_hi), (nmT_lo, nm_lo))):
                        wait_alone(pool, ready, PRIMED + n + 1)
                        pool.dma_start(q_rows[h % 2][3 * HD + r:3 * HD + r + 1, :].rearrange("o (t q) -> o t q", q=P),
                                       row[:]).then_inc(nm_in[h % 2], 16)
                    if more and h < 4:
                        if h == 0:
                            wait_alone(pool, rows_ready, PRIMED + b + 2)
                        gather(2 * h)
                        gather(2 * h + 1)

            each_sequence(pool, sequence)
            for n in range(2):
                pool.wait_ge(nm_in[n], 16 * HEADS * batches)

        @block.tensor
        def _(pe):
            def three(ps, left, right, first, last):
                (lh, ll), (rh, rl) = left, right
                nc.tensor.matmul(ps, lh, rh, start=first, stop=False)
                nc.tensor.matmul(ps, lh, rl, start=False, stop=False)
                return nc.tensor.matmul(ps, ll, rh, start=False, stop=last)

            def bank(n):
                return slice(n * BANK, (n + 1) * BANK)

            def tile(n):
                return slice(n * P, (n + 1) * P)

            def project_q(b, h):
                n = HEADS * b + h
                if h:
                    pe.wait_ge(mx, PRIMED + NT * n)
                else:
                    pe.wait_ge(t_lo, PRIMED + KD * b + 1)
                for c in range(HALVES):
                    for k in range(KD):
                        last = three(S[0][:3 * HD, bank(c)], (wq_hi[:, k, h, :], wq_lo[:, k, h, :]),
                                     (x2T_hi[:, k, bank(c)], x2T_lo[:, k, bank(c)]), k == 0, k == KD - 1)
                last.then_inc(q_ps, 1)

            def scores(b, h, i):
                n = HEADS * b + h
                if i == 0:
                    if h:
                        pe.wait_ge(nm_lo, PRIMED + n)
                    else:
                        pe.wait_ge(t_lo, PRIMED + KD * b + 2)
                        pe.wait_ge(k_lo, PRIMED + HALVES * (b + 1))
                    pe.wait_ge(q_lo, PRIMED + n + 1)
                elif i >= 2:
                    pe.wait_ge(mx, PRIMED + NT * n + i - 1)
                s = S[(i + 1) % 2]
                width = (i + 1) * P
                for c in range(0, width, BANK):
                    c1 = min(width, c + BANK)
                    nc.tensor.matmul(s[:, c:c1], q_rows[h % 2][:3 * HD, tile(i)], k_rows[:3 * HD, c:c1], start=True, stop=True)
                nc.tensor.matmul(s[:, i * P:width], ident_bf[:], mask_bf[:], start=False, stop=True,
                                 skip_group_check=True).then_inc(s_ps, 1)

            def transpose_max(b, h):
                n = HEADS * b + h
                pe.wait_ge(mx, PRIMED + NT * (n + 1))
                nc.tensor.transpose(S[1][:NT, :P], nmax[:], ident[:]).then_inc(nm_ps, 1)

            def scores_T(b, h, c):
                n = HEADS * b + h
                half, t = chunks[c]
                if c == 0:
                    pe.wait_ge(nm_in[h % 2], 16 * HEADS * b + 32 * (h // 2 + 1))
                if h == 0 and c < 2:
                    pe.wait_ge(v_done, PRIMED + 2 * (b + 1))
                else:
                    pe.wait_ge(ex, PRIMED + NCH * n + c - 1)
                off = max(0, t - PER * half) * P
                last = nc.tensor.matmul(ST[c % 2][:, off:], k_rows[:, tile(t)],
                                        q_rows[h % 2][:, half * BANK + off:(half + 1) * BANK], start=True, stop=True)
                if t >= PER * half:
                    last = nc.tensor.matmul(ST[c % 2][:, off:off + P], ident_bf[:], maskT_bf[:], start=False, stop=True,
                                            skip_group_check=True)
                last.then_inc(st_ps, 1)

            def weigh(b, h, c):
                n = HEADS * b + h
                half, t = chunks[c]
                if t == 0 and h:
                    pe.wait_ge(o_used, PRIMED + HALVES * (n - 1) + half + 1)
                pe.wait_ge(ex, PRIMED + NCH * n + c + 1)
                off = max(0, t - PER * half) * P
                nc.tensor.matmul(O[half][:2 * HD, off:], v1[:, t, :], prob[c % 3][:, off:], start=(t == 0), stop=True,
                                 skip_group_check=(t > 0)).then_inc(pv_ps, 1)

            pe.wait_ge(const_in, PRIMED + N_CONST)
            pe.wait_ge(setup, PRIMED + SETUP)

            def sequence(b, more):
                pe.wait_ge(z_done, PRIMED + NT * b)
                pe.wait_ge(x2_done, PRIMED + b + 1)
                for k in range(KD):
                    for t in range(NT):
                        last = nc.tensor.transpose(S[k][:, tile(t)], x2[:, t, tile(k)], ident[:])
                    last.then_inc(t_ps, 1)
                pe.wait_ge(t_lo, PRIMED + KD * b + KD)
                pe.wait_ge(o_used, PRIMED + HALVES * HEADS * b)
                for c in range(HALVES):
                    for k in range(KD):
                        last = three(O[c][:], (wkv_hi[:, k, :], wkv_lo[:, k, :]),
                                     (x2T_hi[:, k, bank(c)], x2T_lo[:, k, bank(c)]), k == 0, k == KD - 1)
                    last.then_inc(kv_ps, 1)
                project_q(b, 0)
                pe.wait_ge(ex, PRIMED + NCH * HEADS * b)
                for c in range(HALVES):
                    pe.wait_ge(kv_sb, PRIMED + HALVES * b + c + 1)
                    for n in range(PER):
                        last = nc.tensor.transpose(ST[c][:, tile(n)], kvT[:, tile(PER * c + n)], ident[:])
                    last.then_inc(v_ps, 1)
                for i in range(NT):
                    scores(b, 0, i)
                transpose_max(b, 0)
                for h in range(HEADS):
                    if h + 1 < HEADS:
                        project_q(b, h + 1)
                    scores_T(b, h, 0)
                    for c in range(NCH):
                        if c + 1 < NCH:
                            scores_T(b, h, c + 1)
                        if h + 1 < HEADS:
                            if c < NT:
                                scores(b, h + 1, c)
                            if c == NT + 1:
                                transpose_max(b, h + 1)
                        weigh(b, h, c)
                for i in range(NT):
                    if i % 2 == 0:
                        pe.wait_ge(att_done, PRIMED + 8 * b + 4 + i // 2 + 1)
                    if i >= 2:
                        pe.wait_ge(z_done, PRIMED + NT * b + i - 1)
                    for k in range(KD):
                        last = nc.tensor.matmul(S[i % 2][:, :D], att[:, k, tile(i)], wp_sb[:, k, :], start=(k == 0),
                                                stop=(k == KD - 1))
                    last.then_inc(pr_ps, 1)

            each_sequence(pe, sequence)

        @block.scalar
        def _(act):
            act.wait_ge(const_in, PRIMED + N_CONST)
            nc.scalar.activation(wkv_hi[:], wkv_raw[:], ACT.Copy).then_inc(setup, 1)
            nc.scalar.activation(wq_hi[:], wq_raw[:], ACT.Copy).then_inc(setup, 1)

            def copy_out(b, h, half):
                act.wait_ge(pv_ps, PRIMED + NCH * (HEADS * b + h) + PER + half * (NCH - PER))
                rows = slice(h % PER * HD, (h % PER + 1) * HD)
                cols = slice(half * BANK, (half + 1) * BANK)
                if h == 0 and half == 0:
                    act.wait_ge(pr_ps, PRIMED + NT * b)
                nc.scalar.activation(att[rows, h // PER, cols], O[half][:HD, :], ACT.Copy)
                nc.scalar.activation(sums[rows, h // PER, cols], O[half][HD:2 * HD, :], ACT.Copy).then_inc(o_used, 1)

            def q_high(b, h):
                act.wait_ge(q_ps, PRIMED + HEADS * b + h + 1)
                nc.scalar.activation(q_rows[h % 2][:3 * HD, :], S[0][:3 * HD, :], ACT.Copy, scale=SCALE).then_inc(q_hi, 1)

            def sequence(b, more):
                for k in range(KD):
                    act.wait_ge(t_ps, PRIMED + KD * b + k + 1)
                    nc.scalar.activation(x2T_hi[:, k, :], S[k][:], ACT.Copy).then_inc(t_hi, 1)
                for c in range(HALVES):
                    act.wait_ge(kv_ps, PRIMED + HALVES * b + c + 1)
                    cols = slice(c * BANK, (c + 1) * BANK)
                    nc.scalar.activation(k_rows[:3 * HD, cols], O[c][:3 * HD, :], ACT.Copy).then_inc(k_hi, 1)
                    nc.scalar.activation(kvT[:, cols], O[c][:], ACT.Copy).then_inc(kv_sb, 1)
                q_high(b, 0)
                for h in range(HEADS):
                    if h + 1 < HEADS:
                        q_high(b, h + 1)
                    n = HEADS * b + h
                    for c, (half, t) in enumerate(chunks):
                        off = max(0, t - PER * half) * P
                        act.wait_ge(st_ps, PRIMED + NCH * n + c + 1)
                        if h or c >= 3:
                            act.wait_ge(pv_ps, PRIMED + NCH * n + c - 2)
                        nc.scalar.activation(prob[c % 3][:, off:], ST[c % 2][:, off:], ACT.Exp).then_inc(ex, 1)
                        if c == 1 and h:
                            copy_out(b, h - 1, 1)
                        if c == PER + 2:
                            copy_out(b, h, 0)
                copy_out(b, HEADS - 1, 1)

            each_sequence(act, sequence)

        @block.vector
        def _(dve):
            dve.wait_ge(const_in, PRIMED + N_CONST)
            dve.wait_ge(setup, PRIMED + 2)
            nc.vector.tensor_tensor(wkv_lo[:], wkv_raw[:], wkv_hi[:], ALU.subtract).then_inc(setup, 1)
            nc.vector.tensor_tensor(wq_lo[:], wq_raw[:], wq_hi[:], ALU.subtract).then_inc(setup, 1)
            nc.vector.tensor_copy(ident_bf[:], ident[:])
            nc.vector.tensor_copy(mask_bf[:], z[:, 0, :P])
            nc.vector.tensor_copy(maskT_bf[:], z[:, 1, :P])
            nc.vector.memset(v1[:], 1.0).then_inc(setup, 1)
            nc.vector.memset(prob[0][:], 0.0).then_inc(setup, 1)
            nc.vector.memset(prob[1][:], 1.0).then_inc(setup, 1)
            dve.wait_ge(setup, PRIMED + SETUP - 4)
            rows = slice(3 * HD, 4 * HD)
            for n in range(HALVES):
                cols = slice(n * BANK, (n + 1) * BANK)
                for m in range(2):
                    nc.vector.tensor_copy(q_rows[m][rows, cols], prob[0][rows, :])
                nc.vector.tensor_copy(k_rows[rows, cols], prob[0][rows, :]).then_inc(setup, 1)
            dve.wait_ge(setup, PRIMED + SETUP - 2)
            for n in range(HALVES):
                nc.vector.tensor_copy(k_rows[3 * HD:3 * HD + 2, n * BANK:(n + 1) * BANK],
                                      prob[1][3 * HD:3 * HD + 2, :]).then_inc(setup, 1)

            n_link = [0]
            base = [0]

            def link(ins, alone=False):
                n_link[0] += 1
                ins.then_inc(chain, 1)
                (wait_alone if alone else lambda e, s, v: e.wait_ge(s, v))(dve, chain, PRIMED + base[0] + n_link[0])

            def normalised(dst, src, stats, mean_var, done):
                for i in range(NT):
                    ins = nc.vector.bn_aggr(mean_var[:, i], stats[:, i])
                link(ins)
                link(nc.vector.tensor_copy(var[:], mean_var[:, :, 1]))
                rsqrt(nc, link, rstd[:], var[:], tmp[:], shifted[:])
                if dst is out_row:
                    dve.wait_ge(x3_st, PRIMED + 16 * seq[0])
                for i in range(NT):
                    ins = nc.vector.tensor_scalar(dst[:, i], src[:, i], mean_var[:, i, 0:1], rstd[:, i:i + 1], ALU.subtract,
                                                  ALU.mult)
                ins.then_inc(done, 1)

            seq = [0]

            def plan(n):
                cols = bass.ds(n * NT, NT)
                for c in range(2):
                    link(nc.vector.tensor_copy(rows_now[c][:], route["row"][c][:, cols]))
                    link(nc.vector.tensor_copy(weight_now[:, c], route["weight"][c][:, cols]))
                nc.vector.memset(unread[:], 0.0).then_inc(rows_ready, 1)

            def residual(n, t):
                link(nc.vector.scalar_tensor_tensor(x2[:, t], y[0][:, t], weight_now[:, 0, t:t + 1], x1[:, t], ALU.mult, ALU.add))
                link(nc.vector.scalar_tensor_tensor(x2[:, t], y[1][:, t], weight_now[:, 1, t:t + 1], x2[:, t], ALU.mult, ALU.add))
                nc.vector.bn_stats(stA[:, t], x2[:, t]).then_inc(stA_done, 1)

            plan(0)
            dve.wait_ge(y_in, 32 * NT)
            dve.wait_ge(x1_ld, PRIMED + 16)
            for t in range(NT):
                residual(0, t)
            dve.wait_ge(stA_done, PRIMED + NT)
            normalised(x2, x2, stA, mvA, x2_done)
            first_links = n_link[0]
            dve.wait_ge(x2_done, PRIMED + 1)

            def q_low(b, h):
                dve.wait_ge(q_hi, PRIMED + HEADS * b + h + 1)
                part = slice(2 * HD, 3 * HD)
                nc.vector.scalar_tensor_tensor(q_rows[h % 2][part, :], S[0][part, :], SCALE, q_rows[h % 2][part, :], ALU.mult,
                                               ALU.subtract).then_inc(q_lo, 1)

            def row_max(b, h, i):
                dve.wait_ge(s_ps, PRIMED + NT * (HEADS * b + h) + i + 1)
                nc.vector.tensor_reduce(nmax[:, i:i + 1], S[(i + 1) % 2][:, :(i + 1) * P], X, ALU.max, negate=True).then_inc(mx, 1)

            def max_rows(b, h):
                n = HEADS * b + h
                dve.wait_ge(nm_ps, PRIMED + n + 1)
                if h:
                    dve.wait_ge(nm_in[(h - 1) % 2], 16 * HEADS * b + 32 * ((h - 1) // 2 + 1))
                nc.vector.tensor_copy(nmT_hi[:], S[1][:NT, :P]).then_inc(nm_hi, 1)
                dve.wait_ge(nm_hi, PRIMED + n + 1)
                nc.vector.tensor_tensor(nmT_lo[:], S[1][:NT, :P], nmT_hi[:], ALU.subtract).then_inc(nm_lo, 1)

            def normalise(b, group, piece):
                if piece % 2 == 0:
                    dve.wait_ge(o_used, PRIMED + HALVES * (HEADS * b + PER * group + PER - 1) + piece // 2 + 1)
                cols = slice(piece * PIECE, (piece + 1) * PIECE)
                link(nc.vector.reciprocal(sums[:, group, cols], sums[:, group, cols]))
                nc.vector.tensor_tensor(att[:, group, cols], att[:, group, cols], sums[:, group, cols],
                                        ALU.mult).then_inc(att_done, 1)

            def sequence(b, more):
                n_link[0] = 0
                base[0] = first_links + LINKS * b
                seq[0] = b
                if more:
                    plan(b + 1)
                for k in range(KD):
                    dve.wait_ge(t_hi, PRIMED + KD * b + k + 1)
                    nc.vector.tensor_tensor(x2T_lo[:, k, :], S[k][:], x2T_hi[:, k, :], ALU.subtract).then_inc(t_lo, 1)
                part = slice(HD, 2 * HD)
                for c in range(HALVES):
                    cols = slice(c * BANK, (c + 1) * BANK)
                    dve.wait_ge(k_hi, PRIMED + HALVES * b + c + 1)
                    dve.wait_ge(kv_sb, PRIMED + HALVES * b + c + 1)
                    nc.vector.tensor_tensor(k_rows[part, cols], O[c][part, :], k_rows[part, cols],
                                            ALU.subtract).then_inc(k_lo, 1)
                q_low(b, 0)
                for c in range(HALVES):
                    dve.wait_ge(v_ps, PRIMED + HALVES * b + c + 1)
                    nc.vector.tensor_copy(v1[:, PER * c:PER * (c + 1), :HD],
                                          ST[c][:].rearrange("p (t s) -> p t s", s=P)[:, :, 3 * HD:]).then_inc(v_done, 1)
                for i in range(NT):
                    row_max(b, 0, i)
                max_rows(b, 0)
                for h in range(HEADS):
                    following = h + 1 < HEADS
                    if following:
                        q_low(b, h + 1)
                        for i in range(5):
                            row_max(b, h + 1, i)
                    if following:
                        for i in range(5, NT):
                            row_max(b, h + 1, i)
                        max_rows(b, h + 1)
                    if more and h in TILES_AT:
                        if h == min(TILES_AT):
                            dve.wait_ge(y_in, 32 * NT * (b + 2))
                            dve.wait_ge(x1_ld, PRIMED + 16 * (b + 2))
                            dve.wait_ge(res_done, PRIMED + b + 1)
                        for t in TILES_AT[h]:
                            residual(b + 1, t)
                    if more and h == HEADS - 1:
                        wait_alone(dve, stA_done, PRIMED + NT * (b + 2))
                        normalised(x2, x2, stA, mvA, x2_done)
                        dve.wait_ge(x2_done, PRIMED + b + 2)
                    if h >= PER and h < 2 * PER:
                        normalise(b, 0, h - PER)
                for piece in range(4):
                    normalise(b, 1, piece)
                dve.wait_ge(res_done, PRIMED + b + 1)
                for i in range(NT):
                    dve.wait_ge(pr_ps, PRIMED + NT * b + i + 1)
                    nc.vector.tensor_tensor(z[:, i], S[i % 2][:, :D], res[:, i], ALU.add).then_inc(z_done, 1)
                    dve.wait_ge(z_done, PRIMED + NT * b + i + 1)
                    nc.vector.bn_stats(st[:, i], z[:, i]).then_inc(st_done, 1)
                wait_alone(dve, st_done, PRIMED + NT * (b + 1))
                normalised(out_row, z, st, mv, x3_done)
                if more:
                    assert n_link[0] == LINKS, (n_link[0], LINKS)

            LINKS = 4 + 2 * NT + 8 + 2 * (2 + RSQRT_LINKS)
            each_sequence(dve, sequence)


def model_program(nc, t, out):
    T, D = t["x"].shape
    batches = t["xT"].shape[0]
    experts = t["expert_weights"].shape[0]
    tiles = T // P
    capacity = T + UNIT
    most_units = (2 * T) // UNIT + experts - 1
    x1, x3 = (nc.dram_tensor(n, [T, D], F32, kind="Internal").ap() for n in ("x1_dram", "x3_dram"))
    slots = nc.dram_tensor("slots_dram", [experts * capacity, D], F32, kind="Internal").ap()
    results = nc.dram_tensor("results_dram", [(most_units + 1) * UNIT, D], F32, kind="Internal").ap()
    with ExitStack() as ctx:
        def sb(n, s, d=F32):
            return ctx.enter_context(nc.sbuf_tensor(n, s, d))

        weights_exact = sb("weights_exact", [1, 1], I32)
        with ExitStack() as routing:
            def rsb(n, s, d=F32):
                return routing.enter_context(nc.sbuf_tensor(n, s, d))

            units = rsb("units", [1, experts + 2], I32)
            route = dict(weight=[rsb(f"weight{c}", [P, tiles]) for c in range(2)],
                         row=[rsb(f"row{c}", [P, tiles], I32) for c in range(2)])
            with ExitStack() as counting:
                def csb(n, s):
                    return counting.enter_context(nc.sbuf_tensor(n, s, F32))

                route.update(rank=[csb(f"rank{c}", [P, tiles]) for c in range(2)],
                             onehot=[csb(f"onehot{c}", [P, tiles, experts]) for c in range(2)],
                             count=csb("count", [P, experts]))
                attend_and_route_phase(nc, t["x"], t["xT"], t["wqT"], t["wkT"], t["wvT"], t["wo"], t["w_router"],
                                       t["b_router"], t, route, x1, slots, batches, capacity)
                plan_phase(nc, route, units, t["unit_starts"], slots, results, capacity, UNIT)
            moe_phase(nc, units, slots, t["expert_weights"], t["expert_biases"], results, t["ident"], capacity, T)
            heads_phase(nc, x1, results, route, t["wkv"], t["wq"], t["wp"], t["bp"], t["ident"], t["mask"], t["maskT"], x3,
                        batches)
        for split in (True, False):
            ffn_phase(nc, weights_exact, x3, t["w1"], t["w2"], t["h1"], t["h2"], t["w3"], t["ffn_scales"], t["w3_scales"],
                      out, t["ident"], split)


def kernel(**inputs):
    import numpy as np
    import concourse.bacc as bacc
    from concourse.bass_utils import run_bass_kernel_spmd

    a = {n: np.asarray(v) for n, v in inputs.items()}
    f32 = np.float32
    B, S, D = a["L0_attn_x"].shape
    E, _, F = a["L0_ffn_W1"].shape

    def rows(w):
        return w.reshape(-1, P, *w.shape[1:]).swapaxes(0, 1)

    def on_all(v):
        return np.broadcast_to(v, (P, v.shape[0]))

    def by_block(v):
        return v.reshape(-1, P).T

    square = np.ones((P, P), f32)
    Wk, Wv, Wq = a["L1_attn_Wk"], a["L1_attn_Wv"], a["L1_attn_Wq"]
    data = {
        "x": a["L0_attn_x"].reshape(B * S, D),
        "xT": a["L0_attn_x"].reshape(B, S, D // P, P).transpose(0, 3, 2, 1),
        "wqT": rows(a["L0_attn_Wq"].T), "wkT": rows(a["L0_attn_Wk"].T), "wvT": rows(a["L0_attn_Wv"].T),
        "wo": rows(a["L0_attn_Wo"]),
        "w_router": rows(a["L0_ffn_W_router"]), "b_router": on_all(a["L0_ffn_b_router"]),
        "expert_weights": np.concatenate([
            a["L0_ffn_W1"].reshape(E, D // P, P, F).transpose(0, 2, 1, 3).reshape(E, P, -1),
            a["L0_ffn_W2"].reshape(E, F // P, P, D).transpose(0, 2, 1, 3).reshape(E, P, -1)], 2),
        "expert_biases": np.concatenate([
            a["L0_ffn_b1"].reshape(E, F // P, P).transpose(0, 2, 1),
            np.broadcast_to(a["L0_ffn_b2"][:, None], (E, P, D))], 2),
        "wkv": rows(np.concatenate([Wk, Wk, Wk, Wv], 1)),
        "wq": rows(np.concatenate([Wq, Wq, Wq], 2).transpose(1, 0, 2)),
        "wp": rows(a["L1_attn_Wp"]), "bp": on_all(a["L1_attn_bp"]),
        "w1": rows(a["L1_ffn_w1_w"].T), "w2": rows(a["L1_ffn_w2_w"].T), "h1": rows(a["L1_ffn_h1_w"].T),
        "h2": rows(a["L1_ffn_h2_w"].T), "w3": rows(a["L1_ffn_w3_w"].T),
        "ffn_scales": np.stack([by_block(a[f"L1_ffn_{n}_s"]) for n in ("w1", "w2", "h1", "h2")], 1),
        "w3_scales": on_all(a["L1_ffn_w3_s"]),
        "ident": np.eye(P, dtype=f32), "mask": np.triu(square, 1) * f32(-1e30), "maskT": np.tril(square, -1) * f32(-1e30),
        "before_me": np.triu(square, 1), "all_ones": square, "iota_e": on_all(np.arange(E, dtype=f32)),
        "unit_starts": on_all(np.arange(0, B * S, UNIT, dtype=f32)),
    }
    nc = bacc.Bacc("TRN2", target_bir_lowering=False, num_devices=1)
    arrays = {n + "_dram": np.ascontiguousarray(v) for n, v in data.items()}
    t = {n[:-5]: nc.dram_tensor(n, v.shape, mybir.dt.from_np(v.dtype), kind="ExternalInput").ap()
         for n, v in arrays.items()}
    out = nc.dram_tensor("out_dram", [B * S, D], F32, kind="ExternalOutput").ap()
    model_program(nc, t, out)
    result = run_bass_kernel_spmd(nc, [arrays], core_ids=[0])
    return result.results[0]["out_dram"].reshape(B, S, D)
```

```python
from contextlib import ExitStack

import concourse.bass as bass
from concourse import mybir
from concourse.alu_op_type import AluOpType as ALU

F32 = mybir.dt.float32
F32R = mybir.dt.float32r
BF16 = mybir.dt.bfloat16
I32 = mybir.dt.int32
U32 = mybir.dt.uint32
ACT = mybir.ActivationFunctionType
X = mybir.AxisListType.X
P = 128
EPS = 1e-5
PRIMED = 1
UNIT = 256


def prime(nc, semaphores):
    with nc.Block() as block:
        @block.gpsimd
        def _(pool):
            for semaphore in semaphores:
                pool.sem_inc(semaphore, PRIMED)


RSQRT_STEPS = 3
RSQRT_LINKS = 3 + 3 * RSQRT_STEPS


def rsqrt_guess(engine, link, y, v, shifted):
    link(engine.tensor_scalar(v, v, EPS, None, ALU.add))
    link(engine.tensor_scalar(shifted, v.bitcast(I32), 1, None, ALU.logical_shift_right))
    link(engine.tensor_scalar(y.bitcast(I32), shifted, -1, 0x5F3759DF, ALU.mult, ALU.add))


def rsqrt_newton(engine, link, y, v, t):
    for _ in range(RSQRT_STEPS):
        link(engine.tensor_tensor(t, y, v, ALU.mult))
        link(engine.tensor_tensor(t, t, y, ALU.mult))
        link(engine.tensor_scalar(t, t, -0.5, 1.5, ALU.mult, ALU.add))
        link(engine.tensor_tensor(y, t, y, ALU.mult))


def rsqrt(nc, link, y, v, t, shifted):
    rsqrt_guess(nc.vector, link, y, v, shifted)
    for _ in range(RSQRT_STEPS):
        link(nc.vector.scalar_tensor_tensor(t, y, -0.5, v, ALU.mult, ALU.mult))
        link(nc.vector.tensor_tensor(t, t, y, ALU.mult))
        link(nc.vector.scalar_tensor_tensor(y, t, 1.5, y, ALU.add, ALU.mult))


FFN_PIECE = 1024


def ffn_phase(nc, flag, x_in, ffn_weights, s_cols, s3_row, out, ident_dram, split):
    T, D = x_in.shape
    KD = D // P
    KF = 1024 // P
    FH = KF * P
    CH = 512
    NT = CH // P
    PAIRS = T // CH // 2
    WDT = F32R if split else F32
    name = "f" if split else "g"
    with ExitStack() as ctx:
        def sb(n, s, d=F32):
            return ctx.enter_context(nc.sbuf_tensor(name + n, s, d))

        primed = []
        ctx.callback(nc.clear_and_free_semaphores, primed)

        def sem(n):
            primed.append(nc.alloc_semaphore(name + n))
            return primed[-1]

        parts = 2 if split else 1
        w1_sb, w2_sb = (sb(n, [P, KD, FH], WDT) for n in ("w1", "w2"))
        h1_sb, h2_sb = (sb(n, [P, KF, FH], WDT) for n in ("h1", "h2"))
        w3_sb = sb("w3", [P, KF, D], WDT)
        ident = sb("ident", [P, P])
        scl = sb("scl", [P, 4, KF])
        half = sb("half", [P, 2, KF])
        s3 = sb("s3", [P, D])
        x = sb("x", [P, 2, NT, D])
        xT = [sb(f"xT{q}", [P, KD, CH], WDT) for q in range(parts)]
        ha = [sb(f"ha{q}", [P, KF, CH], WDT) for q in range(parts)]
        hb = [sb(f"hb{q}", [P, KF, CH], WDT) for q in range(parts)]
        t = sb("t", [P, 2, CH])
        a = sb("a", [P, 2, CH])
        g = sb("g", [P, 2, CH])
        z = sb("z", [P, NT, D])
        st = sb("st", [P, NT, 6])
        mv = sb("mv", [P, NT, 2])
        rstd, var, tmp = (sb(n, [P, NT]) for n in ("rstd", "var", "tmp"))
        shifted = sb("shifted", [P, NT], I32)
        o = sb("o", [P, 2, NT, D])
        mm = [ctx.enter_context(nc.psum_tensor(f"{name}mm{b}", [P, CH], F32)) for b in range(6)]
        psT = [ctx.enter_context(nc.psum_tensor(f"{name}psT{k}", [P, CH], F32)) for k in range(KD)]
        up = [(mm[2 * p], mm[2 * p + 1]) for p in range(3)]
        psY = [mm[4 + n][:, :D] for n in range(2)]

        const_in, w_in, half_done, xT_hi_done, xT_done, up_ps, t_ready, g_done, hi_done = (sem(n) for n in (
            "const_in", "w_in", "half_done", "xT_hi_done", "xT_done", "up_ps", "t_ready", "g_done", "hi_done"))
        x_loaded = [sem(f"x_loaded{j}") for j in range(2)]
        xT_ps = sem("xT_ps")
        a_done = sem("a_done")
        h0_done = sem("h0_done")
        hid_ps = [sem("h1_ps"), sem("h2_ps")]
        gelu_done = [sem("gelu1_done"), sem("gelu2_done")]
        hid_hi = sem("hid_hi")
        split_done = [sem("split1_done"), sem("split2_done")]
        y_ps, y_used, z_done, st_done, mv_done, chain, o_ready = (sem(n) for n in (
            "y_ps", "y_used", "z_done", "st_done", "mv_done", "chain", "o_ready"))
        o_out = [sem(f"o_out{j}") for j in range(2)]
        N_CONST = 16 * 3

        weights = (w1_sb, w2_sb, h1_sb, h2_sb, w3_sb)
        pieces = [ffn_weights[:, q:q + FFN_PIECE] for q in range(0, ffn_weights.shape[1], FFN_PIECE)]
        to = [w.rearrange("p k n -> p (k n)")[:, q:q + FFN_PIECE] for w in (w[:] for w in weights)
              for q in range(0, w.shape[1] * w.shape[2], FFN_PIECE)]
        upto = [sum(w.shape[1] * w.shape[2] for w in weights[:n + 1]) // FFN_PIECE for n in range(len(weights))]
        if split:
            stage = sb("stage", [P, 2, FFN_PIECE])
            stage_in = [sem(f"stage_in{b}") for b in range(2)]
            rounded = sem("rounded")
        prime(nc, primed)
        block = ctx.enter_context(nc.Block())

        def guarded(eng):
            value = eng.value_load(flag[0:1, 0:1], min_val=0, max_val=1)
            return eng.If(1 - value if split else value)

        def chunk_dram(ap, c):
            return ap.rearrange("(c t p) d -> c p t d", t=NT, p=P)[c]

        def each_chunk(eng, chunk):
            chunk(0, 0, True, False)
            chunk(0, 1, False, False)
            with eng.Fori(1, PAIRS - 1) as i:
                for j in range(2):
                    chunk(i, j, False, False)
            chunk(PAIRS - 1, 0, False, False)
            chunk(PAIRS - 1, 1, False, True)

        @block.sync
        def _(sp):
            with guarded(sp):
                for j in range(2):
                    sp.dma_start(x[:, j], chunk_dram(x_in, j)).then_inc(x_loaded[j], 16)
                    if j == 0:
                        sp.dma_start(ident[:], ident_dram).then_inc(const_in, 16)
                sp.dma_start(scl[:], s_cols).then_inc(const_in, 16)
                sp.dma_start(s3[:], s3_row).then_inc(const_in, 16)
                if not split:
                    for n, dst in enumerate(to):
                        sp.dma_start(dst, pieces[n]).then_inc(w_in, 16)
                else:
                    for n in range(len(to)):
                        if n >= 2:
                            sp.wait_ge(rounded, PRIMED + n - 1)
                        sp.dma_start(stage[:, n % 2], pieces[n]).then_inc(stage_in[n % 2], 16)

                def store(i, j):
                    c = 2 * i + j
                    sp.wait_ge(o_ready, PRIMED + NT * (c + 1))
                    sp.dma_start(chunk_dram(out, c), o[:, j]).then_inc(o_out[j], 16)

                with sp.Fori(0, PAIRS - 1) as i:
                    for j in range(2):
                        sp.wait_ge(z_done, PRIMED + NT * (2 * i + j + 1))
                        sp.dma_start(x[:, j], chunk_dram(x_in, 2 * i + j + 2)).then_inc(x_loaded[j], 16)
                        store(i, j)
                for j in range(2):
                    store(PAIRS - 1, j)
                for j in range(2):
                    sp.wait_ge(o_out[j], PRIMED + 16 * PAIRS)

        @block.tensor
        def _(pe):
            def product(ps, w, rhs, k, K):
                for q in range(parts):
                    last = nc.tensor.matmul(ps, w, rhs[q][:, k, :], start=(k == 0 and q == 0),
                                            stop=(k == K - 1 and q == parts - 1))
                return last

            def transposes(i, j):
                pe.wait_ge(x_loaded[j], PRIMED + 16 * (i + 1))
                for k in range(KD):
                    for n in range(NT):
                        last = nc.tensor.transpose(psT[k][:, n * P:(n + 1) * P], x[:, j, n, k * P:(k + 1) * P], ident[:])
                    last.then_inc(xT_ps, 1)

            def weights_there(n):
                if split:
                    pe.wait_ge(rounded, PRIMED + upto[n])
                elif n == 0:
                    pe.wait_ge(w_in, PRIMED + 16 * len(to))

            def chunk(i, j, first, last_one):
                c = 2 * i + j
                if first:
                    pe.wait_ge(const_in, PRIMED + N_CONST)
                    transposes(i, j)
                    weights_there(1 if split else 0)
                pe.wait_ge(xT_done, PRIMED + KD * (c + 1))
                for m in range(KF):
                    if m < 2:
                        pe.wait_ge(gelu_done[1], PRIMED + KF * c)
                    elif m == 2:
                        pe.wait_ge(y_used, PRIMED + NT * c)
                    else:
                        pe.wait_ge(g_done, PRIMED + KF * c + m - 2)
                    cols = slice(m * P, (m + 1) * P)
                    for k in range(KD):
                        product(up[m % 3][0][:], w1_sb[:, k, cols], xT, k, KD)
                    for k in range(KD):
                        last = product(up[m % 3][1][:], w2_sb[:, k, cols], xT, k, KD)
                    last.then_inc(up_ps, 1)
                for layer, w in enumerate((h1_sb, h2_sb)):
                    src = (ha, hb)[layer]
                    if first:
                        weights_there(2 + layer)
                    for m in range(KF):
                        if layer == 0 and m < 4:
                            pe.wait_ge(g_done, PRIMED + KF * c + KF - 1 + m // 2)
                        elif layer == 1 and m < 4:
                            pe.wait_ge(gelu_done[0], PRIMED + KF * c + m + 5)
                        else:
                            pe.wait_ge(gelu_done[layer], PRIMED + KF * c + m - 3)
                        for k in range(KF):
                            if m == 0 and layer == 0:
                                pe.wait_ge(h0_done if split else g_done, PRIMED + KF * c + k + 1)
                            if m == 0 and layer == 1:
                                pe.wait_ge((split_done if split else gelu_done)[0], PRIMED + KF * c + k + 1)
                            last = product(mm[m % 4][:], w[:, k, m * P:(m + 1) * P], src, k, KF)
                        last.then_inc(hid_ps[layer], 1)
                        if layer == 1 and m == KF // 2 and not last_one:
                            transposes(i + j, 1 - j)
                if first:
                    weights_there(4)
                for n in range(NT):
                    if n < 2:
                        pe.wait_ge(y_used, PRIMED + NT * c)
                    else:
                        pe.wait_ge(y_used, PRIMED + NT * c + n - 1)
                    for k in range(KF):
                        if n == 0:
                            pe.wait_ge((split_done if split else gelu_done)[1], PRIMED + KF * c + k + 1)
                        for q in range(parts):
                            last = nc.tensor.matmul(psY[n % 2], ha[q][:, k, n * P:(n + 1) * P], w3_sb[:, k, :],
                                                    start=(k == 0 and q == 0), stop=(k == KF - 1 and q == parts - 1))
                    last.then_inc(y_ps, 1)

            with guarded(pe):
                each_chunk(pe, chunk)

        if split:
            @block.gpsimd
            def _(pool):
                def chunk(i, j, first, last):
                    c = 2 * i + j
                    for m in range(KF):
                        pool.wait_ge(hi_done, PRIMED + KF * c + m + 1)
                        nc.gpsimd.tensor_tensor(ha[1][:, m], g[:, m % 2], ha[0][:, m], ALU.subtract).then_inc(h0_done, 1)

                with guarded(pool):
                    each_chunk(pool, chunk)

        @block.scalar
        def _(act):
            def round_pieces(n0, n1):
                for n in range(n0, n1):
                    act.wait_ge(stage_in[n % 2], PRIMED + 16 * (n // 2 + 1))
                    nc.scalar.activation(to[n], stage[:, n % 2], ACT.Copy).then_inc(rounded, 1)

            def chunk(i, j, first, last):
                c = 2 * i + j

                def high(m):
                    act.wait_ge(g_done, PRIMED + KF * c + m + 1)
                    if m == 0:
                        act.wait_ge(y_ps, PRIMED + NT * c)
                    nc.scalar.activation(ha[0][:, m], g[:, m % 2], ACT.Copy).then_inc(hi_done, 1)

                if first and split:
                    round_pieces(0, upto[1])
                for m in range(KF):
                    act.wait_ge(up_ps, PRIMED + KF * c + m + 1)
                    if m >= 2:
                        act.wait_ge(a_done, PRIMED + KF * c + m - 1)
                    nc.scalar.activation(t[:, m % 2], up[m % 3][0][:], ACT.Tanh,
                                         scale=half[:, 0, m:m + 1]).then_inc(t_ready, 1)
                    if split and m:
                        high(m - 1)
                    if first and split:
                        round_pieces(upto[1] + m, upto[1] + m + 1)
                if split:
                    high(KF - 1)
                for layer in range(2):
                    dst = (hb, ha)[layer]
                    for m in range(KF):
                        act.wait_ge(hid_ps[layer], PRIMED + KF * c + m + 1)
                        if split:
                            if m >= 2:
                                act.wait_ge(split_done[layer], PRIMED + KF * c + m - 1)
                            elif layer == 1:
                                act.wait_ge(split_done[0], PRIMED + KF * c + KF - 1 + m)
                            else:
                                act.wait_ge(h0_done, PRIMED + KF * c + KF - 1 + m)
                            out_m = g[:, m % 2]
                        else:
                            out_m = dst[0][:, m, :]
                        nc.scalar.activation(out_m, mm[m % 4][:], ACT.Gelu,
                                             scale=scl[:, 2 + layer, m:m + 1]).then_inc(gelu_done[layer], 1)
                        if first and split and layer == 0:
                            round_pieces(upto[2] + m, upto[2] + m + 1)
                if first and split:
                    round_pieces(upto[3], upto[4])

            with guarded(act):
                act.wait_ge(half_done, PRIMED + 2)
                each_chunk(act, chunk)

        @block.vector
        def _(dve):
            links = [0]

            def normalise(c, j, i):
                links[0] = 0

                def link(ins):
                    links[0] += 1
                    ins.then_inc(chain, 1)
                    dve.wait_ge(chain, PRIMED + (1 + RSQRT_LINKS) * c + links[0])

                dve.wait_ge(mv_done, PRIMED + NT * c + NT)
                link(nc.vector.tensor_copy(var[:], mv[:, :, 1]))
                rsqrt(nc, link, rstd[:], var[:], tmp[:], shifted[:])
                dve.wait_ge(o_out[j], PRIMED + 16 * i)
                for n in range(NT):
                    nc.vector.tensor_scalar(o[:, j, n], z[:, n], mv[:, n, 0:1], rstd[:, n:n + 1], ALU.subtract,
                                            ALU.mult).then_inc(o_ready, 1)

            def transposed(c, k):
                dve.wait_ge(xT_ps, PRIMED + KD * c + k + 1)
                nc.vector.tensor_copy(xT[0][:, k], psT[k][:]).then_inc(xT_hi_done if split else xT_done, 1)
                if split:
                    dve.wait_ge(xT_hi_done, PRIMED + KD * c + k + 1)
                    nc.vector.tensor_tensor(xT[1][:, k], psT[k][:], xT[0][:, k], ALU.subtract).then_inc(xT_done, 1)

            def chunk(i, j, first, last):
                c = 2 * i + j
                if first:
                    for k in range(KD):
                        transposed(c, k)
                for m in range(KF):
                    p = m % 2
                    dve.wait_ge(t_ready, PRIMED + KF * c + m + 1)
                    nc.vector.scalar_tensor_tensor(a[:, p], t[:, p], 1.0, up[m % 3][0][:], ALU.add, ALU.mult).then_inc(a_done, 1)
                    dve.wait_ge(a_done, PRIMED + KF * c + m + 1)
                    if split:
                        if m >= 2:
                            dve.wait_ge(h0_done, PRIMED + KF * c + m - 1)
                        elif not first:
                            dve.wait_ge(split_done[1], PRIMED + KF * c - 1 + m)
                        nc.vector.scalar_tensor_tensor(g[:, p], up[m % 3][1][:], half[:, 1, m:m + 1], a[:, p],
                                                       ALU.mult, ALU.mult).then_inc(g_done, 1)
                        continue
                    if m == 0:
                        dve.wait_ge(y_ps, PRIMED + NT * c)
                    nc.vector.scalar_tensor_tensor(ha[0][:, m], up[m % 3][1][:], half[:, 1, m:m + 1], a[:, p],
                                                   ALU.mult, ALU.mult).then_inc(g_done, 1)
                for layer in range(2):
                    dst = (hb, ha)[layer]
                    for m in range(KF):
                        if split:
                            dve.wait_ge(gelu_done[layer], PRIMED + KF * c + m + 1)
                            if layer == 1 and m == 0:
                                dve.wait_ge(hid_ps[0], PRIMED + KF * (c + 1))
                            n_split = (2 * c + layer) * KF + m + 1
                            nc.vector.tensor_copy(dst[0][:, m], g[:, m % 2]).then_inc(hid_hi, 1)
                            dve.wait_ge(hid_hi, PRIMED + n_split)
                            nc.vector.tensor_tensor(dst[1][:, m], g[:, m % 2], dst[0][:, m],
                                                    ALU.subtract).then_inc(split_done[layer], 1)
                        if layer == 0 and m == 1 and not first:
                            normalise(c - 1, 1 - j, i + j - 1)
                        if layer == 1 and m >= KF - KD and not last:
                            transposed(c + 1, m - KF + KD)
                for n in range(NT):
                    p = n % 2
                    dve.wait_ge(y_ps, PRIMED + NT * c + n + 1)
                    if n == 0:
                        dve.wait_ge(o_ready, PRIMED + NT * c)
                    nc.vector.tensor_tensor(z[:, n], psY[p], s3[:], ALU.mult).then_inc(y_used, 1)
                    dve.wait_ge(y_used, PRIMED + NT * c + n + 1)
                    nc.vector.tensor_tensor(z[:, n], z[:, n], x[:, j, n, :], ALU.add).then_inc(z_done, 1)
                    dve.wait_ge(z_done, PRIMED + NT * c + n + 1)
                    nc.vector.bn_stats(st[:, n], z[:, n]).then_inc(st_done, 1)
                    dve.wait_ge(half_done, PRIMED + 2)
                    dve.wait_ge(st_done, PRIMED + NT * c + n + 1)
                    nc.vector.bn_aggr(mv[:, n], st[:, n]).then_inc(mv_done, 1)
                if last:
                    normalise(c, j, i)

            with guarded(dve):
                dve.wait_ge(const_in, PRIMED + N_CONST)
                nc.vector.tensor_scalar(half[:, 0], scl[:, 0], 0.5, None, ALU.mult).then_inc(half_done, 1)
                dve.wait_ge(half_done, PRIMED + 1)
                nc.vector.tensor_tensor(half[:, 1], half[:, 0], scl[:, 1], ALU.mult).then_inc(half_done, 1)
                dve.wait_ge(half_done, PRIMED + 2)
                each_chunk(dve, chunk)


def attend_and_route_phase(nc, x_in, xT_in, wqT, wkT, wvT, wo, w_router, b_router, consts, route, x1_out, slots,
                           batches, capacity):
    T, D = x_in.shape
    KD = D // P
    SEQ = T // batches
    NT = SEQ // P
    HALF = SEQ // 2
    E = w_router.shape[2]
    GROUP = 4
    groups = [[(n, min(n + GROUP, i + 1)) for n in range(0, i + 1, GROUP)] for i in range(NT)]
    first_group = [sum(len(g) for g in groups[:i]) for i in range(NT + 1)]
    NG = first_group[NT]
    ROWS_AT = {0: 0, 1: 1, 2: 2, 3: 3}
    LOGITS_AT, COUNTS_AT = 4, 5
    SCALE = float(D) ** -0.5
    with ExitStack() as ctx:
        def sb(n, s, d=F32):
            return ctx.enter_context(nc.sbuf_tensor("a" + n, s, d))

        def psum(n, s):
            return ctx.enter_context(nc.psum_tensor("a" + n, s, F32))

        primed = []
        ctx.callback(nc.clear_and_free_semaphores, primed)

        def sem(n):
            primed.append(nc.alloc_semaphore("a" + n))
            return primed[-1]

        ident, ident_bf, mask_bf, before_me, all_ones = (sb(n, [P, P], d) for n, d in (
            ("ident", F32), ("ident_bf", BF16), ("mask_bf", BF16), ("before_me", F32), ("all_ones", F32)))
        iota_e = sb("iota_e", [P, E])
        br = sb("br", [P, E])
        wr = sb("wr", [P, KD, E])
        raw = [sb(f"raw{n}", [P, KD, D]) for n in range(4)]
        score_hi, score_lo, value_hi, value_lo = (sb(n, [P, KD, D], F32R) for n in ("sc_hi", "sc_lo", "va_hi", "va_lo"))
        xs = sb("xs", [P, KD, SEQ])
        xT_hi, xT_lo, qT_hi, qT_lo = (sb(n, [P, KD, SEQ], F32R) for n in ("xT_hi", "xT_lo", "qT_hi", "qT_lo"))
        v_hi, v_lo = (sb(n, [P, NT, D], F32R) for n in ("v_hi", "v_lo"))
        xin = sb("xin", [P, NT, D])
        prob = sb("prob", [P, 2, SEQ])
        pT_hi, pT_lo = (sb(n, [P, 4, GROUP, P], F32R) for n in ("pT_hi", "pT_lo"))
        nmax, rowsum, recip, var, rstd, tmp = (sb(n, [P, NT]) for n in ("nmax", "rowsum", "recip", "var", "rstd", "tmp"))
        shifted = sb("shifted", [P, NT], I32)
        z = sb("z", [P, NT, D])
        st = sb("st", [P, NT, 6])
        mv = sb("mv", [P, NT, 2])
        xn = sb("xn", [P, NT, D])
        x1T = sb("x1T", [P, KD, SEQ])
        lg, top, both, pos, prod = (sb(n, [P, NT, E]) for n in ("lg", "top", "both", "pos", "prod"))
        top_i = sb("top_i", [P, NT, E], U32)
        top_f = sb("top_f", [P, NT, 2])
        oh = [sb(f"oh{c}", [P, NT, E]) for c in range(2)]
        cum = sb("cum", [P, NT + 1, E])
        gap = sb("gap", [P, NT])
        egap = sb("egap", [P, NT])
        slot_f = sb("slot_f", [P, NT])
        slot_i = [sb(f"slot_i{c}", [P, NT], I32) for c in range(2)]
        S = [psum(f"S{n}", [P, SEQ]) for n in range(2)]
        PT = psum("PT", [P, 2, GROUP, P])
        O = psum("O", [P, D])
        misc = psum("misc", [P, 512])
        PTf = PT[:].rearrange("p a b c -> p (a b c)")

        names = ("const_in xs_in xin_in ab_ps ab_hi ab_lo x_hi x_lo q_ps q_hi q_lo v_ps v_hi v_lo s_ps mx ex pt_ps pt_hi "
                 "pt_lo o_ps z_done chain ln_chain xn_done t_ps t_ev lg_ps both_done px_ps gap_done e_done slot_done sc_out scattered x1_st "
                 "st_done recip_done top_done mv_done").split()
        (const_in, xs_in, xin_in, ab_ps, ab_hi, ab_lo, x_hi, x_lo, q_ps, q_hi, q_lo, v_ps, v_hi_done, v_lo_done, s_ps, mx,
         ex, pt_ps, pt_hi, pt_lo, o_ps, z_done, chain, ln_chain, xn_done, t_ps, t_ev, lg_ps, both_done, px_ps, gap_done, e_done,
         slot_done, sc_out, scattered, x1_st, st_done, recip_done, top_done, mv_done) = (sem(n) for n in names)
        unwatched = {n.engine: sem(f"unwatched{q}") for q, n in
                     enumerate((nc.sync, nc.gpsimd, nc.tensor, nc.scalar, nc.vector))}
        loads = [(ident[:], consts["ident"]), (z[:, 0, :P], consts["mask"]),
                 (before_me[:], consts["before_me"]), (all_ones[:], consts["all_ones"]), (iota_e[:], consts["iota_e"]),
                 (br[:], b_router), (wr[:], w_router)]
        raws = list(zip(raw, (wqT, wkT, wvT, wo)))
        N_CONST = 16 * (len(loads) + len(raws))

        by_gpsimd = [sc_out]
        prime(nc, [s for s in primed if s not in by_gpsimd])
        block = ctx.enter_context(nc.Block())

        def wait_alone(eng, semaphore, value):
            eng.wait_ge(semaphore, value)
            eng.sem_inc(unwatched[eng.engine], 1)

        def tokens(ap, b):
            return ap.rearrange("(b t p) d -> b p t d", t=NT, p=P)[b]

        TRANSPOSES = NT // 2

        def each_sequence(eng, attention, tail):
            attention(0, False, True)
            with eng.Fori(1, batches - 1) as b:
                attention(b, True, True)
            attention(batches - 1, True, False)
            tail(batches - 1)

        @block.sync
        def _(sp):
            for d, s in raws:
                sp.dma_start(d[:], s).then_inc(const_in, 16)
            for d, s in loads:
                sp.dma_start(d, s).then_inc(const_in, 16)
            sp.wait_ge(const_in, PRIMED + N_CONST)

            def attention(b, earlier, later):
                sp.wait_ge(x_lo, PRIMED + b)
                sp.dma_start(xs[:], xT_in[b]).then_inc(xs_in, 16)
                sp.wait_ge(z_done, PRIMED + NT * b)
                sp.dma_start(xin[:], tokens(x_in, b)).then_inc(xin_in, 16)
                if earlier:
                    tail(b - 1)

            def tail(b):
                sp.wait_ge(xn_done, PRIMED + b + 1)
                sp.dma_start(tokens(x1_out, b), xn[:]).then_inc(x1_st, 16)

            each_sequence(sp, attention, tail)
            sp.wait_ge(x1_st, PRIMED + 16 * batches)

        @block.gpsimd
        def _(pool):
            def tail(b):
                wait_alone(pool, slot_done, PRIMED + 2 * b + 2)
                for c in range(2):
                    for t in range(NT):
                        pool.indirect_dma_start(
                            out=slots, out_offset=bass.IndirectOffsetOnAxis(ap=slot_i[c][:, t:t + 1], axis=0),
                            in_=xn[:, t, :], in_offset=None).then_inc(sc_out, 16)
                pool.wait_ge(sc_out, 16 * 2 * NT * (b + 1))
                pool.sem_inc(scattered, 1)

            each_sequence(pool, lambda b, earlier, later: tail(b - 1) if earlier else None, tail)

        @block.tensor
        def _(pe):
            def three(ps, left, right, first, last):
                (lh, ll), (rh, rl) = left, right
                nc.tensor.matmul(ps, lh, rh, start=first, stop=False)
                nc.tensor.matmul(ps, lh, rl, start=False, stop=False)
                return nc.tensor.matmul(ps, ll, rh, start=False, stop=last)

            pe.wait_ge(const_in, PRIMED + N_CONST)
            for pair in range(2):
                if pair:
                    pe.wait_ge(ab_lo, PRIMED + 1)
                for m in range(KD):
                    for k in range(KD):
                        last = nc.tensor.matmul(misc[:, m * D:(m + 1) * D], raw[2 * pair][:, k, m * P:(m + 1) * P],
                                                raw[2 * pair + 1][:, k, :], start=(k == 0), stop=(k == KD - 1))
                last.then_inc(ab_ps, 1)
            pe.wait_ge(ab_lo, PRIMED + 2)

            def scores(b, i):
                s = S[i % 2]
                if i == 0:
                    pe.wait_ge(v_lo_done, PRIMED + 2 * b + 2)
                    pe.wait_ge(q_lo, PRIMED + 2 * b + 2)
                elif i >= 2:
                    pe.wait_ge(ex, PRIMED + NT * b + i - 1)
                width = (i + 1) * P
                for c0 in range(0, width, HALF):
                    c1 = min(width, c0 + HALF)
                    for k in range(KD):
                        three(s[:, c0:c1], (qT_hi[:, k, i * P:(i + 1) * P], qT_lo[:, k, i * P:(i + 1) * P]),
                              (xT_hi[:, k, c0:c1], xT_lo[:, k, c0:c1]), k == 0, k == KD - 1)
                    if c1 == width:
                        last = nc.tensor.matmul(s[:, i * P:width], ident_bf[:], mask_bf[:], start=False, stop=True,
                                                skip_group_check=True)
                last.then_inc(s_ps, 1)

            def transpose_probs(b, i):
                pe.wait_ge(ex, PRIMED + NT * b + i + 1)
                for g, (n0, n1) in enumerate(groups[i]):
                    g += first_group[i]
                    if g >= 2:
                        pe.wait_ge(pt_lo, PRIMED + NG * b + g - 1)
                    for n in range(n0, n1):
                        last = nc.tensor.transpose(PT[:, g % 2, n - n0, :], prob[:, i % 2, n * P:(n + 1) * P], ident[:])
                    last.then_inc(pt_ps, 1)

            def weigh(b, i):
                pe.wait_ge(z_done, PRIMED + NT * b + i)
                for g, (n0, n1) in enumerate(groups[i]):
                    g += first_group[i]
                    pe.wait_ge(pt_lo, PRIMED + NG * b + g + 1)
                    for n in range(n0, n1):
                        last = three(O[:], (pT_hi[:, g % 4, n - n0, :], pT_lo[:, g % 4, n - n0, :]),
                                     (v_hi[:, n, :], v_lo[:, n, :]), n == 0, n == i)
                last.then_inc(o_ps, 1)

            def transpose_rows(b, j):
                if j == 0:
                    pe.wait_ge(xn_done, PRIMED + b + 1)
                    pe.wait_ge(slot_done, PRIMED + 2 * b)
                else:
                    pe.wait_ge(t_ev, PRIMED + TRANSPOSES * b + j)
                for k in range(KD):
                    for n in range(2):
                        last = nc.tensor.transpose(misc[:, (2 * k + n) * P:(2 * k + n + 1) * P],
                                                   xn[:, 2 * j + n, k * P:(k + 1) * P], ident[:])
                last.then_inc(t_ps, 1)

            def logits(b):
                pe.wait_ge(t_ev, PRIMED + TRANSPOSES * (b + 1))
                for t in range(NT):
                    for k in range(KD):
                        last = nc.tensor.matmul(misc[:, t * E:(t + 1) * E], x1T[:, k, t * P:(t + 1) * P], wr[:, k, :],
                                                start=(k == 0), stop=(k == KD - 1))
                last.then_inc(lg_ps, 1)

            def counts(b):
                pe.wait_ge(both_done, PRIMED + b + 1)
                flat = both[:].rearrange("p t e -> p (t e)")
                nc.tensor.matmul(misc[:, NT * E:2 * NT * E], before_me[:], flat, start=True, stop=True)
                nc.tensor.matmul(misc[:, 2 * NT * E:3 * NT * E], all_ones[:], flat, start=True, stop=True).then_inc(px_ps, 1)

            def attention(b, earlier, later):
                pe.wait_ge(x_lo, PRIMED + b + 1)
                pe.wait_ge(ex, PRIMED + NT * b)
                for m in range(KD):
                    for c in range(2):
                        cs = slice(c * HALF, (c + 1) * HALF)
                        for k in range(KD):
                            last = three(S[m][:, cs], (score_hi[:, k, m * P:(m + 1) * P], score_lo[:, k, m * P:(m + 1) * P]),
                                         (xT_hi[:, k, cs], xT_lo[:, k, cs]), k == 0, k == KD - 1)
                    last.then_inc(q_ps, 1)
                for half in range(2):
                    dst = (PTf, S[0][:])[half]
                    if half == 0:
                        pe.wait_ge(pt_lo, PRIMED + NG * b)
                    else:
                        pe.wait_ge(q_lo, PRIMED + 2 * b + 1)
                    for n in range(NT // 2):
                        t = half * NT // 2 + n
                        for k in range(KD):
                            last = three(dst[:, n * D:(n + 1) * D],
                                         (xT_hi[:, k, t * P:(t + 1) * P], xT_lo[:, k, t * P:(t + 1) * P]),
                                         (value_hi[:, k, :], value_lo[:, k, :]), k == 0, k == KD - 1)
                    last.then_inc(v_ps, 1)
                scores(b, 0)
                for i in range(NT):
                    if i + 1 < NT:
                        scores(b, i + 1)
                    if earlier and i in ROWS_AT:
                        transpose_rows(b - 1, ROWS_AT[i])
                    if earlier and i == COUNTS_AT:
                        counts(b - 1)
                    transpose_probs(b, i)
                    if i:
                        weigh(b, i - 1)
                    if earlier and i == LOGITS_AT:
                        logits(b - 1)
                weigh(b, NT - 1)

            def tail(b):
                for j in range(TRANSPOSES):
                    transpose_rows(b, j)
                logits(b)
                counts(b)

            each_sequence(pe, attention, tail)

        @block.scalar
        def _(act):
            for pair, hi in enumerate((score_hi, value_hi)):
                act.wait_ge(ab_ps, PRIMED + pair + 1)
                nc.scalar.activation(hi[:].rearrange("p k d -> p (k d)"), misc[:], ACT.Copy,
                                     scale=SCALE if pair == 0 else 1.0).then_inc(ab_hi, 1)

            def rows_out(b, j):
                act.wait_ge(t_ps, PRIMED + TRANSPOSES * b + j + 1)
                nc.scalar.activation(x1T[:, :, 2 * j * P:(2 * j + 2) * P], misc[:].rearrange("p (k t) -> p k t", k=KD),
                                     ACT.Copy).then_inc(t_ev, 1)

            def weights(b):
                act.wait_ge(gap_done, PRIMED + b + 1)
                nc.scalar.activation(egap[:], gap[:], ACT.Exp).then_inc(e_done, 1)

            def x_high(b):
                act.wait_ge(xs_in, PRIMED + 16 * b + 16)
                act.wait_ge(s_ps, PRIMED + NT * b)
                nc.scalar.activation(xT_hi[:], xs[:], ACT.Copy).then_inc(x_hi, 1)

            def attention(b, earlier, later):
                for m in range(KD):
                    act.wait_ge(q_ps, PRIMED + 2 * b + m + 1)
                    nc.scalar.activation(qT_hi[:, m, :], S[m][:], ACT.Copy).then_inc(q_hi, 1)
                for half in range(2):
                    src = (PTf, S[0][:])[half]
                    act.wait_ge(v_ps, PRIMED + 2 * b + half + 1)
                    nc.scalar.activation(v_hi[:, half * NT // 2:(half + 1) * NT // 2, :].rearrange("p t d -> p (t d)"), src,
                                         ACT.Copy).then_inc(v_hi_done, 1)

                def exp(i):
                    act.wait_ge(mx, PRIMED + NT * b + i + 1)
                    if i >= 2:
                        act.wait_ge(pt_ps, PRIMED + NG * b + first_group[i - 1])
                    width = (i + 1) * P
                    nc.scalar.activation(prob[:, i % 2, :width], S[i % 2][:, :width], ACT.Exp, bias=nmax[:, i:i + 1],
                                         accum_out=rowsum[:, i:i + 1]).then_inc(ex, 1)

                exp(0)
                for i in range(NT):
                    if i + 1 < NT:
                        exp(i + 1)
                    if earlier and i in ROWS_AT:
                        rows_out(b - 1, ROWS_AT[i])
                    for g, (n0, n1) in enumerate(groups[i]):
                        g += first_group[i]
                        act.wait_ge(pt_ps, PRIMED + NG * b + g + 1)
                        if i >= 2:
                            act.wait_ge(o_ps, PRIMED + NT * b + i - 1)
                        nc.scalar.activation(pT_hi[:, g % 4, :n1 - n0, :], PT[:, g % 2, :n1 - n0, :],
                                             ACT.Copy).then_inc(pt_hi, 1)
                    if earlier and i == COUNTS_AT:
                        weights(b - 1)
                if later:
                    x_high(b + 1)

            def tail(b):
                for j in range(TRANSPOSES):
                    rows_out(b, j)
                weights(b)

            x_high(0)
            each_sequence(act, attention, tail)

        @block.vector
        def _(dve):
            LINKS = 1 + 1 + 1 + 1 + 2 + 1 + NT + 1 + 2 * 4 + 1
            dve.wait_ge(const_in, PRIMED + N_CONST)
            nc.vector.tensor_copy(ident_bf[:], ident[:])
            nc.vector.tensor_copy(mask_bf[:], z[:, 0, :P])
            for pair, (hi, lo) in enumerate(((score_hi, score_lo), (value_hi, value_lo))):
                dve.wait_ge(ab_hi, PRIMED + pair + 1)
                nc.vector.scalar_tensor_tensor(lo[:].rearrange("p k d -> p (k d)"), misc[:], SCALE if pair == 0 else 1.0,
                                               hi[:].rearrange("p k d -> p (k d)"), ALU.mult, ALU.subtract).then_inc(ab_lo, 1)
            nc.vector.memset(cum[:, NT, :], 0.0).then_inc(chain, 1)

            def make_tail(b):
                n_link = [0]

                def link(ins, alone=False):
                    n_link[0] += 1
                    ins.then_inc(chain, 1)
                    (wait_alone if alone else lambda e, s, v: e.wait_ge(s, v))(dve, chain, PRIMED + LINKS * b + n_link[0] + 1)

                def choose():
                    wait_alone(dve, lg_ps, PRIMED + b + 1)
                    link(nc.vector.tensor_tensor(lg[:], misc[:, :NT * E].rearrange("p (t e) -> p t e", e=E),
                                                 br[:].unsqueeze(1).to_broadcast([P, NT, E]), ALU.add), alone=True)
                    for t in range(NT):
                        ins = nc.vector.max(top[:, t], lg[:, t])
                    link(ins, alone=True)
                    for t in range(NT):
                        ins = nc.vector.max_index(top_i[:, t], top[:, t], lg[:, t])
                    link(ins)
                    nc.vector.tensor_tensor(gap[:], top[:, :, 1], top[:, :, 0], ALU.subtract).then_inc(gap_done, 1)
                    link(nc.vector.tensor_copy(top_f[:], top_i[:, :, 0:2]))
                    for c in range(2):
                        ins = nc.vector.tensor_tensor(oh[c][:], iota_e[:].unsqueeze(1).to_broadcast([P, NT, E]),
                                                      top_f[:, :, c:c + 1].to_broadcast([P, NT, E]), ALU.is_equal)
                    ins.then_inc(top_done, 1)
                    dve.wait_ge(top_done, PRIMED + b + 1)
                    nc.vector.tensor_tensor(both[:], oh[0][:], oh[1][:], ALU.add).then_inc(both_done, 1)

                def place():
                    dve.wait_ge(e_done, PRIMED + b + 1)
                    link(nc.vector.tensor_scalar(gap[:], egap[:], 1.0, None, ALU.add))
                    w0 = route["weight"][0][:, bass.ds(b * NT, NT)]
                    w1 = route["weight"][1][:, bass.ds(b * NT, NT)]
                    link(nc.vector.reciprocal(w0, gap[:]))
                    nc.vector.tensor_tensor(w1, egap[:], w0, ALU.mult)
                    dve.wait_ge(px_ps, PRIMED + b + 1)
                    link(nc.vector.tensor_copy(cum[:, 0, :], cum[:, NT, :]))
                    for t in range(NT):
                        link(nc.vector.tensor_tensor(cum[:, t + 1, :], misc[:, (2 * NT + t) * E:(2 * NT + t + 1) * E],
                                                     cum[:, t, :], ALU.add))
                    link(nc.vector.tensor_tensor(pos[:], misc[:, NT * E:2 * NT * E].rearrange("p (t e) -> p t e", e=E),
                                                 cum[:, :NT, :], ALU.add))
                    for c in range(2):
                        rank = route["rank"][c][:, bass.ds(b * NT, NT)]
                        keep = route["onehot"][c][:, bass.ds(b * NT, NT), :]
                        nc.vector.tensor_copy(keep, oh[c][:]).then_inc(chain, 1)
                        n_link[0] += 1
                        link(nc.vector.tensor_tensor(prod[:], oh[c][:], pos[:], ALU.mult))
                        link(nc.vector.tensor_reduce(rank, prod[:], X, ALU.add))
                        link(nc.vector.scalar_tensor_tensor(slot_f[:], top_f[:, :, c], float(capacity), rank, ALU.mult,
                                                            ALU.add))
                        nc.vector.tensor_copy(slot_i[c][:], slot_f[:]).then_inc(slot_done, 1)
                    dve.wait_ge(slot_done, PRIMED + 2 * b + 2)
                    link(nc.vector.tensor_copy(route["count"][:], cum[:, NT, :]))
                    assert n_link[0] == LINKS, (n_link[0], LINKS)

                return choose, place

            def x_low(b):
                dve.wait_ge(x_hi, PRIMED + b + 1)
                nc.vector.tensor_tensor(xT_lo[:], xs[:], xT_hi[:], ALU.subtract).then_inc(x_lo, 1)

            def normalised():
                for i in range(NT):
                    ins = nc.vector.tensor_scalar(xn[:, i], z[:, i], mv[:, i, 0:1], rstd[:, i:i + 1], ALU.subtract, ALU.mult)
                ins.then_inc(xn_done, 1)

            def attention(b, earlier, later):
                if earlier:
                    choose, place = make_tail(b - 1)
                for m in range(KD):
                    dve.wait_ge(q_hi, PRIMED + 2 * b + m + 1)
                    nc.vector.tensor_tensor(qT_lo[:, m, :], S[m][:], qT_hi[:, m, :], ALU.subtract).then_inc(q_lo, 1)
                for half in range(2):
                    src = (PTf, S[0][:])[half]
                    rows = slice(half * NT // 2, (half + 1) * NT // 2)
                    dve.wait_ge(v_hi_done, PRIMED + 2 * b + half + 1)
                    nc.vector.tensor_tensor(v_lo[:, rows, :].rearrange("p t d -> p (t d)"), src,
                                            v_hi[:, rows, :].rearrange("p t d -> p (t d)"), ALU.subtract).then_inc(v_lo_done, 1)

                if earlier:
                    dve.wait_ge(x1_st, PRIMED + 16 * (b - 1))
                    dve.wait_ge(scattered, PRIMED + b - 1)
                    normalised()

                def row_max(i):
                    dve.wait_ge(s_ps, PRIMED + NT * b + i + 1)
                    nc.vector.tensor_reduce(nmax[:, i:i + 1], S[i % 2][:, :(i + 1) * P], X, ALU.max, negate=True).then_inc(mx, 1)

                def residual(i):
                    dve.wait_ge(ex, PRIMED + NT * b + i + 1)
                    nc.vector.reciprocal(recip[:, i:i + 1], rowsum[:, i:i + 1]).then_inc(recip_done, 1)
                    dve.wait_ge(o_ps, PRIMED + NT * b + i + 1)
                    dve.wait_ge(xin_in, PRIMED + 16 * b + 16)
                    if i == 0 and earlier:
                        dve.wait_ge(xn_done, PRIMED + b)
                    dve.wait_ge(recip_done, PRIMED + NT * b + i + 1)
                    nc.vector.scalar_tensor_tensor(z[:, i], O[:], recip[:, i:i + 1], xin[:, i], ALU.mult,
                                                   ALU.add).then_inc(z_done, 1)
                    dve.wait_ge(z_done, PRIMED + NT * b + i + 1)
                    nc.vector.bn_stats(st[:, i], z[:, i]).then_inc(st_done, 1)

                row_max(0)
                for i in range(NT):
                    if i + 1 < NT:
                        row_max(i + 1)
                    for g, (n0, n1) in enumerate(groups[i]):
                        g += first_group[i]
                        dve.wait_ge(pt_hi, PRIMED + NG * b + g + 1)
                        nc.vector.tensor_tensor(pT_lo[:, g % 4, :n1 - n0, :], PT[:, g % 2, :n1 - n0, :],
                                                pT_hi[:, g % 4, :n1 - n0, :], ALU.subtract).then_inc(pt_lo, 1)
                    if i:
                        residual(i - 1)
                    if earlier and i == LOGITS_AT:
                        choose()
                    if earlier and i == COUNTS_AT:
                        place()
                if later:
                    x_low(b + 1)
                residual(NT - 1)
                wait_alone(dve, st_done, PRIMED + NT * b + NT)
                for i in range(NT):
                    ins = nc.vector.bn_aggr(mv[:, i], st[:, i])

                def link(ins):
                    n_link[0] += 1
                    ins.then_inc(mv_done, 1)
                    dve.wait_ge(mv_done, PRIMED + (2 + RSQRT_LINKS) * b + n_link[0])

                n_link = [0]
                link(ins)
                link(nc.vector.tensor_copy(var[:], mv[:, :, 1]))
                rsqrt(nc, link, rstd[:], var[:], tmp[:], shifted[:])

            def tail(b):
                dve.wait_ge(x1_st, PRIMED + 16 * b)
                dve.wait_ge(scattered, PRIMED + b)
                normalised()
                choose, place = make_tail(b)
                choose()
                place()

            x_low(0)
            each_sequence(dve, attention, tail)


def plan_phase(nc, route, units, starts_dram, slots, results, capacity, unit):
    E = route["count"].shape[1]
    D = slots.shape[1]
    TILES = route["rank"][0].shape[1]
    STARTS = starts_dram.shape[1]
    with ExitStack() as ctx:
        def sb(n, s, d=F32):
            return ctx.enter_context(nc.sbuf_tensor("p" + n, s, d))

        def sem(n):
            return ctx.enter_context(nc.semaphore("p" + n))

        starts = sb("starts", [P, STARTS])
        begun = sb("begun", [P, E, STARTS])
        taken = sb("taken", [P, E])
        before = sb("before", [P, E + 2])
        first_row = sb("first_row", [P, E])
        count_i = sb("count_i", [1, E], I32)
        zeros = sb("zeros", [P, unit // P, D])
        by_expert = sb("by_expert", [P, TILES, E])
        row_f = sb("row_f", [P, TILES])
        starts_in, zeros_done, counted, zeros_out, unreached_out, step = (sem(n) for n in ("starts_in", "zeros_done", "counted",
                                                                            "zeros_out",
                                                                                           "unreached_out", "step"))
        prime(nc, [])
        block = ctx.enter_context(nc.Block())

        @block.sync
        def _(sp):
            sp.dma_start(starts[:], starts_dram).then_inc(starts_in, 16)
            sp.wait_ge(counted, 1)
            sp.wait_ge(zeros_done, 1)
            for e in range(E):
                n = sp.value_load(count_i[0:1, e:e + 1], min_val=0, max_val=TILES * P)
                sp.dma_start(slots[bass.ds(e * capacity + n, unit), :].rearrange("(n p) d -> p n d", p=P), zeros[:]
                             ).then_inc(zeros_out, 16)
            sp.wait_ge(zeros_out, 16 * E)

        sure_units = 2 * TILES * P // unit
        most_units = results.shape[0] // unit - 1

        @block.scalar
        def _(act):
            act.wait_ge(zeros_done, 1)
            for n in range(sure_units + 1, most_units + 1):
                act.dma_start(results[n * unit:(n + 1) * unit, :].rearrange("(n p) d -> p n d", p=P), zeros[:]
                              ).then_inc(unreached_out, 16)
            act.wait_ge(unreached_out, 16 * (most_units - sure_units))

        @block.gpsimd
        def _(pool):
            nc.gpsimd.memset(zeros[:], 0.0).then_inc(zeros_done, 1)

        @block.vector
        def _(dve):
            steps = [0]

            def then(ins):
                steps[0] += 1
                ins.then_inc(step, 1)
                dve.wait_ge(step, steps[0])

            nc.vector.tensor_copy(count_i[:], route["count"][0:1, :]).then_inc(counted, 1)
            dve.wait_ge(starts_in, 16)
            then(nc.vector.tensor_tensor(begun[:], route["count"][:].unsqueeze(2).to_broadcast([P, E, STARTS]),
                                         starts[:].unsqueeze(1).to_broadcast([P, E, STARTS]), ALU.is_gt))
            then(nc.vector.tensor_reduce(taken[:], begun[:], X, ALU.add))
            then(nc.vector.memset(before[:], 0.0))
            for e in range(E):
                then(nc.vector.tensor_tensor(before[:, e + 2:e + 3], before[:, e + 1:e + 2], taken[:, e:e + 1], ALU.add))
            then(nc.vector.tensor_copy(units[:], before[0:1, :]))
            then(nc.vector.tensor_scalar(first_row[:], before[:, 1:E + 1], float(unit), float(unit), ALU.mult, ALU.add))
            for c in range(2):
                then(nc.vector.tensor_tensor(by_expert[:], route["onehot"][c][:],
                                             first_row[:].unsqueeze(1).to_broadcast([P, TILES, E]), ALU.mult))
                then(nc.vector.tensor_reduce(row_f[:], by_expert[:], X, ALU.add))
                then(nc.vector.tensor_tensor(row_f[:], row_f[:], route["rank"][c][:], ALU.add))
                then(nc.vector.tensor_copy(route["row"][c][:], row_f[:]))


def moe_phase(nc, units, slots, w_pack, b_pack, results, ident_dram, capacity, most_tokens):
    D = slots.shape[1]
    KD = D // P
    E, _, WN = w_pack.shape
    F = WN // (2 * KD)
    KF = F // P
    U = 256
    NH = U // P
    MAX_UNITS = most_tokens // U
    GROUP = 4
    MOST = results.shape[0] // U - 1
    with ExitStack() as ctx:
        def sb(n, s, d=F32):
            return ctx.enter_context(nc.sbuf_tensor("e" + n, s, d))

        def psum(n, s):
            return ctx.enter_context(nc.psum_tensor("e" + n, s, F32))

        primed = []
        ctx.callback(nc.clear_and_free_semaphores, primed)

        def sem(n):
            primed.append(nc.alloc_semaphore("e" + n))
            return primed[-1]

        ident = sb("ident", [P, P])
        stage = sb("stage", [P, WN])
        w_hi = [sb(f"w_hi{b}", [P, WN], F32R) for b in range(2)]
        w_lo = [sb(f"w_lo{b}", [P, WN], F32R) for b in range(2)]
        bias = sb("bias", [P, 2, KF + D])
        x = sb("x", [P, NH, D])
        xT_hi = sb("xT_hi", [P, KD, U], F32R)
        xT_lo = sb("xT_lo", [P, KD, U], F32R)
        h = sb("h", [P, 4, U])
        h_hi = sb("h_hi", [P, KF, U], F32R)
        h_lo = sb("h_lo", [P, KF, U], F32R)
        y = sb("y", [P, NH, D])
        psH = [psum(f"psH{b}", [P, U]) for b in range(4)]
        psT = psum("psT", [P, KD, U])
        psY = [psum(f"psY{n}", [P, D]) for n in range(NH)]

        ident_in = sem("ident_in")
        staged = sem("staged")
        bias_in = [sem(f"bias_in{b}") for b in range(2)]
        hi_done = sem("hi_done")
        lo_done = sem("lo_done")
        x_in = sem("x_in")
        xT_ps = sem("xT_ps")
        xT_hi_done = sem("xT_hi_done")
        xT_done = sem("xT_done")
        h_ps = sem("h_ps")
        h_act = sem("h_act")
        h_hi_done = sem("h_hi_done")
        h_done = sem("h_done")
        y_ps = sem("y_ps")
        y_done = sem("y_done")
        y_out = sem("y_out")

        unwatched = {n.engine: sem(f"unwatched{q}") for q, n in
                     enumerate((nc.sync, nc.gpsimd, nc.tensor, nc.scalar, nc.vector))}

        by_gpsimd = [staged, *bias_in]
        prime(nc, [s for s in primed if s not in by_gpsimd])
        block = ctx.enter_context(nc.Block())

        def w1(buf, k, m):
            return buf[:, k * F + m * P:k * F + (m + 1) * P]

        def w2(buf, k):
            return buf[:, KD * F + k * D:KD * F + (k + 1) * D]

        def wait_alone(eng, semaphore, value):
            eng.wait_ge(semaphore, value)
            eng.sem_inc(unwatched[eng.engine], 1)

        def for_units(eng, per_expert, per_unit):
            with eng.Fori(0, E // 2) as pair:
                for b in range(2):
                    e = 2 * pair + b
                    before = eng.value_load(units[0:1, bass.ds(e + 1, 1)], min_val=0, max_val=MOST)
                    upto = eng.value_load(units[0:1, bass.ds(e + 2, 1)], min_val=0, max_val=MOST)
                    per_expert(e, b, before, upto)
                    with eng.Fori(before, before + MAX_UNITS, GROUP) as g0:
                        with eng.If(g0 < upto):
                            with eng.Fori(g0, g0 + GROUP) as g:
                                with eng.If(g < upto):
                                    per_unit(e, b, g - before, g)

        @block.sync
        def _(sp):
            sp.dma_start(ident[:], ident_dram).then_inc(ident_in, 16)
            def per_unit(e, b, t, g):
                sp.wait_ge(xT_ps, PRIMED + g)
                row = nc.s_assert_within(e * capacity + t * U, 0, E * capacity - U, skip_runtime_bounds_check_because="g stays within the units counted")
                sp.dma_start(x[:], slots[bass.ds(row, U), :].rearrange("(n p) d -> p n d", p=P)).then_inc(x_in, 16)

            for_units(sp, lambda *_: None, per_unit)
            total = sp.value_load(units[0:1, E + 1:E + 2], min_val=0, max_val=MOST)
            sp.wait_ge(xT_ps, PRIMED + total)
            sp.dma_start(x[:], slots[0:U, :].rearrange("(n p) d -> p n d", p=P)).then_inc(x_in, 16)
            wait_alone(sp, x_in, PRIMED + 16 * total + 16)

        @block.gpsimd
        def _(pool):
            pool.dma_start(stage[:], w_pack[0]).then_inc(staged, 16)
            with pool.Fori(0, E // 2) as pair:
                for b in range(2):
                    e = 2 * pair + b
                    held = pool.value_load(units[0:1, bass.ds(e, 1)], min_val=0, max_val=MOST)
                    wait_alone(pool, y_ps, PRIMED + held)
                    pool.wait_ge(y_done, PRIMED + NH * held + 1)
                    pool.dma_start(bias[:, b], b_pack[e]).then_inc(bias_in[b], 16)
                    wait_alone(pool, staged, 16 * (e + 1))
                    nc.gpsimd.tensor_copy(w_hi[b][:], stage[:]).then_inc(hi_done, 1)
                    pool.wait_ge(hi_done, PRIMED + e + 1)
                    nc.gpsimd.tensor_tensor(w_lo[b][:], stage[:], w_hi[b][:], ALU.subtract).then_inc(lo_done, 1)
                    pool.wait_ge(lo_done, PRIMED + e + 1)
                    pool.dma_start(stage[:], w_pack[(e + 1) % E]).then_inc(staged, 16)
            pool.wait_ge(staged, 16 * (E + 1))

        @block.tensor
        def _(pe):
            def transposes():
                for k in range(KD):
                    for n in range(NH):
                        last = nc.tensor.transpose(psT[:, k, n * P:(n + 1) * P], x[:, n, k * P:(k + 1) * P], ident[:])
                last.then_inc(xT_ps, 1)

            def per_expert(e, b, before, upto):
                wait_alone(pe, lo_done, PRIMED + e + 1)

            def per_unit(e, b, t, g):
                pe.wait_ge(xT_done, PRIMED + g + 1)
                for m in range(KF):
                    if m < 4:
                        pe.wait_ge(h_done, PRIMED + KF * g)
                    else:
                        pe.wait_ge(h_act, PRIMED + KF * g + m - 3)
                    for k in range(KD):
                        for n, (w, v) in enumerate(((w_hi, xT_hi), (w_hi, xT_lo), (w_lo, xT_hi))):
                            last = nc.tensor.matmul(psH[m % 4][:], w1(w[b], k, m), v[:, k, :], start=(k == 0 and n == 0),
                                                    stop=(k == KD - 1 and n == 2))
                    last.then_inc(h_ps, 1)
                pe.wait_ge(x_in, PRIMED + 16 * g + 32)
                transposes()
                pe.wait_ge(y_done, PRIMED + NH * g + 1)
                for n in range(NH):
                    for k in range(KF):
                        if n == 0:
                            pe.wait_ge(h_done, PRIMED + KF * g + k + 1)
                        for q, (v, w) in enumerate(((h_hi, w_hi), (h_lo, w_hi), (h_hi, w_lo))):
                            last = nc.tensor.matmul(psY[n][:], v[:, k, n * P:(n + 1) * P], w2(w[b], k),
                                                    start=(k == 0 and q == 0), stop=(k == KF - 1 and q == 2))
                last.then_inc(y_ps, 1)

            pe.wait_ge(ident_in, PRIMED + 16)
            pe.wait_ge(x_in, PRIMED + 16)
            transposes()
            for_units(pe, per_expert, per_unit)

        @block.scalar
        def _(act):
            def store(g):
                act.wait_ge(y_done, PRIMED + NH * g + 1)
                act.dma_start(results[bass.ds(nc.s_assert_within(g * U, 0, MOST * U, skip_runtime_bounds_check_because="g stays within the units counted"), U), :].rearrange("(n p) d -> p n d", p=P), y[:]).then_inc(y_out, 16)

            def per_expert(e, b, before, upto):
                wait_alone(act, bias_in[b], 8 * (e - b) + 16)

            def per_unit(e, b, t, g):
                for m in range(KF):
                    act.wait_ge(h_ps, PRIMED + KF * g + m + 1)
                    if m >= 4:
                        act.wait_ge(h_done, PRIMED + KF * g + m - 3)
                    nc.scalar.activation(h[:, m % 4], psH[m % 4][:], ACT.Relu, bias=bias[:, b, m:m + 1]).then_inc(h_act, 1)
                    if m == 3:
                        store(g)

            for_units(act, per_expert, per_unit)
            total = act.value_load(units[0:1, E + 1:E + 2], min_val=0, max_val=MOST)
            store(total)
            wait_alone(act, y_out, PRIMED + 16 * total + 16)

        @block.vector
        def _(dve):
            def transposed(g):
                dve.wait_ge(xT_ps, PRIMED + g + 1)
                nc.vector.tensor_copy(xT_hi[:], psT[:]).then_inc(xT_hi_done, 1)
                dve.wait_ge(xT_hi_done, PRIMED + g + 1)
                nc.vector.tensor_tensor(xT_lo[:], psT[:], xT_hi[:], ALU.subtract).then_inc(xT_done, 1)

            def per_expert(e, b, before, upto):
                wait_alone(dve, bias_in[b], 8 * (e - b) + 16)

            def per_unit(e, b, t, g):
                for m in range(KF):
                    dve.wait_ge(h_act, PRIMED + KF * g + m + 1)
                    nc.vector.tensor_copy(h_hi[:, m], h[:, m % 4]).then_inc(h_hi_done, 1)
                    dve.wait_ge(h_hi_done, PRIMED + KF * g + m + 1)
                    nc.vector.tensor_tensor(h_lo[:, m], h[:, m % 4], h_hi[:, m], ALU.subtract).then_inc(h_done, 1)
                transposed(g + 1)
                dve.wait_ge(y_ps, PRIMED + g + 1)
                dve.wait_ge(y_out, PRIMED + 16 * g + 16)
                for n in range(NH):
                    nc.vector.tensor_tensor(y[:, n], psY[n][:], bias[:, b, KF:], ALU.add).then_inc(y_done, 1)

            nc.vector.memset(y[:], 0.0).then_inc(y_done, 1)
            dve.wait_ge(ident_in, PRIMED + 16)
            transposed(0)
            for_units(dve, per_expert, per_unit)


def heads_phase(nc, x1_in, results, route, wkv3, wq, wp, bp_row, ident_dram, mask_dram, maskT_dram, x3_out,
                batches, ffn_weights, flag):
    T, D = x1_in.shape
    KD = D // P
    SEQ = T // batches
    NT = SEQ // P
    BANK = 512
    HALVES = SEQ // BANK
    PER = BANK // P
    HD = wkv3.shape[2] // 4
    HEADS = D // HD
    QB = 3
    HEADS_IN = [len(range(n, HEADS, QB)) for n in range(QB)]
    CHECK = ffn_weights.shape[1] // (batches * HEADS)
    SCALE = float(D) ** -0.5
    with ExitStack() as ctx:
        def sb(n, s, d=F32):
            return ctx.enter_context(nc.sbuf_tensor("m" + n, s, d))

        def psum(n, s):
            return ctx.enter_context(nc.psum_tensor("m" + n, s, F32))

        primed = []
        ctx.callback(nc.clear_and_free_semaphores, primed)

        def sem(n):
            primed.append(nc.alloc_semaphore("m" + n))
            return primed[-1]

        ident, ident_bf, mask_bf, maskT_bf = (sb(n, [P, P], d) for n, d in (
            ("ident", F32), ("ident_bf", BF16), ("mask_bf", BF16), ("maskT_bf", BF16)))
        wkv_raw = sb("wkv_raw", [P, KD, P])
        wkv_hi, wkv_lo = (sb(n, [P, KD, P], F32R) for n in ("wkv_hi", "wkv_lo"))
        wq_raw = sb("wq_raw", [P, KD, D])
        wq_hi, wq_lo = (sb(n, [P, KD, D], F32R) for n in ("wq_hi", "wq_lo"))
        q4_hi, q4_lo = (sb(n, [P, KD, SEQ], F32R) for n in ("q4_hi", "q4_lo"))
        wp_sb = sb("wp", [P, KD, D])
        bp = sb("bp", [P, D])
        x1 = sb("x1", [P, NT, D])
        y = [sb(f"y{c}", [P, NT, D]) for c in range(2)]
        x2 = sb("x2", [P, NT, D])
        res = sb("res", [P, NT, D])
        x2T_hi, x2T_lo = (sb(n, [P, KD, SEQ], F32R) for n in ("x2T_hi", "x2T_lo"))
        kvT = sb("kvT", [P, SEQ])
        k_rows = sb("k_rows", [P, SEQ], F32R)
        q_rows = [sb(f"q_rows{n}", [P, SEQ], F32R) for n in range(QB)]
        v1 = sb("v1", [P, NT, 2 * HD])
        prob = [sb(f"prob{n}", [P, BANK]) for n in range(3)]
        nmax = sb("nmax", [P, NT])
        nmT_hi, nmT_lo = (sb(n, [NT, P], F32R) for n in ("nmT_hi", "nmT_lo"))
        sums = sb("sums", [P, KD, SEQ])
        att = sb("att", [P, KD, SEQ])
        z = sb("z", [P, NT, D])
        st, stA = (sb(n, [P, NT, 6]) for n in ("st", "stA"))
        mv, mvA = (sb(n, [P, NT, 2]) for n in ("mv", "mvA"))
        rstd, var, tmp = (sb(n, [P, NT]) for n in ("rstd", "var", "tmp"))
        shifted = sb("shifted", [P, NT], I32)
        checked = sb("checked", [P, 2, CHECK])
        check_round = sb("check_round", [P, 2, CHECK], F32R)
        unequal = sb("unequal", [P, CHECK])
        miss = sb("miss", [P, HEADS])
        misses = sb("misses", [P, 1])
        missed = sb("missed", [P, 1])
        ones = sb("ones", [P, 1])
        rows_now = [sb(f"rows_now{c}", [P, NT], I32) for c in range(2)]
        weight_now = sb("weight_now", [P, 2, NT])
        unread = sb("unread", [1, 1])
        out_row = sb("out_row", [P, NT, D])
        S = [psum(f"S{n}", [P, SEQ]) for n in range(2)]
        ST = [psum(f"ST{n}", [P, BANK]) for n in range(2)]
        O = [psum(f"O{n}", [P, BANK]) for n in range(HALVES)]

        names = ("const_in setup x1_in rows_ready x2_done res_done t_ps t_hi t_lo kv_ps kv_sb k_hi k_lo v_ps "
                 "v_done q_ps q_hi q_lo s_ps mx nm_ps nm_hi nm_lo st_ps ex pv_ps o_used att_done pr_ps z_done chain x3_done "
                 "x3_st st_done stA_done "
                 "check_hi compared miss_done total_ps flag_done").split()
        (const_in, setup, x1_ld, rows_ready, x2_done, res_done, t_ps, t_hi, t_lo, kv_ps, kv_sb, k_hi, k_lo, v_ps,
         v_done, q_ps, q_hi, q_lo, s_ps, mx, nm_ps, nm_hi, nm_lo, st_ps, ex, pv_ps, o_used, att_done, pr_ps, z_done, chain,
         x3_done, x3_st, st_done, stA_done, check_hi, compared, miss_done, total_ps, flag_done) = (sem(n) for n in names)
        y_in = [sem(f"y_in{t}") for t in range(NT)]
        nm_in = [sem(f"nm_in{n}") for n in range(QB)]
        q_in = [sem(f"q_in{n}") for n in range(QB)]
        check_in = [sem(f"check_in{n}") for n in range(2)]
        unwatched = {n.engine: sem(f"unwatched{q}") for q, n in
                     enumerate((nc.sync, nc.gpsimd, nc.tensor, nc.scalar, nc.vector))}
        loads = [(ident[:], ident_dram), (z[:, 0, :P], mask_dram), (z[:, 1, :P], maskT_dram), (wkv_raw[:], wkv3), (wq_raw[:], wq), (wp_sb[:], wp), (bp[:], bp_row)]
        N_CONST = 16 * len(loads)
        SETUP = 2 + 5 + 2 * HALVES

        chunks = [(half, t) for half in range(HALVES) for t in range(PER * (half + 1))]
        NCH = len(chunks)
        TILES_AT = {1: (0, 1), 2: (2, 3), 3: (4, 5), 4: (6,), 5: (7,)}
        NORMALISE_AT = 6
        SCORES_AT = {0: (0, 1), 1: (2,), 2: (3,), 3: (4,), 4: (5,), 5: (6,), 6: (7,)}
        MAX_AT = 8
        ROWS_AT = {0: 0, 1: 1}
        Q_AT = {4: 0, 6: 1}
        PIECE = SEQ // 4
        assert HEADS == 8 and NT == 8

        by_gpsimd = [*y_in, *nm_in, *q_in]
        prime(nc, [s for s in primed if s not in by_gpsimd])
        block = ctx.enter_context(nc.Block())

        def wait_alone(eng, semaphore, value):
            eng.wait_ge(semaphore, value)
            eng.sem_inc(unwatched[eng.engine], 1)

        def tokens(ap, b):
            return ap.rearrange("(b t p) d -> b p t d", t=NT, p=P)[b]

        def each_sequence(eng, body):
            body(0, False, True)
            with eng.Fori(1, batches - 1) as b:
                body(b, True, True)
            body(batches - 1, True, False)

        def of_head(b, h):
            return HEADS_IN[h % QB] * b + h // QB + 1

        @block.sync
        def _(sp):
            sp.dma_start(x1[:], tokens(x1_in, 0)).then_inc(x1_ld, 16)
            for d, s in loads:
                sp.dma_start(d, s).then_inc(const_in, 16)

            def store(b):
                sp.wait_ge(x3_done, PRIMED + b + 1)
                sp.dma_start(tokens(x3_out, b), out_row[:]).then_inc(x3_st, 16)

            def sequence(b, earlier, more):
                if more:
                    sp.wait_ge(x2_done, PRIMED + b + 1)
                    sp.dma_start(x1[:], tokens(x1_in, b + 1)).then_inc(x1_ld, 16)
                for h in range(HEADS):
                    n = HEADS * b + h
                    if earlier or h >= 2:
                        sp.wait_ge(compared, PRIMED + n - 1)
                    sp.dma_start(checked[:, h % 2], ffn_weights[:, bass.ds(n * CHECK, CHECK)]).then_inc(check_in[h % 2], 16)
                    if earlier and h == 3:
                        store(b - 1)

            each_sequence(sp, sequence)
            store(batches - 1)
            sp.wait_ge(x3_st, PRIMED + 16 * batches)

        @block.gpsimd
        def _(pool):
            def gather(t):
                for c in range(2):
                    pool.indirect_dma_start(out=y[c][:, t, :], out_offset=None, in_=results,
                                            in_offset=bass.IndirectOffsetOnAxis(ap=rows_now[c][:, t:t + 1], axis=0)
                                            ).then_inc(y_in[t], 16)

            pool.wait_ge(rows_ready, PRIMED + 1)
            for t in range(NT):
                gather(t)
            pool.wait_ge(const_in, PRIMED + N_CONST)
            pool.wait_ge(setup, PRIMED + SETUP)

            def stack(b, h, earlier=True):
                if h >= QB:
                    wait_alone(pool, st_ps, PRIMED + NCH * (HEADS * b + h - QB + 1))
                elif earlier:
                    wait_alone(pool, st_ps, PRIMED + NCH * (HEADS * (b - 1) + QB * (HEADS_IN[h] - 1) + h + 1))
                rows = slice(h % PER * HD, (h % PER + 1) * HD)
                for r, part in enumerate((q4_hi, q4_hi, q4_lo)):
                    pool.dma_start(q_rows[h % QB][r * HD:(r + 1) * HD, :], part[rows, h // PER, :]).then_inc(q_in[h % QB], 16)

            def sequence(b, earlier, more):
                if not earlier:
                    pool.wait_ge(q_lo, PRIMED + 1)
                    stack(b, 0, False)
                    stack(b, 1, False)
                for h in range(HEADS):
                    n = HEADS * b + h
                    for r, (row, ready) in enumerate(((nmT_hi, nm_hi), (nmT_lo, nm_lo))):
                        wait_alone(pool, ready, PRIMED + n + 1)
                        pool.dma_start(q_rows[h % QB][3 * HD + r:3 * HD + r + 1, :].rearrange("o (t q) -> o t q", q=P),
                                       row[:]).then_inc(nm_in[h % QB], 16)
                    if h + 2 < HEADS:
                        if h + 2 == PER:
                            wait_alone(pool, q_lo, PRIMED + KD * b + 2)
                        stack(b, h + 2, earlier)
                    if h == 0:
                        pool.wait_ge(z_done, PRIMED + NT * b)
                        pool.wait_ge(x2_done, PRIMED + b + 1)
                        nc.gpsimd.tensor_tensor(res[:], x2[:], bp[:].unsqueeze(1).to_broadcast([P, NT, D]),
                                                ALU.add).then_inc(res_done, 1)
                    if more and h < 4:
                        if h == 0:
                            wait_alone(pool, rows_ready, PRIMED + b + 2)
                        gather(2 * h)
                        gather(2 * h + 1)
                if more:
                    wait_alone(pool, q_lo, PRIMED + KD * (b + 1) + 1)
                    stack(b + 1, 0)
                    stack(b + 1, 1)

            each_sequence(pool, sequence)
            for n in range(QB):
                pool.wait_ge(nm_in[n], 32 * of_head(batches - 1, HEADS - QB + (n - HEADS) % QB))

        @block.tensor
        def _(pe):
            def three(ps, left, right, first, last):
                (lh, ll), (rh, rl) = left, right
                nc.tensor.matmul(ps, lh, rh, start=first, stop=False)
                nc.tensor.matmul(ps, lh, rl, start=False, stop=False)
                return nc.tensor.matmul(ps, ll, rh, start=False, stop=last)

            def bank(n):
                return slice(n * BANK, (n + 1) * BANK)

            def tile(n):
                return slice(n * P, (n + 1) * P)

            def project_q(b, g):
                pe.wait_ge(t_lo, PRIMED + KD * (b + 1))
                for c in range(HALVES):
                    for k in range(KD):
                        last = three(S[g][:, bank(c)], (wq_hi[:, k, tile(g)], wq_lo[:, k, tile(g)]),
                                     (x2T_hi[:, k, bank(c)], x2T_lo[:, k, bank(c)]), k == 0, k == KD - 1)
                last.then_inc(q_ps, 1)

            def scores(b, h, i):
                n = HEADS * b + h
                if i == 0:
                    if h:
                        pe.wait_ge(nm_lo, PRIMED + n)
                    else:
                        pe.wait_ge(q_lo, PRIMED + KD * (b + 1))
                        pe.wait_ge(z_done, PRIMED + NT * b)
                        pe.wait_ge(k_lo, PRIMED + HALVES * (b + 1))
                    pe.wait_ge(q_in[h % QB], 48 * of_head(b, h))
                elif i >= 2 or h:
                    pe.wait_ge(mx, PRIMED + NT * n + i - 1)
                s = S[i % 2]
                width = (i + 1) * P
                for c in range(0, width, BANK):
                    c1 = min(width, c + BANK)
                    nc.tensor.matmul(s[:, c:c1], q_rows[h % QB][:3 * HD, tile(i)], k_rows[:3 * HD, c:c1], start=True, stop=True)
                nc.tensor.matmul(s[:, i * P:width], ident_bf[:], mask_bf[:], start=False, stop=True,
                                 skip_group_check=True).then_inc(s_ps, 1)

            def transpose_max(b, h):
                n = HEADS * b + h
                pe.wait_ge(mx, PRIMED + NT * (n + 1))
                nc.tensor.transpose(S[0][:NT, :P], nmax[:], ident[:]).then_inc(nm_ps, 1)

            def scores_T(b, h, c):
                n = HEADS * b + h
                half, t = chunks[c]
                if c == 0:
                    pe.wait_ge(nm_in[h % QB], 32 * of_head(b, h))
                if h == 0 and c < 2:
                    pe.wait_ge(v_done, PRIMED + 2 * (b + 1))
                else:
                    pe.wait_ge(ex, PRIMED + NCH * n + c - 1)
                off = max(0, t - PER * half) * P
                last = nc.tensor.matmul(ST[c % 2][:, off:], k_rows[:, tile(t)],
                                        q_rows[h % QB][:, half * BANK + off:(half + 1) * BANK], start=True, stop=True)
                if t >= PER * half:
                    last = nc.tensor.matmul(ST[c % 2][:, off:off + P], ident_bf[:], maskT_bf[:], start=False, stop=True,
                                            skip_group_check=True)
                last.then_inc(st_ps, 1)

            def weigh(b, h, c):
                n = HEADS * b + h
                half, t = chunks[c]
                if t == 0 and h:
                    pe.wait_ge(o_used, PRIMED + HALVES * (n - 1) + half + 1)
                pe.wait_ge(ex, PRIMED + NCH * n + c + 1)
                off = max(0, t - PER * half) * P
                nc.tensor.matmul(O[half][:2 * HD, off:], v1[:, t, :], prob[c % 3][:, off:], start=(t == 0), stop=True,
                                 skip_group_check=(t > 0)).then_inc(pv_ps, 1)

            pe.wait_ge(const_in, PRIMED + N_CONST)
            pe.wait_ge(setup, PRIMED + SETUP)

            def transpose_rows(b, k):
                pe.wait_ge(x2_done, PRIMED + b + 1)
                for t in range(NT):
                    last = nc.tensor.transpose(S[k][:, tile(t)], x2[:, t, tile(k)], ident[:])
                last.then_inc(t_ps, 1)

            def sequence(b, earlier, more):
                if not earlier:
                    for k in range(KD):
                        transpose_rows(b, k)
                    for g in range(KD):
                        project_q(b, g)
                pe.wait_ge(o_used, PRIMED + HALVES * HEADS * b)
                for c in range(HALVES):
                    for k in range(KD):
                        last = three(O[c][:], (wkv_hi[:, k, :], wkv_lo[:, k, :]),
                                     (x2T_hi[:, k, bank(c)], x2T_lo[:, k, bank(c)]), k == 0, k == KD - 1)
                    last.then_inc(kv_ps, 1)
                pe.wait_ge(ex, PRIMED + NCH * HEADS * b)
                for c in range(HALVES):
                    pe.wait_ge(kv_sb, PRIMED + HALVES * b + c + 1)
                    for n in range(PER):
                        last = nc.tensor.transpose(ST[c][:, tile(n)], kvT[:, tile(PER * c + n)], ident[:])
                    last.then_inc(v_ps, 1)
                for i in range(NT):
                    scores(b, 0, i)
                transpose_max(b, 0)
                for h in range(HEADS):
                    scores_T(b, h, 0)
                    for c in range(NCH):
                        if c + 1 < NCH:
                            scores_T(b, h, c + 1)
                        if h + 1 < HEADS:
                            for i in SCORES_AT.get(c, ()):
                                scores(b, h + 1, i)
                            if c == MAX_AT:
                                transpose_max(b, h + 1)
                        elif more:
                            if c == 0:
                                pe.wait_ge(nm_lo, PRIMED + HEADS * (b + 1))
                            if c in ROWS_AT:
                                transpose_rows(b + 1, ROWS_AT[c])
                            if c in Q_AT:
                                project_q(b + 1, Q_AT[c])
                        weigh(b, h, c)
                if more:
                    pe.wait_ge(q_lo, PRIMED + KD * (b + 2))
                for i in range(NT):
                    if i % 2 == 0:
                        pe.wait_ge(att_done, PRIMED + 8 * b + 4 + i // 2 + 1)
                    if i >= 2:
                        pe.wait_ge(z_done, PRIMED + NT * b + i - 1)
                    for k in range(KD):
                        last = nc.tensor.matmul(S[i % 2][:, :D], att[:, k, tile(i)], wp_sb[:, k, :], start=(k == 0),
                                                stop=(k == KD - 1))
                    last.then_inc(pr_ps, 1)

            each_sequence(pe, sequence)
            pe.wait_ge(miss_done, PRIMED + 2 * batches)
            nc.tensor.matmul(ST[0][:1, :1], misses[:], ones[:], start=True, stop=True).then_inc(total_ps, 1)

        @block.scalar
        def _(act):
            act.wait_ge(const_in, PRIMED + N_CONST)
            nc.scalar.activation(wkv_hi[:], wkv_raw[:], ACT.Copy).then_inc(setup, 1)
            nc.scalar.activation(wq_hi[:], wq_raw[:], ACT.Copy).then_inc(setup, 1)

            def copy_out(b, h, half):
                act.wait_ge(pv_ps, PRIMED + NCH * (HEADS * b + h) + PER + half * (NCH - PER))
                rows = slice(h % PER * HD, (h % PER + 1) * HD)
                cols = slice(half * BANK, (half + 1) * BANK)
                if h == 0 and half == 0:
                    act.wait_ge(pr_ps, PRIMED + NT * b)
                nc.scalar.activation(att[rows, h // PER, cols], O[half][:HD, :], ACT.Copy)
                nc.scalar.activation(sums[rows, h // PER, cols], O[half][HD:2 * HD, :], ACT.Copy).then_inc(o_used, 1)

            def rows_high(b, k):
                act.wait_ge(t_ps, PRIMED + KD * b + k + 1)
                nc.scalar.activation(x2T_hi[:, k, :], S[k][:], ACT.Copy).then_inc(t_hi, 1)

            def q_high(b, g):
                act.wait_ge(q_ps, PRIMED + KD * b + g + 1)
                nc.scalar.activation(q4_hi[:, g, :], S[g][:], ACT.Copy, scale=SCALE).then_inc(q_hi, 1)

            def check(b, h, earlier):
                n = HEADS * b + h
                act.wait_ge(check_in[h % 2], PRIMED + HEADS // 2 * 16 * b + 16 * (h // 2 + 1))
                if earlier or h >= 2:
                    act.wait_ge(compared, PRIMED + n - 1)
                nc.scalar.activation(check_round[:, h % 2], checked[:, h % 2], ACT.Copy).then_inc(check_hi, 1)

            def sequence(b, earlier, more):
                if not earlier:
                    for k in range(KD):
                        rows_high(b, k)
                    for g in range(KD):
                        q_high(b, g)
                for c in range(HALVES):
                    act.wait_ge(kv_ps, PRIMED + HALVES * b + c + 1)
                    cols = slice(c * BANK, (c + 1) * BANK)
                    nc.scalar.activation(k_rows[:3 * HD, cols], O[c][:3 * HD, :], ACT.Copy).then_inc(k_hi, 1)
                    nc.scalar.activation(kvT[:, cols], O[c][:], ACT.Copy).then_inc(kv_sb, 1)
                for h in range(HEADS):
                    n = HEADS * b + h
                    for c, (half, t) in enumerate(chunks):
                        off = max(0, t - PER * half) * P
                        act.wait_ge(st_ps, PRIMED + NCH * n + c + 1)
                        if h or c >= 3:
                            act.wait_ge(pv_ps, PRIMED + NCH * n + c - 2)
                        nc.scalar.activation(prob[c % 3][:, off:], ST[c % 2][:, off:], ACT.Exp).then_inc(ex, 1)
                        if c == 1 and h:
                            copy_out(b, h - 1, 1)
                        if c == PER + 2:
                            copy_out(b, h, 0)
                        if c == PER + 4:
                            check(b, h, earlier)
                        if more and h == HEADS - 1:
                            if c - 1 in ROWS_AT:
                                rows_high(b + 1, ROWS_AT[c - 1])
                            if c - 2 in Q_AT:
                                q_high(b + 1, Q_AT[c - 2])
                copy_out(b, HEADS - 1, 1)

            each_sequence(act, sequence)

        @block.vector
        def _(dve):
            n_link = [0]
            base = [0]

            def link(ins, alone=False):
                n_link[0] += 1
                ins.then_inc(chain, 1)
                (wait_alone if alone else lambda e, s, v: e.wait_ge(s, v))(dve, chain, PRIMED + base[0] + n_link[0])

            def normalised(dst, src, stats, mean_var, done):
                for i in range(NT):
                    ins = nc.vector.bn_aggr(mean_var[:, i], stats[:, i])
                link(ins)
                link(nc.vector.tensor_copy(var[:], mean_var[:, :, 1]))
                rsqrt(nc, link, rstd[:], var[:], tmp[:], shifted[:])
                if dst is out_row:
                    dve.wait_ge(x3_st, PRIMED + 16 * seq[0])
                for i in range(NT):
                    ins = nc.vector.tensor_scalar(dst[:, i], src[:, i], mean_var[:, i, 0:1], rstd[:, i:i + 1], ALU.subtract,
                                                  ALU.mult)
                ins.then_inc(done, 1)

            seq = [0]

            def plan(n):
                cols = bass.ds(n * NT, NT)
                for c in range(2):
                    link(nc.vector.tensor_copy(rows_now[c][:], route["row"][c][:, cols]))
                    link(nc.vector.tensor_copy(weight_now[:, c], route["weight"][c][:, cols]))
                nc.vector.memset(unread[:], 0.0).then_inc(rows_ready, 1)

            def residual(n, t):
                dve.wait_ge(y_in[t], 32 * (n + 1))
                link(nc.vector.scalar_tensor_tensor(x2[:, t], y[0][:, t], weight_now[:, 0, t:t + 1], x1[:, t], ALU.mult, ALU.add))
                link(nc.vector.scalar_tensor_tensor(x2[:, t], y[1][:, t], weight_now[:, 1, t:t + 1], x2[:, t], ALU.mult, ALU.add))
                nc.vector.bn_stats(stA[:, t], x2[:, t]).then_inc(stA_done, 1)

            plan(0)
            dve.wait_ge(const_in, PRIMED + N_CONST)
            dve.wait_ge(setup, PRIMED + 2)
            nc.vector.tensor_tensor(wkv_lo[:], wkv_raw[:], wkv_hi[:], ALU.subtract).then_inc(setup, 1)
            nc.vector.tensor_tensor(wq_lo[:], wq_raw[:], wq_hi[:], ALU.subtract).then_inc(setup, 1)
            nc.vector.tensor_copy(ident_bf[:], ident[:])
            nc.vector.tensor_copy(mask_bf[:], z[:, 0, :P])
            nc.vector.tensor_copy(maskT_bf[:], z[:, 1, :P])
            nc.vector.memset(ones[:], 1.0)
            nc.vector.memset(misses[:], 0.0)
            nc.vector.memset(v1[:], 1.0).then_inc(setup, 1)
            nc.vector.memset(prob[0][:], 0.0).then_inc(setup, 1)
            nc.vector.memset(prob[1][:], 1.0).then_inc(setup, 1)
            dve.wait_ge(setup, PRIMED + SETUP - 4)
            rows = slice(3 * HD, 4 * HD)
            for n in range(HALVES):
                cols = slice(n * BANK, (n + 1) * BANK)
                for m in range(QB):
                    nc.vector.tensor_copy(q_rows[m][rows, cols], prob[0][rows, :])
                nc.vector.tensor_copy(k_rows[rows, cols], prob[0][rows, :]).then_inc(setup, 1)
            dve.wait_ge(setup, PRIMED + SETUP - 2)
            for n in range(HALVES):
                nc.vector.tensor_copy(k_rows[3 * HD:3 * HD + 2, n * BANK:(n + 1) * BANK],
                                      prob[1][3 * HD:3 * HD + 2, :]).then_inc(setup, 1)

            dve.wait_ge(x1_ld, PRIMED + 16)
            for t in range(NT):
                residual(0, t)
            dve.wait_ge(stA_done, PRIMED + NT)
            normalised(x2, x2, stA, mvA, x2_done)
            first_links = n_link[0]
            dve.wait_ge(x2_done, PRIMED + 1)

            def rows_low(b, k):
                dve.wait_ge(t_hi, PRIMED + KD * b + k + 1)
                nc.vector.tensor_tensor(x2T_lo[:, k, :], S[k][:], x2T_hi[:, k, :], ALU.subtract).then_inc(t_lo, 1)

            def q_low(b, g):
                dve.wait_ge(q_hi, PRIMED + KD * b + g + 1)
                nc.vector.scalar_tensor_tensor(q4_lo[:, g, :], S[g][:], SCALE, q4_hi[:, g, :], ALU.mult,
                                               ALU.subtract).then_inc(q_lo, 1)

            def compare(b, h):
                n = HEADS * b + h
                dve.wait_ge(check_hi, PRIMED + n + 1)
                dve.wait_ge(compared, PRIMED + n)
                nc.vector.scalar_tensor_tensor(unequal[:], checked[:, h % 2], 1.0, check_round[:, h % 2], ALU.mult,
                                               ALU.not_equal, accum_out=miss[:, h:h + 1]).then_inc(compared, 1)

            def sum_misses(b):
                dve.wait_ge(compared, PRIMED + HEADS * (b + 1))
                nc.vector.reduce_sum(missed[:], miss[:], X).then_inc(miss_done, 1)
                dve.wait_ge(miss_done, PRIMED + 2 * b + 1)
                nc.vector.tensor_tensor(misses[:], misses[:], missed[:], ALU.add).then_inc(miss_done, 1)
                dve.wait_ge(miss_done, PRIMED + 2 * b + 2)

            def row_max(b, h, i):
                dve.wait_ge(s_ps, PRIMED + NT * (HEADS * b + h) + i + 1)
                nc.vector.tensor_reduce(nmax[:, i:i + 1], S[i % 2][:, :(i + 1) * P], X, ALU.max, negate=True).then_inc(mx, 1)

            def max_rows(b, h):
                n = HEADS * b + h
                dve.wait_ge(nm_ps, PRIMED + n + 1)
                if h:
                    dve.wait_ge(nm_in[(h - 1) % QB], 32 * of_head(b, h - 1))
                nc.vector.tensor_copy(nmT_hi[:], S[0][:NT, :P]).then_inc(nm_hi, 1)
                dve.wait_ge(nm_hi, PRIMED + n + 1)
                nc.vector.tensor_tensor(nmT_lo[:], S[0][:NT, :P], nmT_hi[:], ALU.subtract).then_inc(nm_lo, 1)

            def normalise(b, group, piece):
                if piece % 2 == 0:
                    dve.wait_ge(o_used, PRIMED + HALVES * (HEADS * b + PER * group + PER - 1) + piece // 2 + 1)
                cols = slice(piece * PIECE, (piece + 1) * PIECE)
                link(nc.vector.reciprocal(sums[:, group, cols], sums[:, group, cols]))
                nc.vector.tensor_tensor(att[:, group, cols], att[:, group, cols], sums[:, group, cols],
                                        ALU.mult).then_inc(att_done, 1)

            def sequence(b, earlier, more):
                n_link[0] = 0
                base[0] = first_links + (4 + 2 * NT + 8 + 2 + RSQRT_LINKS) if earlier else first_links
                if earlier:
                    base[0] = base[0] + LINKS * (b - 1)
                seq[0] = b - 1
                if not earlier:
                    for k in range(KD):
                        rows_low(b, k)
                    for g in range(KD):
                        q_low(b, g)
                part = slice(HD, 2 * HD)
                for c in range(HALVES):
                    cols = slice(c * BANK, (c + 1) * BANK)
                    dve.wait_ge(k_hi, PRIMED + HALVES * b + c + 1)
                    dve.wait_ge(kv_sb, PRIMED + HALVES * b + c + 1)
                    nc.vector.tensor_tensor(k_rows[part, cols], O[c][part, :], k_rows[part, cols],
                                            ALU.subtract).then_inc(k_lo, 1)
                for c in range(HALVES):
                    dve.wait_ge(v_ps, PRIMED + HALVES * b + c + 1)
                    nc.vector.tensor_copy(v1[:, PER * c:PER * (c + 1), :HD],
                                          ST[c][:].rearrange("p (t s) -> p t s", s=P)[:, :, 3 * HD:]).then_inc(v_done, 1)
                for i in range(NT):
                    row_max(b, 0, i)
                max_rows(b, 0)
                if more:
                    plan(b + 1)
                for h in range(HEADS):
                    following = h + 1 < HEADS
                    if following:
                        for i in range(NT):
                            row_max(b, h + 1, i)
                        max_rows(b, h + 1)
                    if earlier and h == 0:
                        wait_alone(dve, st_done, PRIMED + NT * b)
                        normalised(out_row, z, st, mv, x3_done)
                    if more and h in TILES_AT:
                        if h == min(TILES_AT):
                            dve.wait_ge(x1_ld, PRIMED + 16 * (b + 2))
                            dve.wait_ge(res_done, PRIMED + b + 1)
                        for t in TILES_AT[h]:
                            residual(b + 1, t)
                    if more and h == NORMALISE_AT:
                        wait_alone(dve, stA_done, PRIMED + NT * (b + 2))
                        normalised(x2, x2, stA, mvA, x2_done)
                        dve.wait_ge(x2_done, PRIMED + b + 2)
                    if more and h == HEADS - 1:
                        for k in range(KD):
                            rows_low(b + 1, k)
                    if PER <= h < 2 * PER:
                        normalise(b, 0, h - PER)
                    if more and h == HEADS - 1:
                        for g in range(KD):
                            q_low(b + 1, g)
                    if h == HEADS - 1:
                        normalise(b, 1, 0)
                        normalise(b, 1, 1)
                    compare(b, h)
                sum_misses(b)
                for piece in range(2, 4):
                    normalise(b, 1, piece)
                dve.wait_ge(res_done, PRIMED + b + 1)
                for i in range(NT):
                    dve.wait_ge(pr_ps, PRIMED + NT * b + i + 1)
                    if i == 0 and earlier:
                        dve.wait_ge(x3_done, PRIMED + b)
                    nc.vector.tensor_tensor(z[:, i], S[i % 2][:, :D], res[:, i], ALU.add).then_inc(z_done, 1)
                    dve.wait_ge(z_done, PRIMED + NT * b + i + 1)
                    nc.vector.bn_stats(st[:, i], z[:, i]).then_inc(st_done, 1)
                if not more:
                    dve.wait_ge(st_done, PRIMED + NT * batches)
                    seq[0] = b
                    normalised(out_row, z, st, mv, x3_done)
                if more and earlier:
                    assert n_link[0] == LINKS, (n_link[0], LINKS)

            LINKS = 4 + 2 * NT + 8 + 2 * (2 + RSQRT_LINKS)
            each_sequence(dve, sequence)
            dve.wait_ge(total_ps, PRIMED + 1)
            nc.vector.tensor_scalar(flag[0:1, 0:1], ST[0][:1, :1], 0.0, None, ALU.is_gt).then_inc(flag_done, 1)
            dve.wait_ge(flag_done, PRIMED + 1)


def model_program(nc, t, out):
    T, D = t["x"].shape
    batches = t["xT"].shape[0]
    experts = t["expert_weights"].shape[0]
    tiles = T // P
    capacity = T + UNIT
    most_units = (2 * T) // UNIT + experts - 1
    x1, x3 = (nc.dram_tensor(n, [T, D], F32, kind="Internal").ap() for n in ("x1_dram", "x3_dram"))
    slots = nc.dram_tensor("slots_dram", [experts * capacity, D], F32, kind="Internal").ap()
    results = nc.dram_tensor("results_dram", [(most_units + 1) * UNIT, D], F32, kind="Internal").ap()
    with ExitStack() as ctx:
        def sb(n, s, d=F32):
            return ctx.enter_context(nc.sbuf_tensor(n, s, d))

        weights_inexact = sb("weights_inexact", [1, 1], I32)
        with ExitStack() as routing:
            def rsb(n, s, d=F32):
                return routing.enter_context(nc.sbuf_tensor(n, s, d))

            units = rsb("units", [1, experts + 2], I32)
            route = dict(weight=[rsb(f"weight{c}", [P, tiles]) for c in range(2)],
                         row=[rsb(f"row{c}", [P, tiles], I32) for c in range(2)])
            with ExitStack() as counting:
                def csb(n, s):
                    return counting.enter_context(nc.sbuf_tensor(n, s, F32))

                route.update(rank=[csb(f"rank{c}", [P, tiles]) for c in range(2)],
                             onehot=[csb(f"onehot{c}", [P, tiles, experts]) for c in range(2)],
                             count=csb("count", [P, experts]))
                attend_and_route_phase(nc, t["x"], t["xT"], t["wqT"], t["wkT"], t["wvT"], t["wo"], t["w_router"],
                                       t["b_router"], t, route, x1, slots, batches, capacity)
                plan_phase(nc, route, units, t["unit_starts"], slots, results, capacity, UNIT)
            moe_phase(nc, units, slots, t["expert_weights"], t["expert_biases"], results, t["ident"], capacity, T)
            heads_phase(nc, x1, results, route, t["wkv"], t["wq"], t["wp"], t["bp"], t["ident"], t["mask"], t["maskT"], x3,
                        batches, t["ffn_weights"], weights_inexact)
        for split in (True, False):
            ffn_phase(nc, weights_inexact, x3, t["ffn_weights"], t["ffn_scales"], t["w3_scales"], out,
                      t["ident"], split)


def kernel(**inputs):
    import numpy as np
    import concourse.bacc as bacc
    from concourse.bass_utils import run_bass_kernel_spmd

    a = {n: np.asarray(v) for n, v in inputs.items()}
    f32 = np.float32
    B, S, D = a["L0_attn_x"].shape
    E, _, F = a["L0_ffn_W1"].shape

    def rows(w):
        return w.reshape(-1, P, *w.shape[1:]).swapaxes(0, 1)

    def on_all(v):
        return np.broadcast_to(v, (P, v.shape[0]))

    def by_block(v):
        return v.reshape(-1, P).T

    square = np.ones((P, P), f32)
    Wk, Wv, Wq = a["L1_attn_Wk"], a["L1_attn_Wv"], a["L1_attn_Wq"]
    data = {
        "x": a["L0_attn_x"].reshape(B * S, D),
        "xT": a["L0_attn_x"].reshape(B, S, D // P, P).transpose(0, 3, 2, 1),
        "wqT": rows(a["L0_attn_Wq"].T), "wkT": rows(a["L0_attn_Wk"].T), "wvT": rows(a["L0_attn_Wv"].T),
        "wo": rows(a["L0_attn_Wo"]),
        "w_router": rows(a["L0_ffn_W_router"]), "b_router": on_all(a["L0_ffn_b_router"]),
        "expert_weights": np.concatenate([
            a["L0_ffn_W1"].reshape(E, D // P, P, F).transpose(0, 2, 1, 3).reshape(E, P, -1),
            a["L0_ffn_W2"].reshape(E, F // P, P, D).transpose(0, 2, 1, 3).reshape(E, P, -1)], 2),
        "expert_biases": np.concatenate([
            a["L0_ffn_b1"].reshape(E, F // P, P).transpose(0, 2, 1),
            np.broadcast_to(a["L0_ffn_b2"][:, None], (E, P, D))], 2),
        "wkv": rows(np.concatenate([Wk, Wk, Wk, Wv], 1)),
        "wq": rows(Wq.transpose(1, 0, 2).reshape(D, -1)),
        "wp": rows(a["L1_attn_Wp"]), "bp": on_all(a["L1_attn_bp"]),
        "ffn_weights": np.concatenate([rows(a[f"L1_ffn_{n}_w"].T).reshape(P, -1) for n in ("w1", "w2", "h1", "h2", "w3")], 1),
        "ffn_scales": np.stack([by_block(a[f"L1_ffn_{n}_s"]) for n in ("w1", "w2", "h1", "h2")], 1),
        "w3_scales": on_all(a["L1_ffn_w3_s"]),
        "ident": np.eye(P, dtype=f32), "mask": np.triu(square, 1) * f32(-1e30), "maskT": np.tril(square, -1) * f32(-1e30),
        "before_me": np.triu(square, 1), "all_ones": square, "iota_e": on_all(np.arange(E, dtype=f32)),
        "unit_starts": on_all(np.arange(0, B * S, UNIT, dtype=f32)),
    }
    nc = bacc.Bacc("TRN2", target_bir_lowering=False, num_devices=1)
    arrays = {n + "_dram": np.ascontiguousarray(v) for n, v in data.items()}
    t = {n[:-5]: nc.dram_tensor(n, v.shape, mybir.dt.from_np(v.dtype), kind="ExternalInput").ap()
         for n, v in arrays.items()}
    out = nc.dram_tensor("out_dram", [B * S, D], F32, kind="ExternalOutput").ap()
    model_program(nc, t, out)
    result = run_bass_kernel_spmd(nc, [arrays], core_ids=[0])
    return result.results[0]["out_dram"].reshape(B, S, D)
```

```python
from contextlib import ExitStack

import concourse.bass as bass
from concourse import mybir
from concourse.alu_op_type import AluOpType as ALU

F32 = mybir.dt.float32
F32R = mybir.dt.float32r
BF16 = mybir.dt.bfloat16
I32 = mybir.dt.int32
U32 = mybir.dt.uint32
ACT = mybir.ActivationFunctionType
X = mybir.AxisListType.X
P = 128
EPS = 1e-5
PRIMED = 1
UNIT = 256


def prime(nc, semaphores):
    with nc.Block() as block:
        @block.gpsimd
        def _(pool):
            for semaphore in semaphores:
                pool.sem_inc(semaphore, PRIMED)


RSQRT_STEPS = 3
RSQRT_LINKS = 3 + 3 * RSQRT_STEPS


def rsqrt(nc, link, y, v, t, shifted):
    link(nc.vector.tensor_scalar(v, v, EPS, None, ALU.add))
    link(nc.vector.tensor_scalar(shifted, v.bitcast(I32), 1, None, ALU.logical_shift_right))
    link(nc.vector.tensor_scalar(y.bitcast(I32), shifted, -1, 0x5F3759DF, ALU.mult, ALU.add))
    for _ in range(RSQRT_STEPS):
        link(nc.vector.scalar_tensor_tensor(t, y, -0.5, v, ALU.mult, ALU.mult))
        link(nc.vector.tensor_tensor(t, t, y, ALU.mult))
        link(nc.vector.scalar_tensor_tensor(y, t, 1.5, y, ALU.add, ALU.mult))


FFN_PIECE = 1024


def ffn_phase(nc, flag, x_in, ffn_weights, s_cols, s3_row, out, ident_dram, split):
    T, D = x_in.shape
    KD = D // P
    KF = 1024 // P
    FH = KF * P
    CH = 512
    NT = CH // P
    PAIRS = T // CH // 2
    WDT = F32R if split else F32
    name = "f" if split else "g"
    with ExitStack() as ctx:
        def sb(n, s, d=F32):
            return ctx.enter_context(nc.sbuf_tensor(name + n, s, d))

        primed = []
        ctx.callback(nc.clear_and_free_semaphores, primed)

        def sem(n):
            primed.append(nc.alloc_semaphore(name + n))
            return primed[-1]

        parts = 2 if split else 1
        w1_sb, w2_sb = (sb(n, [P, KD, FH], WDT) for n in ("w1", "w2"))
        h1_sb, h2_sb = (sb(n, [P, KF, FH], WDT) for n in ("h1", "h2"))
        w3_sb = sb("w3", [P, KF, D], WDT)
        ident = sb("ident", [P, P])
        scl = sb("scl", [P, 4, KF])
        half = sb("half", [P, 2, KF])
        s3 = sb("s3", [P, D])
        x = sb("x", [P, 2, NT, D])
        xT = [sb(f"xT{q}", [P, KD, CH], WDT) for q in range(parts)]
        ha = [sb(f"ha{q}", [P, KF, CH], WDT) for q in range(parts)]
        hb = [sb(f"hb{q}", [P, KF, CH], WDT) for q in range(parts)]
        t = sb("t", [P, 2, CH])
        a = sb("a", [P, 2, CH])
        g = sb("g", [P, 2, CH])
        z = sb("z", [P, NT, D])
        st = sb("st", [P, NT, 6])
        mv = sb("mv", [P, NT, 2])
        rstd, var, tmp = (sb(n, [P, NT]) for n in ("rstd", "var", "tmp"))
        shifted = sb("shifted", [P, NT], I32)
        o = sb("o", [P, 2, NT, D])
        mm = [ctx.enter_context(nc.psum_tensor(f"{name}mm{b}", [P, CH], F32)) for b in range(6)]
        psT = [ctx.enter_context(nc.psum_tensor(f"{name}psT{k}", [P, CH], F32)) for k in range(KD)]
        up = [(mm[2 * p], mm[2 * p + 1]) for p in range(3)]
        psY = [mm[4 + n][:, :D] for n in range(2)]

        const_in, w_in, half_done, xT_hi_done, xT_done, up_ps, t_ready, g_done, hi_done = (sem(n) for n in (
            "const_in", "w_in", "half_done", "xT_hi_done", "xT_done", "up_ps", "t_ready", "g_done", "hi_done"))
        x_loaded = [sem(f"x_loaded{j}") for j in range(2)]
        xT_ps = sem("xT_ps")
        a_done = sem("a_done")
        h0_done = sem("h0_done")
        hid_ps = [sem("h1_ps"), sem("h2_ps")]
        gelu_done = [sem("gelu1_done"), sem("gelu2_done")]
        hid_hi = sem("hid_hi")
        split_done = [sem("split1_done"), sem("split2_done")]
        y_ps, y_used, z_done, st_done, mv_done, chain, o_ready = (sem(n) for n in (
            "y_ps", "y_used", "z_done", "st_done", "mv_done", "chain", "o_ready"))
        o_out = [sem(f"o_out{j}") for j in range(2)]
        N_CONST = 16 * 3

        weights = (w1_sb, w2_sb, h1_sb, h2_sb, w3_sb)
        pieces = [ffn_weights[:, q:q + FFN_PIECE] for q in range(0, ffn_weights.shape[1], FFN_PIECE)]
        to = [w.rearrange("p k n -> p (k n)")[:, q:q + FFN_PIECE] for w in (w[:] for w in weights)
              for q in range(0, w.shape[1] * w.shape[2], FFN_PIECE)]
        upto = [sum(w.shape[1] * w.shape[2] for w in weights[:n + 1]) // FFN_PIECE for n in range(len(weights))]
        if split:
            staged = sb("staged", [P, 2, FFN_PIECE])
            outputs = o[:].rearrange("p j n d -> p (j n d)")
            stage = [outputs[:, n * FFN_PIECE:(n + 1) * FFN_PIECE] if n < 2 else staged[:, n % 2, :]
                     for n in range(len(pieces))]
            stage_in = [sem(f"stage_in{b}") for b in range(4)]

            def stage_sem(n):
                return (stage_in[n], 1) if n < 2 else (stage_in[2 + n % 2], n // 2)

            rounded = sem("rounded")
        prime(nc, primed)
        block = ctx.enter_context(nc.Block())

        def guarded(eng):
            value = eng.value_load(flag[0:1, 0:1], min_val=0, max_val=1)
            return eng.If(1 - value if split else value)

        def chunk_dram(ap, c):
            return ap.rearrange("(c t p) d -> c p t d", t=NT, p=P)[c]

        def each_chunk(eng, chunk):
            chunk(0, 0, True, False)
            chunk(0, 1, False, False)
            with eng.Fori(1, PAIRS - 1) as i:
                for j in range(2):
                    chunk(i, j, False, False)
            chunk(PAIRS - 1, 0, False, False)
            chunk(PAIRS - 1, 1, False, True)

        @block.sync
        def _(sp):
            with guarded(sp):
                sp.dma_start(x[:, 0], chunk_dram(x_in, 0)).then_inc(x_loaded[0], 16)
                sp.dma_start(ident[:], ident_dram).then_inc(const_in, 16)
                sp.dma_start(scl[:], s_cols).then_inc(const_in, 16)
                sp.dma_start(s3[:], s3_row).then_inc(const_in, 16)
                if not split:
                    sp.dma_start(x[:, 1], chunk_dram(x_in, 1)).then_inc(x_loaded[1], 16)
                if not split:
                    for n, dst in enumerate(to):
                        sp.dma_start(dst, pieces[n]).then_inc(w_in, 16)
                else:
                    for n in range(len(to)):
                        if n >= 4:
                            sp.wait_ge(rounded, PRIMED + n - 1)
                        sp.dma_start(stage[n], pieces[n]).then_inc(stage_sem(n)[0], 16)
                        if n == 3:
                            sp.dma_start(x[:, 1], chunk_dram(x_in, 1)).then_inc(x_loaded[1], 16)

                def store(i, j):
                    c = 2 * i + j
                    sp.wait_ge(o_ready, PRIMED + NT * (c + 1))
                    sp.dma_start(chunk_dram(out, c), o[:, j]).then_inc(o_out[j], 16)

                with sp.Fori(0, PAIRS - 1) as i:
                    for j in range(2):
                        sp.wait_ge(z_done, PRIMED + NT * (2 * i + j + 1))
                        sp.dma_start(x[:, j], chunk_dram(x_in, 2 * i + j + 2)).then_inc(x_loaded[j], 16)
                        store(i, j)
                for j in range(2):
                    store(PAIRS - 1, j)
                for j in range(2):
                    sp.wait_ge(o_out[j], PRIMED + 16 * PAIRS)

        @block.tensor
        def _(pe):
            def product(ps, w, rhs, k, K):
                for q in range(parts):
                    last = nc.tensor.matmul(ps, w, rhs[q][:, k, :], start=(k == 0 and q == 0),
                                            stop=(k == K - 1 and q == parts - 1))
                return last

            def transposes(i, j):
                pe.wait_ge(x_loaded[j], PRIMED + 16 * (i + 1))
                for k in range(KD):
                    for n in range(NT):
                        last = nc.tensor.transpose(psT[k][:, n * P:(n + 1) * P], x[:, j, n, k * P:(k + 1) * P], ident[:])
                    last.then_inc(xT_ps, 1)

            def weights_there(n):
                if split:
                    pe.wait_ge(rounded, PRIMED + upto[n])
                elif n == 0:
                    pe.wait_ge(w_in, PRIMED + 16 * len(to))

            def chunk(i, j, first, last_one):
                c = 2 * i + j
                if first:
                    pe.wait_ge(const_in, PRIMED + N_CONST)
                    transposes(i, j)
                    weights_there(1 if split else 0)
                pe.wait_ge(xT_done, PRIMED + KD * (c + 1))
                for m in range(KF):
                    if m < 2:
                        pe.wait_ge(gelu_done[1], PRIMED + KF * c)
                    elif m == 2:
                        pe.wait_ge(y_used, PRIMED + NT * c)
                    else:
                        pe.wait_ge(g_done, PRIMED + KF * c + m - 2)
                    cols = slice(m * P, (m + 1) * P)
                    for k in range(KD):
                        product(up[m % 3][0][:], w1_sb[:, k, cols], xT, k, KD)
                    for k in range(KD):
                        last = product(up[m % 3][1][:], w2_sb[:, k, cols], xT, k, KD)
                    last.then_inc(up_ps, 1)
                for layer, w in enumerate((h1_sb, h2_sb)):
                    src = (ha, hb)[layer]
                    if first:
                        weights_there(2 + layer)
                    for m in range(KF):
                        if layer == 0 and m < 4:
                            pe.wait_ge(g_done, PRIMED + KF * c + KF - 1 + m // 2)
                        elif layer == 1 and m < 4:
                            pe.wait_ge(gelu_done[0], PRIMED + KF * c + m + 5)
                        else:
                            pe.wait_ge(gelu_done[layer], PRIMED + KF * c + m - 3)
                        for k in range(KF):
                            if m == 0 and layer == 0:
                                pe.wait_ge(h0_done if split else g_done, PRIMED + KF * c + k + 1)
                            if m == 0 and layer == 1:
                                pe.wait_ge((split_done if split else gelu_done)[0], PRIMED + KF * c + k + 1)
                            last = product(mm[m % 4][:], w[:, k, m * P:(m + 1) * P], src, k, KF)
                        last.then_inc(hid_ps[layer], 1)
                        if layer == 1 and m == KF // 2 and not last_one:
                            transposes(i + j, 1 - j)
                if first:
                    weights_there(4)
                for n in range(NT):
                    if n < 2:
                        pe.wait_ge(y_used, PRIMED + NT * c)
                    else:
                        pe.wait_ge(y_used, PRIMED + NT * c + n - 1)
                    for k in range(KF):
                        if n == 0:
                            pe.wait_ge((split_done if split else gelu_done)[1], PRIMED + KF * c + k + 1)
                        for q in range(parts):
                            last = nc.tensor.matmul(psY[n % 2], ha[q][:, k, n * P:(n + 1) * P], w3_sb[:, k, :],
                                                    start=(k == 0 and q == 0), stop=(k == KF - 1 and q == parts - 1))
                    last.then_inc(y_ps, 1)

            with guarded(pe):
                each_chunk(pe, chunk)

        if split:
            @block.gpsimd
            def _(pool):
                def chunk(i, j, first, last):
                    c = 2 * i + j
                    for m in range(KF):
                        pool.wait_ge(hi_done, PRIMED + KF * c + m + 1)
                        nc.gpsimd.tensor_tensor(ha[1][:, m], g[:, m % 2], ha[0][:, m], ALU.subtract).then_inc(h0_done, 1)

                with guarded(pool):
                    each_chunk(pool, chunk)

        @block.scalar
        def _(act):
            def round_pieces(n0, n1):
                for n in range(n0, n1):
                    act.wait_ge(stage_sem(n)[0], PRIMED + 16 * stage_sem(n)[1])
                    nc.scalar.activation(to[n], stage[n], ACT.Copy).then_inc(rounded, 1)

            def chunk(i, j, first, last):
                c = 2 * i + j

                def high(m):
                    act.wait_ge(g_done, PRIMED + KF * c + m + 1)
                    if m == 0:
                        act.wait_ge(y_ps, PRIMED + NT * c)
                    nc.scalar.activation(ha[0][:, m], g[:, m % 2], ACT.Copy).then_inc(hi_done, 1)

                if first and split:
                    round_pieces(0, upto[1])
                for m in range(KF):
                    act.wait_ge(up_ps, PRIMED + KF * c + m + 1)
                    if m >= 2:
                        act.wait_ge(a_done, PRIMED + KF * c + m - 1)
                    nc.scalar.activation(t[:, m % 2], up[m % 3][0][:], ACT.Tanh,
                                         scale=half[:, 0, m:m + 1]).then_inc(t_ready, 1)
                    if split and m:
                        high(m - 1)
                    if first and split:
                        round_pieces(upto[1] + m, upto[1] + m + 1)
                if split:
                    high(KF - 1)
                for layer in range(2):
                    dst = (hb, ha)[layer]
                    for m in range(KF):
                        act.wait_ge(hid_ps[layer], PRIMED + KF * c + m + 1)
                        if split:
                            if m >= 2:
                                act.wait_ge(split_done[layer], PRIMED + KF * c + m - 1)
                            elif layer == 1:
                                act.wait_ge(split_done[0], PRIMED + KF * c + KF - 1 + m)
                            else:
                                act.wait_ge(h0_done, PRIMED + KF * c + KF - 1 + m)
                            out_m = g[:, m % 2]
                        else:
                            out_m = dst[0][:, m, :]
                        nc.scalar.activation(out_m, mm[m % 4][:], ACT.Gelu,
                                             scale=scl[:, 2 + layer, m:m + 1]).then_inc(gelu_done[layer], 1)
                        if first and split and layer == 0:
                            round_pieces(upto[2] + m, upto[2] + m + 1)
                if first and split:
                    round_pieces(upto[3], upto[4])

            with guarded(act):
                act.wait_ge(half_done, PRIMED + 2)
                each_chunk(act, chunk)

        @block.vector
        def _(dve):
            links = [0]

            def normalise(c, j, i):
                links[0] = 0

                def link(ins):
                    links[0] += 1
                    ins.then_inc(chain, 1)
                    dve.wait_ge(chain, PRIMED + (1 + RSQRT_LINKS) * c + links[0])

                dve.wait_ge(mv_done, PRIMED + NT * c + NT)
                link(nc.vector.tensor_copy(var[:], mv[:, :, 1]))
                rsqrt(nc, link, rstd[:], var[:], tmp[:], shifted[:])
                dve.wait_ge(o_out[j], PRIMED + 16 * i)
                for n in range(NT):
                    nc.vector.tensor_scalar(o[:, j, n], z[:, n], mv[:, n, 0:1], rstd[:, n:n + 1], ALU.subtract,
                                            ALU.mult).then_inc(o_ready, 1)

            def transposed(c, k):
                dve.wait_ge(xT_ps, PRIMED + KD * c + k + 1)
                nc.vector.tensor_copy(xT[0][:, k], psT[k][:]).then_inc(xT_hi_done if split else xT_done, 1)
                if split:
                    dve.wait_ge(xT_hi_done, PRIMED + KD * c + k + 1)
                    nc.vector.tensor_tensor(xT[1][:, k], psT[k][:], xT[0][:, k], ALU.subtract).then_inc(xT_done, 1)

            def chunk(i, j, first, last):
                c = 2 * i + j
                if first:
                    for k in range(KD):
                        transposed(c, k)
                for m in range(KF):
                    p = m % 2
                    dve.wait_ge(t_ready, PRIMED + KF * c + m + 1)
                    nc.vector.scalar_tensor_tensor(a[:, p], t[:, p], 1.0, up[m % 3][0][:], ALU.add, ALU.mult).then_inc(a_done, 1)
                    dve.wait_ge(a_done, PRIMED + KF * c + m + 1)
                    if split:
                        if m >= 2:
                            dve.wait_ge(h0_done, PRIMED + KF * c + m - 1)
                        elif not first:
                            dve.wait_ge(split_done[1], PRIMED + KF * c - 1 + m)
                        nc.vector.scalar_tensor_tensor(g[:, p], up[m % 3][1][:], half[:, 1, m:m + 1], a[:, p],
                                                       ALU.mult, ALU.mult).then_inc(g_done, 1)
                        continue
                    if m == 0:
                        dve.wait_ge(y_ps, PRIMED + NT * c)
                    nc.vector.scalar_tensor_tensor(ha[0][:, m], up[m % 3][1][:], half[:, 1, m:m + 1], a[:, p],
                                                   ALU.mult, ALU.mult).then_inc(g_done, 1)
                for layer in range(2):
                    dst = (hb, ha)[layer]
                    for m in range(KF):
                        if split:
                            dve.wait_ge(gelu_done[layer], PRIMED + KF * c + m + 1)
                            if layer == 1 and m == 0:
                                dve.wait_ge(hid_ps[0], PRIMED + KF * (c + 1))
                            n_split = (2 * c + layer) * KF + m + 1
                            nc.vector.tensor_copy(dst[0][:, m], g[:, m % 2]).then_inc(hid_hi, 1)
                            dve.wait_ge(hid_hi, PRIMED + n_split)
                            nc.vector.tensor_tensor(dst[1][:, m], g[:, m % 2], dst[0][:, m],
                                                    ALU.subtract).then_inc(split_done[layer], 1)
                        if layer == 0 and m == 1 and not first:
                            normalise(c - 1, 1 - j, i + j - 1)
                        if layer == 1 and m >= KF - KD and not last:
                            transposed(c + 1, m - KF + KD)
                for n in range(NT):
                    p = n % 2
                    dve.wait_ge(y_ps, PRIMED + NT * c + n + 1)
                    if n == 0:
                        dve.wait_ge(o_ready, PRIMED + NT * c)
                    nc.vector.tensor_tensor(z[:, n], psY[p], s3[:], ALU.mult).then_inc(y_used, 1)
                    dve.wait_ge(y_used, PRIMED + NT * c + n + 1)
                    nc.vector.tensor_tensor(z[:, n], z[:, n], x[:, j, n, :], ALU.add).then_inc(z_done, 1)
                    dve.wait_ge(z_done, PRIMED + NT * c + n + 1)
                    nc.vector.bn_stats(st[:, n], z[:, n]).then_inc(st_done, 1)
                    dve.wait_ge(half_done, PRIMED + 2)
                    dve.wait_ge(st_done, PRIMED + NT * c + n + 1)
                    nc.vector.bn_aggr(mv[:, n], st[:, n]).then_inc(mv_done, 1)
                if last:
                    normalise(c, j, i)

            with guarded(dve):
                dve.wait_ge(const_in, PRIMED + N_CONST)
                nc.vector.tensor_scalar(half[:, 0], scl[:, 0], 0.5, None, ALU.mult).then_inc(half_done, 1)
                dve.wait_ge(half_done, PRIMED + 1)
                nc.vector.tensor_tensor(half[:, 1], half[:, 0], scl[:, 1], ALU.mult).then_inc(half_done, 1)
                dve.wait_ge(half_done, PRIMED + 2)
                each_chunk(dve, chunk)


def attend_and_route_phase(nc, x_in, xT_in, wqT, wkT, wvT, wo, w_router, b_router, consts, route, x1_out, slots,
                           batches, capacity, units, starts_dram, results, first_expert, expert_weights):
    T, D = x_in.shape
    KD = D // P
    SEQ = T // batches
    NT = SEQ // P
    HALF = SEQ // 2
    E = w_router.shape[2]
    GROUP = 4
    groups = [[(n, min(n + GROUP, i + 1)) for n in range(0, i + 1, GROUP)] for i in range(NT)]
    first_group = [sum(len(g) for g in groups[:i]) for i in range(NT + 1)]
    NG = first_group[NT]
    ROWS_AT = {2: 1, 3: 3}
    LATE_ROWS_AT = {1: 0, 2: 2}
    LOGITS_AT, COUNTS_AT = 4, 5
    SCALE = float(D) ** -0.5
    with ExitStack() as ctx:
        def sb(n, s, d=F32):
            return ctx.enter_context(nc.sbuf_tensor("a" + n, s, d))

        def psum(n, s):
            return ctx.enter_context(nc.psum_tensor("a" + n, s, F32))

        primed = []
        ctx.callback(nc.clear_and_free_semaphores, primed)

        def sem(n):
            primed.append(nc.alloc_semaphore("a" + n))
            return primed[-1]

        ident, ident_bf, mask_bf, before_me, all_ones = (sb(n, [P, P], d) for n, d in (
            ("ident", F32), ("ident_bf", BF16), ("mask_bf", BF16), ("before_me", F32), ("all_ones", F32)))
        starts = sb("starts", [P, T // UNIT])
        begun = sb("begun", [P, E, T // UNIT])
        taken = sb("taken", [P, E])
        before = sb("before", [P, E + 2])
        first_row = sb("first_row", [P, E])
        count_i = sb("count_i", [1, E], I32)
        zeros = sb("zeros", [P, UNIT // P, D])
        by_expert = sb("by_expert", [P, T // P, E])
        row_f = sb("row_f", [P, T // P])
        iota_e = sb("iota_e", [P, E])
        br = sb("br", [P, E])
        wr = sb("wr", [P, KD, E])
        raw = [sb(f"raw{n}", [P, KD, D]) for n in range(4)]
        score_hi, score_lo, value_hi, value_lo = (sb(n, [P, KD, D], F32R) for n in ("sc_hi", "sc_lo", "va_hi", "va_lo"))
        xs = sb("xs", [P, KD, SEQ])
        xT_hi, xT_lo, qT_hi, qT_lo = (sb(n, [P, KD, SEQ], F32R) for n in ("xT_hi", "xT_lo", "qT_hi", "qT_lo"))
        v_hi, v_lo = (sb(n, [P, NT, D], F32R) for n in ("v_hi", "v_lo"))
        xin = sb("xin", [P, NT, D])
        prob = sb("prob", [P, 2, SEQ])
        pT_hi, pT_lo = (sb(n, [P, 4, GROUP, P], F32R) for n in ("pT_hi", "pT_lo"))
        nmax, rowsum, recip, var, rstd, tmp = (sb(n, [P, NT]) for n in ("nmax", "rowsum", "recip", "var", "rstd", "tmp"))
        shifted = sb("shifted", [P, NT], I32)
        z = sb("z", [P, NT, D])
        st = sb("st", [P, NT, 6])
        mv = sb("mv", [P, NT, 2])
        xn = sb("xn", [P, NT, D])
        x1T = sb("x1T", [P, KD, SEQ])
        lg, top, both, pos, prod = (sb(n, [P, NT, E]) for n in ("lg", "top", "both", "pos", "prod"))
        top_i = sb("top_i", [P, NT, E], U32)
        top_f = sb("top_f", [P, NT, 2])
        oh = [sb(f"oh{c}", [P, NT, E]) for c in range(2)]
        cum = sb("cum", [P, NT + 1, E])
        gap = sb("gap", [P, NT])
        egap = sb("egap", [P, NT])
        slot_f = sb("slot_f", [P, NT])
        slot_i = [sb(f"slot_i{c}", [P, NT], I32) for c in range(2)]
        S = [psum(f"S{n}", [P, SEQ]) for n in range(2)]
        PT = psum("PT", [P, 2, GROUP, P])
        O = psum("O", [P, D])
        misc = psum("misc", [P, 512])
        PTf = PT[:].rearrange("p a b c -> p (a b c)")

        names = ("const_in xs_in xin_in ab_ps ab_hi ab_lo x_hi x_lo q_ps q_hi q_lo v_ps v_hi v_lo s_ps mx ex pt_ps pt_hi "
                 "pt_lo o_ps z_done chain ln_chain xn_done xn_rest_done t_ps t_ev lg_ps both_done px_ps gap_done e_done slot_done sc_out scattered x1_st "
                 "st_done recip_done top_done mv_done zeros_done counted zeros_out "
                 "unreached_out step first_in first_hi first_lo").split()
        (const_in, xs_in, xin_in, ab_ps, ab_hi, ab_lo, x_hi, x_lo, q_ps, q_hi, q_lo, v_ps, v_hi_done, v_lo_done, s_ps, mx,
         ex, pt_ps, pt_hi, pt_lo, o_ps, z_done, chain, ln_chain, xn_done, xn_rest_done, t_ps, t_ev, lg_ps, both_done, px_ps, gap_done, e_done,
         slot_done, sc_out, scattered, x1_st, st_done, recip_done, top_done, mv_done, zeros_done, counted,
         zeros_out, unreached_out, step, first_in, first_hi, first_lo) = (sem(n) for n in names)
        unwatched = {n.engine: sem(f"unwatched{q}") for q, n in
                     enumerate((nc.sync, nc.gpsimd, nc.tensor, nc.scalar, nc.vector))}
        loads = [(ident[:], consts["ident"]), (z[:, 0, :P], consts["mask"]),
                 (before_me[:], consts["before_me"]), (all_ones[:], consts["all_ones"]), (iota_e[:], consts["iota_e"]),
                 (br[:], b_router), (wr[:], w_router),
                 (starts[:], starts_dram)]
        raws = list(zip(raw, (wqT, wkT, wvT, wo)))
        N_CONST = 16 * (len(loads) + len(raws))

        by_gpsimd = [sc_out]
        prime(nc, [s for s in primed if s not in by_gpsimd and s not in unwatched.values()])
        block = ctx.enter_context(nc.Block())

        def wait_alone(eng, semaphore, value):
            eng.wait_ge(semaphore, value)
            eng.sem_inc(unwatched[eng.engine], 1)

        def tokens(ap, b):
            return ap.rearrange("(b t p) d -> b p t d", t=NT, p=P)[b]

        HALF_ROWS = NT // 2
        SURE_UNITS = 2 * T // UNIT
        TRANSPOSES = NT // 2

        def each_sequence(eng, attention, tail):
            attention(0, False, True)
            with eng.Fori(1, batches - 1) as b:
                attention(b, True, True)
            attention(batches - 1, True, False)
            tail(batches - 1)

        @block.sync
        def _(sp):
            for d, s in raws[:2]:
                sp.dma_start(d[:], s).then_inc(const_in, 16)
            sp.dma_start(xs[:], xT_in[0]).then_inc(xs_in, 16)
            for d, s in raws[2:]:
                sp.dma_start(d[:], s).then_inc(const_in, 16)
            for d, s in loads:
                sp.dma_start(d, s).then_inc(const_in, 16)
            sp.dma_start(xin[:], tokens(x_in, 0)).then_inc(xin_in, 16)
            sp.wait_ge(const_in, PRIMED + N_CONST)

            def attention(b, earlier, later):
                if not earlier:
                    sp.wait_ge(zeros_done, PRIMED + 1)
                    for n in range(SURE_UNITS + 1, results.shape[0] // UNIT):
                        sp.dma_start(results[n * UNIT:(n + 1) * UNIT, :].rearrange("(n p) d -> p n d", p=P), zeros[:]
                                     ).then_inc(unreached_out, 16)
                    sp.dma_start(first_expert[0][:], expert_weights[0]).then_inc(first_in, 16)
                if earlier:
                    sp.wait_ge(x_lo, PRIMED + b)
                    sp.dma_start(xs[:], xT_in[b]).then_inc(xs_in, 16)
                    sp.wait_ge(z_done, PRIMED + NT * b)
                    sp.dma_start(xin[:], tokens(x_in, b)).then_inc(xin_in, 16)
                if earlier:
                    tail(b - 1, xn)

            def tail(b, rows=xin):
                sp.wait_ge(xn_done, PRIMED + b + 1)
                sp.wait_ge(xn_rest_done, PRIMED + b + 1)
                sp.dma_start(tokens(x1_out, b), rows[:]).then_inc(x1_st, 16)

            each_sequence(sp, attention, tail)
            sp.wait_ge(counted, PRIMED + 1)
            for e in range(E):
                n = sp.value_load(count_i[0:1, e:e + 1], min_val=0, max_val=T)
                sp.dma_start(slots[bass.ds(e * capacity + n, UNIT), :].rearrange("(n p) d -> p n d", p=P), zeros[:]
                             ).then_inc(zeros_out, 16)
            sp.wait_ge(zeros_out, PRIMED + 16 * E)
            sp.wait_ge(unreached_out, PRIMED + 16 * (results.shape[0] // UNIT - SURE_UNITS - 1))
            sp.wait_ge(x1_st, PRIMED + 16 * batches)

        @block.gpsimd
        def _(pool):
            def tail(b, rows=xin, rest=False):
                if rest:
                    wait_alone(pool, x1_st, PRIMED + 16 * b)
                    wait_alone(pool, mv_done, PRIMED + (2 + RSQRT_LINKS) * (b + 1))
                    for i in range(HALF_ROWS, NT):
                        ins = nc.gpsimd.tensor_scalar(xn[:, i], z[:, i], mv[:, i, 0:1], rstd[:, i:i + 1], ALU.subtract, ALU.mult)
                    ins.then_inc(xn_rest_done, 1)
                wait_alone(pool, slot_done, PRIMED + 2 * b + 2)
                for c in range(2):
                    for t in range(NT):
                        pool.indirect_dma_start(
                            out=slots, out_offset=bass.IndirectOffsetOnAxis(ap=slot_i[c][:, t:t + 1], axis=0),
                            in_=rows[:, t, :], in_offset=None).then_inc(sc_out, 16)
                pool.wait_ge(sc_out, 16 * 2 * NT * (b + 1))
                pool.sem_inc(scattered, 1)

            nc.gpsimd.memset(zeros[:], 0.0).then_inc(zeros_done, 1)
            each_sequence(pool, lambda b, earlier, later: tail(b - 1, xn, True) if earlier else None, tail)

        @block.tensor
        def _(pe):
            def three(ps, left, right, first, last):
                (lh, ll), (rh, rl) = left, right
                nc.tensor.matmul(ps, lh, rh, start=first, stop=False)
                nc.tensor.matmul(ps, lh, rl, start=False, stop=False)
                return nc.tensor.matmul(ps, ll, rh, start=False, stop=last)

            pe.wait_ge(const_in, PRIMED + N_CONST)
            for pair in range(2):
                if pair:
                    pe.wait_ge(ab_lo, PRIMED + 1)
                for m in range(KD):
                    for k in range(KD):
                        last = nc.tensor.matmul(misc[:, m * D:(m + 1) * D], raw[2 * pair][:, k, m * P:(m + 1) * P],
                                                raw[2 * pair + 1][:, k, :], start=(k == 0), stop=(k == KD - 1))
                last.then_inc(ab_ps, 1)
            pe.wait_ge(ab_lo, PRIMED + 2)

            def scores(b, i):
                s = S[i % 2]
                if i == 0:
                    pe.wait_ge(v_lo_done, PRIMED + 2 * b + 2)
                    pe.wait_ge(q_lo, PRIMED + 2 * b + 2)
                elif i >= 2:
                    pe.wait_ge(ex, PRIMED + NT * b + i - 1)
                width = (i + 1) * P
                for c0 in range(0, width, HALF):
                    c1 = min(width, c0 + HALF)
                    for k in range(KD):
                        three(s[:, c0:c1], (qT_hi[:, k, i * P:(i + 1) * P], qT_lo[:, k, i * P:(i + 1) * P]),
                              (xT_hi[:, k, c0:c1], xT_lo[:, k, c0:c1]), k == 0, k == KD - 1)
                    if c1 == width:
                        last = nc.tensor.matmul(s[:, i * P:width], ident_bf[:], mask_bf[:], start=False, stop=True,
                                                skip_group_check=True)
                last.then_inc(s_ps, 1)

            def transpose_probs(b, i):
                pe.wait_ge(ex, PRIMED + NT * b + i + 1)
                for g, (n0, n1) in enumerate(groups[i]):
                    g += first_group[i]
                    if g >= 2:
                        pe.wait_ge(pt_lo, PRIMED + NG * b + g - 1)
                    for n in range(n0, n1):
                        last = nc.tensor.transpose(PT[:, g % 2, n - n0, :], prob[:, i % 2, n * P:(n + 1) * P], ident[:])
                    last.then_inc(pt_ps, 1)

            def weigh(b, i):
                pe.wait_ge(z_done, PRIMED + NT * b + i)
                for g, (n0, n1) in enumerate(groups[i]):
                    g += first_group[i]
                    pe.wait_ge(pt_lo, PRIMED + NG * b + g + 1)
                    for n in range(n0, n1):
                        last = three(O[:], (pT_hi[:, g % 4, n - n0, :], pT_lo[:, g % 4, n - n0, :]),
                                     (v_hi[:, n, :], v_lo[:, n, :]), n == 0, n == i)
                last.then_inc(o_ps, 1)

            def transpose_rows(b, j, rows=xn):
                if j == 0:
                    pe.wait_ge(xn_done, PRIMED + b + 1)
                    pe.wait_ge(slot_done, PRIMED + 2 * b)
                else:
                    pe.wait_ge(t_ev, PRIMED + TRANSPOSES * b + j)
                if 2 * j == HALF_ROWS:
                    pe.wait_ge(xn_rest_done, PRIMED + b + 1)
                for k in range(KD):
                    for n in range(2):
                        last = nc.tensor.transpose(misc[:, (2 * k + n) * P:(2 * k + n + 1) * P],
                                                   rows[:, 2 * j + n, k * P:(k + 1) * P], ident[:])
                last.then_inc(t_ps, 1)

            def logits(b):
                pe.wait_ge(t_ev, PRIMED + TRANSPOSES * (b + 1))
                for t in range(NT):
                    for k in range(KD):
                        last = nc.tensor.matmul(misc[:, t * E:(t + 1) * E], x1T[:, k, t * P:(t + 1) * P], wr[:, k, :],
                                                start=(k == 0), stop=(k == KD - 1))
                last.then_inc(lg_ps, 1)

            def counts(b):
                pe.wait_ge(both_done, PRIMED + b + 1)
                flat = both[:].rearrange("p t e -> p (t e)")
                nc.tensor.matmul(misc[:, NT * E:2 * NT * E], before_me[:], flat, start=True, stop=True)
                nc.tensor.matmul(misc[:, 2 * NT * E:3 * NT * E], all_ones[:], flat, start=True, stop=True).then_inc(px_ps, 1)

            def attention(b, earlier, later):
                pe.wait_ge(x_lo, PRIMED + b + 1)
                pe.wait_ge(ex, PRIMED + NT * b)
                for m in range(KD):
                    for c in range(2):
                        cs = slice(c * HALF, (c + 1) * HALF)
                        for k in range(KD):
                            last = three(S[m][:, cs], (score_hi[:, k, m * P:(m + 1) * P], score_lo[:, k, m * P:(m + 1) * P]),
                                         (xT_hi[:, k, cs], xT_lo[:, k, cs]), k == 0, k == KD - 1)
                    last.then_inc(q_ps, 1)
                for half in range(2):
                    dst = (PTf, S[0][:])[half]
                    if half == 0:
                        pe.wait_ge(pt_lo, PRIMED + NG * b)
                    else:
                        pe.wait_ge(q_lo, PRIMED + 2 * b + 1)
                    for n in range(NT // 2):
                        t = half * NT // 2 + n
                        for k in range(KD):
                            last = three(dst[:, n * D:(n + 1) * D],
                                         (xT_hi[:, k, t * P:(t + 1) * P], xT_lo[:, k, t * P:(t + 1) * P]),
                                         (value_hi[:, k, :], value_lo[:, k, :]), k == 0, k == KD - 1)
                    last.then_inc(v_ps, 1)
                scores(b, 0)
                for i in range(NT):
                    if i + 1 < NT:
                        scores(b, i + 1)
                    if earlier and i in ROWS_AT:
                        transpose_rows(b - 1, ROWS_AT[i])
                    if earlier and i == COUNTS_AT:
                        counts(b - 1)
                    transpose_probs(b, i)
                    if earlier and i in LATE_ROWS_AT:
                        transpose_rows(b - 1, LATE_ROWS_AT[i])
                    if i:
                        weigh(b, i - 1)
                    if earlier and i == LOGITS_AT:
                        logits(b - 1)
                weigh(b, NT - 1)

            def tail(b):
                for j in range(TRANSPOSES):
                    transpose_rows(b, j, xin)
                logits(b)
                counts(b)

            each_sequence(pe, attention, tail)

        @block.scalar
        def _(act):
            for pair, hi in enumerate((score_hi, value_hi)):
                act.wait_ge(ab_ps, PRIMED + pair + 1)
                nc.scalar.activation(hi[:].rearrange("p k d -> p (k d)"), misc[:], ACT.Copy,
                                     scale=SCALE if pair == 0 else 1.0).then_inc(ab_hi, 1)

            def rows_out(b, j):
                act.wait_ge(t_ps, PRIMED + TRANSPOSES * b + j + 1)
                nc.scalar.activation(x1T[:, :, 2 * j * P:(2 * j + 2) * P], misc[:].rearrange("p (k t) -> p k t", k=KD),
                                     ACT.Copy).then_inc(t_ev, 1)

            def weights(b):
                act.wait_ge(gap_done, PRIMED + b + 1)
                nc.scalar.activation(egap[:], gap[:], ACT.Exp).then_inc(e_done, 1)

            def x_high(b):
                act.wait_ge(xs_in, PRIMED + 16 * b + 16)
                act.wait_ge(s_ps, PRIMED + NT * b)
                nc.scalar.activation(xT_hi[:], xs[:], ACT.Copy).then_inc(x_hi, 1)

            def attention(b, earlier, later):
                for m in range(KD):
                    act.wait_ge(q_ps, PRIMED + 2 * b + m + 1)
                    nc.scalar.activation(qT_hi[:, m, :], S[m][:], ACT.Copy).then_inc(q_hi, 1)
                for half in range(2):
                    src = (PTf, S[0][:])[half]
                    act.wait_ge(v_ps, PRIMED + 2 * b + half + 1)
                    nc.scalar.activation(v_hi[:, half * NT // 2:(half + 1) * NT // 2, :].rearrange("p t d -> p (t d)"), src,
                                         ACT.Copy).then_inc(v_hi_done, 1)

                def exp(i):
                    act.wait_ge(mx, PRIMED + NT * b + i + 1)
                    if i >= 2:
                        act.wait_ge(pt_ps, PRIMED + NG * b + first_group[i - 1])
                    width = (i + 1) * P
                    nc.scalar.activation(prob[:, i % 2, :width], S[i % 2][:, :width], ACT.Exp, bias=nmax[:, i:i + 1],
                                         accum_out=rowsum[:, i:i + 1]).then_inc(ex, 1)

                exp(0)
                for i in range(NT):
                    if i + 1 < NT:
                        exp(i + 1)
                    if earlier and i in ROWS_AT:
                        rows_out(b - 1, ROWS_AT[i])
                    for g, (n0, n1) in enumerate(groups[i]):
                        g += first_group[i]
                        act.wait_ge(pt_ps, PRIMED + NG * b + g + 1)
                        if i >= 2:
                            act.wait_ge(o_ps, PRIMED + NT * b + i - 1)
                        nc.scalar.activation(pT_hi[:, g % 4, :n1 - n0, :], PT[:, g % 2, :n1 - n0, :],
                                             ACT.Copy).then_inc(pt_hi, 1)
                    if earlier and i in LATE_ROWS_AT:
                        rows_out(b - 1, LATE_ROWS_AT[i])
                    if earlier and i == COUNTS_AT:
                        weights(b - 1)
                if later:
                    x_high(b + 1)

            def tail(b):
                for j in range(TRANSPOSES):
                    rows_out(b, j)
                weights(b)

            x_high(0)
            each_sequence(act, attention, tail)
            act.wait_ge(first_in, PRIMED + 16)
            nc.scalar.activation(first_expert[1][:], first_expert[0][:], ACT.Copy).then_inc(first_hi, 1)

        @block.vector
        def _(dve):
            LINKS = 1 + 1 + 1 + 1 + 2 + 1 + NT + 1 + 2 * 4 + 1
            dve.wait_ge(const_in, PRIMED + N_CONST)
            nc.vector.tensor_copy(ident_bf[:], ident[:])
            nc.vector.tensor_copy(mask_bf[:], z[:, 0, :P])
            for pair, (hi, lo) in enumerate(((score_hi, score_lo), (value_hi, value_lo))):
                dve.wait_ge(ab_hi, PRIMED + pair + 1)
                nc.vector.scalar_tensor_tensor(lo[:].rearrange("p k d -> p (k d)"), misc[:], SCALE if pair == 0 else 1.0,
                                               hi[:].rearrange("p k d -> p (k d)"), ALU.mult, ALU.subtract).then_inc(ab_lo, 1)
            nc.vector.memset(cum[:, NT, :], 0.0).then_inc(chain, 1)

            def make_tail(b):
                n_link = [0]

                def link(ins, alone=False):
                    n_link[0] += 1
                    ins.then_inc(chain, 1)
                    (wait_alone if alone else lambda e, s, v: e.wait_ge(s, v))(dve, chain, PRIMED + LINKS * b + n_link[0] + 1)

                def choose():
                    wait_alone(dve, lg_ps, PRIMED + b + 1)
                    link(nc.vector.tensor_tensor(lg[:], misc[:, :NT * E].rearrange("p (t e) -> p t e", e=E),
                                                 br[:].unsqueeze(1).to_broadcast([P, NT, E]), ALU.add), alone=True)
                    for t in range(NT):
                        ins = nc.vector.max(top[:, t], lg[:, t])
                    link(ins, alone=True)
                    for t in range(NT):
                        ins = nc.vector.max_index(top_i[:, t], top[:, t], lg[:, t])
                    link(ins)
                    nc.vector.tensor_tensor(gap[:], top[:, :, 1], top[:, :, 0], ALU.subtract).then_inc(gap_done, 1)
                    link(nc.vector.tensor_copy(top_f[:], top_i[:, :, 0:2]))
                    for c in range(2):
                        ins = nc.vector.tensor_tensor(oh[c][:], iota_e[:].unsqueeze(1).to_broadcast([P, NT, E]),
                                                      top_f[:, :, c:c + 1].to_broadcast([P, NT, E]), ALU.is_equal)
                    ins.then_inc(top_done, 1)
                    dve.wait_ge(top_done, PRIMED + b + 1)
                    nc.vector.tensor_tensor(both[:], oh[0][:], oh[1][:], ALU.add).then_inc(both_done, 1)

                def weigh():
                    dve.wait_ge(e_done, PRIMED + b + 1)
                    link(nc.vector.tensor_scalar(gap[:], egap[:], 1.0, None, ALU.add))
                    w0 = route["weight"][0][:, bass.ds(b * NT, NT)]
                    w1 = route["weight"][1][:, bass.ds(b * NT, NT)]
                    link(nc.vector.reciprocal(w0, gap[:]))
                    nc.vector.tensor_tensor(w1, egap[:], w0, ALU.mult)

                def count():
                    dve.wait_ge(px_ps, PRIMED + b + 1)
                    link(nc.vector.tensor_copy(cum[:, 0, :], cum[:, NT, :]))
                    for t in range(NT):
                        link(nc.vector.tensor_tensor(cum[:, t + 1, :], misc[:, (2 * NT + t) * E:(2 * NT + t + 1) * E],
                                                     cum[:, t, :], ALU.add))
                    link(nc.vector.tensor_tensor(pos[:], misc[:, NT * E:2 * NT * E].rearrange("p (t e) -> p t e", e=E),
                                                 cum[:, :NT, :], ALU.add))

                def place():
                    dve.wait_ge(scattered, PRIMED + b)
                    for c in range(2):
                        rank = route["rank"][c][:, bass.ds(b * NT, NT)]
                        keep = route["onehot"][c][:, bass.ds(b * NT, NT), :]
                        nc.vector.tensor_copy(keep, oh[c][:]).then_inc(chain, 1)
                        n_link[0] += 1
                        link(nc.vector.tensor_tensor(prod[:], oh[c][:], pos[:], ALU.mult))
                        link(nc.vector.tensor_reduce(rank, prod[:], X, ALU.add))
                        link(nc.vector.scalar_tensor_tensor(slot_f[:], top_f[:, :, c], float(capacity), rank, ALU.mult,
                                                            ALU.add))
                        nc.vector.tensor_copy(slot_i[c][:], slot_f[:]).then_inc(slot_done, 1)
                    dve.wait_ge(slot_done, PRIMED + 2 * b + 2)
                    link(nc.vector.tensor_copy(route["count"][:], cum[:, NT, :]))
                    assert n_link[0] == LINKS, (n_link[0], LINKS)

                return choose, weigh, count, place

            def x_low(b):
                dve.wait_ge(x_hi, PRIMED + b + 1)
                nc.vector.tensor_tensor(xT_lo[:], xs[:], xT_hi[:], ALU.subtract).then_inc(x_lo, 1)

            def normalised(first, end, done, rows=xn):
                for i in range(first, end):
                    ins = nc.vector.tensor_scalar(rows[:, i], z[:, i], mv[:, i, 0:1], rstd[:, i:i + 1], ALU.subtract, ALU.mult)
                ins.then_inc(done, 1)

            def attention(b, earlier, later):
                if earlier:
                    choose, weigh, count, place = make_tail(b - 1)
                for m in range(KD):
                    dve.wait_ge(q_hi, PRIMED + 2 * b + m + 1)
                    nc.vector.tensor_tensor(qT_lo[:, m, :], S[m][:], qT_hi[:, m, :], ALU.subtract).then_inc(q_lo, 1)
                for half in range(2):
                    src = (PTf, S[0][:])[half]
                    rows = slice(half * NT // 2, (half + 1) * NT // 2)
                    dve.wait_ge(v_hi_done, PRIMED + 2 * b + half + 1)
                    nc.vector.tensor_tensor(v_lo[:, rows, :].rearrange("p t d -> p (t d)"), src,
                                            v_hi[:, rows, :].rearrange("p t d -> p (t d)"), ALU.subtract).then_inc(v_lo_done, 1)

                def row_max(i):
                    dve.wait_ge(s_ps, PRIMED + NT * b + i + 1)
                    nc.vector.tensor_reduce(nmax[:, i:i + 1], S[i % 2][:, :(i + 1) * P], X, ALU.max, negate=True).then_inc(mx, 1)

                def residual(i):
                    dve.wait_ge(ex, PRIMED + NT * b + i + 1)
                    nc.vector.reciprocal(recip[:, i:i + 1], rowsum[:, i:i + 1]).then_inc(recip_done, 1)
                    dve.wait_ge(o_ps, PRIMED + NT * b + i + 1)
                    dve.wait_ge(xin_in, PRIMED + 16 * b + 16)
                    if i == 0 and earlier:
                        dve.wait_ge(xn_done, PRIMED + b)
                    if i == HALF_ROWS and earlier:
                        dve.wait_ge(xn_rest_done, PRIMED + b)
                    dve.wait_ge(recip_done, PRIMED + NT * b + i + 1)
                    nc.vector.scalar_tensor_tensor(z[:, i], O[:], recip[:, i:i + 1], xin[:, i], ALU.mult,
                                                   ALU.add).then_inc(z_done, 1)
                    dve.wait_ge(z_done, PRIMED + NT * b + i + 1)
                    nc.vector.bn_stats(st[:, i], z[:, i]).then_inc(st_done, 1)

                row_max(0)
                for i in range(NT):
                    if i + 1 < NT:
                        row_max(i + 1)
                    for g, (n0, n1) in enumerate(groups[i]):
                        g += first_group[i]
                        dve.wait_ge(pt_hi, PRIMED + NG * b + g + 1)
                        nc.vector.tensor_tensor(pT_lo[:, g % 4, :n1 - n0, :], PT[:, g % 2, :n1 - n0, :],
                                                pT_hi[:, g % 4, :n1 - n0, :], ALU.subtract).then_inc(pt_lo, 1)
                    if earlier and i == 0:
                        dve.wait_ge(x1_st, PRIMED + 16 * (b - 1))
                        dve.wait_ge(scattered, PRIMED + b - 1)
                        normalised(0, HALF_ROWS, xn_done)
                    if i:
                        residual(i - 1)
                    if earlier and i == LOGITS_AT:
                        choose()
                    if earlier and i == COUNTS_AT:
                        weigh()
                        count()
                    if earlier and i == COUNTS_AT + 1:
                        place()
                if later:
                    x_low(b + 1)
                residual(NT - 1)
                if earlier:
                    dve.wait_ge(xn_rest_done, PRIMED + b)
                wait_alone(dve, st_done, PRIMED + NT * b + NT)
                for i in range(NT):
                    ins = nc.vector.bn_aggr(mv[:, i], st[:, i])

                def link(ins):
                    n_link[0] += 1
                    ins.then_inc(mv_done, 1)
                    dve.wait_ge(mv_done, PRIMED + (2 + RSQRT_LINKS) * b + n_link[0])

                n_link = [0]
                link(ins)
                link(nc.vector.tensor_copy(var[:], mv[:, :, 1]))
                rsqrt(nc, link, rstd[:], var[:], tmp[:], shifted[:])

            def tail(b):
                dve.wait_ge(z_done, PRIMED + NT * batches)
                normalised(0, HALF_ROWS, xn_done, xin)
                normalised(HALF_ROWS, NT, xn_rest_done, xin)
                for step in make_tail(b):
                    step()

            x_low(0)
            each_sequence(dve, attention, tail)
            steps = [0]

            def then(ins):
                steps[0] += 1
                ins.then_inc(step, 1)
                dve.wait_ge(step, PRIMED + steps[0])

            dve.wait_ge(chain, PRIMED + LINKS * batches + 1)
            nc.vector.tensor_copy(count_i[:], route["count"][0:1, :]).then_inc(counted, 1)
            then(nc.vector.tensor_tensor(begun[:], route["count"][:].unsqueeze(2).to_broadcast([P, E, T // UNIT]),
                                         starts[:].unsqueeze(1).to_broadcast([P, E, T // UNIT]), ALU.is_gt))
            then(nc.vector.tensor_reduce(taken[:], begun[:], X, ALU.add))
            then(nc.vector.memset(before[:], 0.0))
            for e in range(E):
                then(nc.vector.tensor_tensor(before[:, e + 2:e + 3], before[:, e + 1:e + 2], taken[:, e:e + 1], ALU.add))
            then(nc.vector.tensor_copy(units[:], before[0:1, :]))
            then(nc.vector.tensor_scalar(first_row[:], before[:, 1:E + 1], float(UNIT), float(UNIT), ALU.mult, ALU.add))
            for c in range(2):
                then(nc.vector.tensor_tensor(by_expert[:], route["onehot"][c][:],
                                             first_row[:].unsqueeze(1).to_broadcast([P, T // P, E]), ALU.mult))
                then(nc.vector.tensor_reduce(row_f[:], by_expert[:], X, ALU.add))
                then(nc.vector.tensor_tensor(row_f[:], row_f[:], route["rank"][c][:], ALU.add))
                then(nc.vector.tensor_copy(route["row"][c][:], row_f[:]))
            dve.wait_ge(first_hi, PRIMED + 1)
            nc.vector.tensor_tensor(first_expert[2][:], first_expert[0][:], first_expert[1][:],
                                    ALU.subtract).then_inc(first_lo, 1)


def moe_phase(nc, units, first_expert, slots, w_pack, b_pack, results, ident_dram, capacity, most_tokens):
    D = slots.shape[1]
    KD = D // P
    E, _, WN = w_pack.shape
    F = WN // (2 * KD)
    KF = F // P
    U = 256
    NH = U // P
    MAX_UNITS = most_tokens // U
    GROUPS = (MAX_UNITS, 8, 4, 1)
    MOST = results.shape[0] // U - 1
    with ExitStack() as ctx:
        def sb(n, s, d=F32):
            return ctx.enter_context(nc.sbuf_tensor("e" + n, s, d))

        def psum(n, s):
            return ctx.enter_context(nc.psum_tensor("e" + n, s, F32))

        primed = []
        ctx.callback(nc.clear_and_free_semaphores, primed)

        def sem(n):
            primed.append(nc.alloc_semaphore("e" + n))
            return primed[-1]

        ident = sb("ident", [P, P])
        stage = first_expert[0]
        w_hi = [first_expert[1], sb("w_hi1", [P, WN], F32R)]
        w_lo = [first_expert[2], sb("w_lo1", [P, WN], F32R)]
        bias = sb("bias", [P, 2, KF + D])
        x = sb("x", [P, NH, D])
        xT_hi = sb("xT_hi", [P, KD, U], F32R)
        xT_lo = sb("xT_lo", [P, KD, U], F32R)
        h = sb("h", [P, 4, U])
        h_hi = sb("h_hi", [P, KF, U], F32R)
        h_lo = sb("h_lo", [P, KF, U], F32R)
        y = sb("y", [P, NH, D])
        psH = [psum(f"psH{b}", [P, U]) for b in range(4)]
        psT = psum("psT", [P, KD, U])
        psY = [psum(f"psY{n}", [P, D]) for n in range(NH)]

        ident_in = sem("ident_in")
        staged = sem("staged")
        bias_in = [sem(f"bias_in{b}") for b in range(2)]
        hi_done = sem("hi_done")
        lo_done = sem("lo_done")
        x_in = sem("x_in")
        xT_ps = sem("xT_ps")
        xT_hi_done = sem("xT_hi_done")
        xT_done = sem("xT_done")
        h_ps = sem("h_ps")
        h_act = sem("h_act")
        h_hi_done = sem("h_hi_done")
        h_done = sem("h_done")
        y_ps = sem("y_ps")
        y_done = sem("y_done")
        y_out = sem("y_out")

        unwatched = {n.engine: sem(f"unwatched{q}") for q, n in
                     enumerate((nc.sync, nc.gpsimd, nc.tensor, nc.scalar, nc.vector))}

        by_gpsimd = [staged, *bias_in]
        prime(nc, [s for s in primed if s not in by_gpsimd and s not in unwatched.values()])
        block = ctx.enter_context(nc.Block())

        def w1(buf, k, m):
            return buf[:, k * F + m * P:k * F + (m + 1) * P]

        def w2(buf, k):
            return buf[:, KD * F + k * D:KD * F + (k + 1) * D]

        def wait_alone(eng, semaphore, value):
            eng.wait_ge(semaphore, value)
            eng.sem_inc(unwatched[eng.engine], 1)

        def for_units(eng, per_expert, per_unit):
            with eng.Fori(0, E // 2) as pair:
                for b in range(2):
                    e = 2 * pair + b
                    before = eng.value_load(units[0:1, bass.ds(e + 1, 1)], min_val=0, max_val=MOST)
                    upto = eng.value_load(units[0:1, bass.ds(e + 2, 1)], min_val=0, max_val=MOST)
                    per_expert(e, b, before, upto)

                    def units_from(first, sizes):
                        with eng.Fori(first, first + sizes[0], sizes[1]) as g:
                            with eng.If(g < upto):
                                if sizes[1] == 1:
                                    per_unit(e, b, g - before, g)
                                else:
                                    units_from(g, sizes[1:])

                    units_from(before, GROUPS)

        @block.sync
        def _(sp):
            sp.dma_start(ident[:], ident_dram).then_inc(ident_in, 16)
            def per_unit(e, b, t, g):
                sp.wait_ge(xT_ps, PRIMED + g)
                row = nc.s_assert_within(e * capacity + t * U, 0, E * capacity - U, skip_runtime_bounds_check_because="g stays within the units counted")
                sp.dma_start(x[:], slots[bass.ds(row, U), :].rearrange("(n p) d -> p n d", p=P)).then_inc(x_in, 16)

            for_units(sp, lambda *_: None, per_unit)
            total = sp.value_load(units[0:1, E + 1:E + 2], min_val=0, max_val=MOST)
            sp.wait_ge(xT_ps, PRIMED + total)
            sp.dma_start(x[:], slots[0:U, :].rearrange("(n p) d -> p n d", p=P)).then_inc(x_in, 16)
            wait_alone(sp, x_in, PRIMED + 16 * total + 16)

        @block.gpsimd
        def _(pool):
            pool.dma_start(bias[:, 0], b_pack[0]).then_inc(bias_in[0], 16)
            pool.dma_start(stage[:], w_pack[1]).then_inc(staged, 16)

            def prepare(e, b):
                pool.dma_start(bias[:, b], b_pack[e]).then_inc(bias_in[b], 16)
                wait_alone(pool, staged, 16 * e)
                nc.gpsimd.tensor_copy(w_hi[b][:], stage[:]).then_inc(hi_done, 1)
                pool.wait_ge(hi_done, PRIMED + e)
                nc.gpsimd.tensor_tensor(w_lo[b][:], stage[:], w_hi[b][:], ALU.subtract).then_inc(lo_done, 1)
                pool.wait_ge(lo_done, PRIMED + e)
                pool.dma_start(stage[:], w_pack[(e + 1) % E]).then_inc(staged, 16)

            prepare(1, 1)
            with pool.Fori(1, E // 2) as pair:
                for b in range(2):
                    e = 2 * pair + b
                    held = pool.value_load(units[0:1, bass.ds(e, 1)], min_val=0, max_val=MOST)
                    wait_alone(pool, y_ps, PRIMED + held)
                    pool.wait_ge(y_done, PRIMED + NH * held + 1)
                    prepare(e, b)
            pool.wait_ge(staged, 16 * E)

        @block.tensor
        def _(pe):
            def transposes():
                for k in range(KD):
                    for n in range(NH):
                        last = nc.tensor.transpose(psT[:, k, n * P:(n + 1) * P], x[:, n, k * P:(k + 1) * P], ident[:])
                last.then_inc(xT_ps, 1)

            def per_expert(e, b, before, upto):
                wait_alone(pe, lo_done, PRIMED + e)

            def per_unit(e, b, t, g):
                pe.wait_ge(xT_done, PRIMED + g + 1)
                for m in range(KF):
                    if m < 4:
                        pe.wait_ge(h_done, PRIMED + KF * g)
                    else:
                        pe.wait_ge(h_act, PRIMED + KF * g + m - 3)
                    for k in range(KD):
                        for n, (w, v) in enumerate(((w_hi, xT_hi), (w_hi, xT_lo), (w_lo, xT_hi))):
                            last = nc.tensor.matmul(psH[m % 4][:], w1(w[b], k, m), v[:, k, :], start=(k == 0 and n == 0),
                                                    stop=(k == KD - 1 and n == 2))
                    last.then_inc(h_ps, 1)
                pe.wait_ge(x_in, PRIMED + 16 * g + 32)
                transposes()
                pe.wait_ge(y_done, PRIMED + NH * g + 1)
                for n in range(NH):
                    for k in range(KF):
                        if n == 0:
                            pe.wait_ge(h_done, PRIMED + KF * g + k + 1)
                        for q, (v, w) in enumerate(((h_hi, w_hi), (h_lo, w_hi), (h_hi, w_lo))):
                            last = nc.tensor.matmul(psY[n][:], v[:, k, n * P:(n + 1) * P], w2(w[b], k),
                                                    start=(k == 0 and q == 0), stop=(k == KF - 1 and q == 2))
                last.then_inc(y_ps, 1)

            pe.wait_ge(ident_in, PRIMED + 16)
            pe.wait_ge(x_in, PRIMED + 16)
            transposes()
            for_units(pe, per_expert, per_unit)

        @block.scalar
        def _(act):
            def store(g):
                act.wait_ge(y_done, PRIMED + NH * g + 1)
                act.dma_start(results[bass.ds(nc.s_assert_within(g * U, 0, MOST * U, skip_runtime_bounds_check_because="g stays within the units counted"), U), :].rearrange("(n p) d -> p n d", p=P), y[:]).then_inc(y_out, 16)

            def per_expert(e, b, before, upto):
                wait_alone(act, bias_in[b], 8 * (e - b) + 16)

            def per_unit(e, b, t, g):
                for m in range(KF):
                    act.wait_ge(h_ps, PRIMED + KF * g + m + 1)
                    if m >= 4:
                        act.wait_ge(h_done, PRIMED + KF * g + m - 3)
                    nc.scalar.activation(h[:, m % 4], psH[m % 4][:], ACT.Relu, bias=bias[:, b, m:m + 1]).then_inc(h_act, 1)
                    if m == 3:
                        store(g)

            for_units(act, per_expert, per_unit)
            total = act.value_load(units[0:1, E + 1:E + 2], min_val=0, max_val=MOST)
            store(total)
            wait_alone(act, y_out, PRIMED + 16 * total + 16)

        @block.vector
        def _(dve):
            def transposed(g):
                dve.wait_ge(xT_ps, PRIMED + g + 1)
                nc.vector.tensor_copy(xT_hi[:], psT[:]).then_inc(xT_hi_done, 1)
                dve.wait_ge(xT_hi_done, PRIMED + g + 1)
                nc.vector.tensor_tensor(xT_lo[:], psT[:], xT_hi[:], ALU.subtract).then_inc(xT_done, 1)

            def per_expert(e, b, before, upto):
                wait_alone(dve, bias_in[b], 8 * (e - b) + 16)

            def per_unit(e, b, t, g):
                for m in range(KF):
                    dve.wait_ge(h_act, PRIMED + KF * g + m + 1)
                    nc.vector.tensor_copy(h_hi[:, m], h[:, m % 4]).then_inc(h_hi_done, 1)
                    dve.wait_ge(h_hi_done, PRIMED + KF * g + m + 1)
                    nc.vector.tensor_tensor(h_lo[:, m], h[:, m % 4], h_hi[:, m], ALU.subtract).then_inc(h_done, 1)
                transposed(g + 1)
                dve.wait_ge(y_ps, PRIMED + g + 1)
                dve.wait_ge(y_out, PRIMED + 16 * g + 16)
                for n in range(NH):
                    nc.vector.tensor_tensor(y[:, n], psY[n][:], bias[:, b, KF:], ALU.add).then_inc(y_done, 1)

            nc.vector.memset(y[:], 0.0).then_inc(y_done, 1)
            dve.wait_ge(ident_in, PRIMED + 16)
            transposed(0)
            for_units(dve, per_expert, per_unit)


def heads_phase(nc, x1_in, results, route, wkv3, wq, wp, bp_row, ident_dram, mask_dram, maskT_dram, x3_out,
                batches, ffn_weights, flag):
    T, D = x1_in.shape
    KD = D // P
    SEQ = T // batches
    NT = SEQ // P
    BANK = 512
    HALVES = SEQ // BANK
    PER = BANK // P
    HD = wkv3.shape[2] // 4
    HEADS = D // HD
    QB = 3
    HEADS_IN = [len(range(n, HEADS, QB)) for n in range(QB)]
    CHECK = ffn_weights.shape[1] // (batches * HEADS)
    SCALE = float(D) ** -0.5
    with ExitStack() as ctx:
        def sb(n, s, d=F32):
            return ctx.enter_context(nc.sbuf_tensor("m" + n, s, d))

        def psum(n, s):
            return ctx.enter_context(nc.psum_tensor("m" + n, s, F32))

        primed = []
        ctx.callback(nc.clear_and_free_semaphores, primed)

        def sem(n):
            primed.append(nc.alloc_semaphore("m" + n))
            return primed[-1]

        ident, ident_bf, mask_bf, maskT_bf = (sb(n, [P, P], d) for n, d in (
            ("ident", F32), ("ident_bf", BF16), ("mask_bf", BF16), ("maskT_bf", BF16)))
        wkv_raw = sb("wkv_raw", [P, KD, P])
        wkv_hi, wkv_lo = (sb(n, [P, KD, P], F32R) for n in ("wkv_hi", "wkv_lo"))
        wq_raw = sb("wq_raw", [P, KD, D])
        wq_hi, wq_lo = (sb(n, [P, KD, D], F32R) for n in ("wq_hi", "wq_lo"))
        q4_hi, q4_lo = (sb(n, [P, KD, SEQ], F32R) for n in ("q4_hi", "q4_lo"))
        wp_sb = sb("wp", [P, KD, D])
        bp = sb("bp", [P, D])
        x1 = sb("x1", [P, NT, D])
        y = [sb(f"y{c}", [P, NT, D]) for c in range(2)]
        x2 = sb("x2", [P, NT, D])
        res = sb("res", [P, NT, D])
        x2T_hi, x2T_lo = (sb(n, [P, KD, SEQ], F32R) for n in ("x2T_hi", "x2T_lo"))
        kvT = sb("kvT", [P, SEQ])
        k_rows = sb("k_rows", [P, SEQ], F32R)
        q_rows = [sb(f"q_rows{n}", [P, SEQ], F32R) for n in range(QB)]
        v1 = sb("v1", [P, NT, 2 * HD])
        prob = [sb(f"prob{n}", [P, BANK]) for n in range(3)]
        nmax = sb("nmax", [P, NT])
        nmT_hi, nmT_lo = (sb(n, [NT, P], F32R) for n in ("nmT_hi", "nmT_lo"))
        sums = sb("sums", [P, KD, SEQ])
        att = sb("att", [P, KD, SEQ])
        z = sb("z", [P, NT, D])
        st, stA = (sb(n, [P, NT, 6]) for n in ("st", "stA"))
        mv, mvA = (sb(n, [P, NT, 2]) for n in ("mv", "mvA"))
        rstd, var, tmp = (sb(n, [P, NT]) for n in ("rstd", "var", "tmp"))
        shifted = sb("shifted", [P, NT], I32)
        checked = sb("checked", [P, 2, CHECK])
        check_round = sb("check_round", [P, 2, CHECK], F32R)
        unequal = sb("unequal", [P, CHECK])
        miss = sb("miss", [P, HEADS])
        misses = sb("misses", [P, 1])
        missed = sb("missed", [P, 1])
        ones = sb("ones", [P, 1])
        rows_now = [sb(f"rows_now{c}", [P, NT], I32) for c in range(2)]
        weight_now = sb("weight_now", [P, 2, NT])
        unread = sb("unread", [1, 1])
        out_row = sb("out_row", [P, NT, D])
        S = [psum(f"S{n}", [P, SEQ]) for n in range(2)]
        ST = [psum(f"ST{n}", [P, BANK]) for n in range(2)]
        O = [psum(f"O{n}", [P, BANK]) for n in range(HALVES)]

        names = ("const_in setup padded x1_in rows_ready x2_done res_done t_ps t_hi t_lo kv_ps kv_sb k_hi k_lo v_ps "
                 "v_done q_ps q_hi q_lo s_ps mx nm_ps nm_hi nm_lo st_ps ex pv_ps o_used att_done pr_ps z_done chain x3_done "
                 "x3_st st_done stA_done "
                 "check_hi compared miss_done total_ps flag_done").split()
        (const_in, setup, padded, x1_ld, rows_ready, x2_done, res_done, t_ps, t_hi, t_lo, kv_ps, kv_sb, k_hi, k_lo, v_ps,
         v_done, q_ps, q_hi, q_lo, s_ps, mx, nm_ps, nm_hi, nm_lo, st_ps, ex, pv_ps, o_used, att_done, pr_ps, z_done, chain,
         x3_done, x3_st, st_done, stA_done, check_hi, compared, miss_done, total_ps, flag_done) = (sem(n) for n in names)
        y_in = [sem(f"y_in{t}") for t in range(NT)]
        nm_in = [sem(f"nm_in{n}") for n in range(QB)]
        q_in = [sem(f"q_in{n}") for n in range(QB)]
        check_in = [sem(f"check_in{n}") for n in range(2)]
        unwatched = {n.engine: sem(f"unwatched{q}") for q, n in
                     enumerate((nc.sync, nc.gpsimd, nc.tensor, nc.scalar, nc.vector))}
        loads = [(ident[:], ident_dram), (z[:, 0, :P], mask_dram), (z[:, 1, :P], maskT_dram), (wkv_raw[:], wkv3), (wq_raw[:], wq), (wp_sb[:], wp), (bp[:], bp_row)]
        N_CONST = 16 * len(loads)
        SETUP = 4
        PADDED = 3 + 2 * HALVES

        chunks = [(half, t) for half in range(HALVES) for t in range(PER * (half + 1))]
        NCH = len(chunks)
        TILES_AT = {1: (0, 1), 2: (2, 3), 3: (4, 5), 4: (6,), 5: (7,)}
        NORMALISE_AT = 6
        SCORES_AT = {0: (0, 1, 2), 1: (3, 4), 2: (5,), 3: (6,), 4: (7,)}
        MAX_AT = 6
        ROWS_AT = {0: 0, 1: 1}
        Q_AT = {3: 0, 5: 1}
        PIECE = SEQ // 4
        OUT_EARLY = 4
        assert HEADS == 8 and NT == 8

        by_gpsimd = [*y_in, *nm_in, *q_in]
        prime(nc, [s for s in primed if s not in by_gpsimd and s not in unwatched.values()])
        block = ctx.enter_context(nc.Block())

        def wait_alone(eng, semaphore, value):
            eng.wait_ge(semaphore, value)
            eng.sem_inc(unwatched[eng.engine], 1)

        def tokens(ap, b):
            return ap.rearrange("(b t p) d -> b p t d", t=NT, p=P)[b]

        def each_sequence(eng, body):
            body(0, False, True)
            with eng.Fori(1, batches - 1) as b:
                body(b, True, True)
            body(batches - 1, True, False)

        def of_head(b, h):
            return HEADS_IN[h % QB] * b + h // QB + 1

        @block.sync
        def _(sp):
            sp.dma_start(x1[:], tokens(x1_in, 0)).then_inc(x1_ld, 16)
            for d, s in loads:
                sp.dma_start(d, s).then_inc(const_in, 16)

            def store(b):
                sp.wait_ge(x3_done, PRIMED + b + 1)
                sp.dma_start(tokens(x3_out, b), out_row[:]).then_inc(x3_st, 16)

            def sequence(b, earlier, more):
                if more:
                    sp.wait_ge(x2_done, PRIMED + b + 1)
                    sp.dma_start(x1[:], tokens(x1_in, b + 1)).then_inc(x1_ld, 16)
                for h in range(HEADS):
                    n = HEADS * b + h
                    if earlier or h >= 2:
                        sp.wait_ge(compared, PRIMED + n - 1)
                    sp.dma_start(checked[:, h % 2], ffn_weights[:, bass.ds(n * CHECK, CHECK)]).then_inc(check_in[h % 2], 16)
                    if earlier and h == 3:
                        store(b - 1)

            each_sequence(sp, sequence)
            store(batches - 1)
            sp.wait_ge(x3_st, PRIMED + 16 * batches)

        @block.gpsimd
        def _(pool):
            def gather(t):
                for c in range(2):
                    pool.indirect_dma_start(out=y[c][:, t, :], out_offset=None, in_=results,
                                            in_offset=bass.IndirectOffsetOnAxis(ap=rows_now[c][:, t:t + 1], axis=0)
                                            ).then_inc(y_in[t], 16)

            pool.wait_ge(rows_ready, PRIMED + 1)
            for t in range(NT):
                gather(t)
            pool.wait_ge(const_in, PRIMED + N_CONST)
            pool.wait_ge(padded, PRIMED + PADDED)

            def stack(b, h, earlier=True):
                if h >= QB:
                    wait_alone(pool, st_ps, PRIMED + NCH * (HEADS * b + h - QB + 1))
                elif earlier:
                    wait_alone(pool, st_ps, PRIMED + NCH * (HEADS * (b - 1) + QB * (HEADS_IN[h] - 1) + h + 1))
                rows = slice(h % PER * HD, (h % PER + 1) * HD)
                for r, part in enumerate((q4_hi, q4_hi, q4_lo)):
                    pool.dma_start(q_rows[h % QB][r * HD:(r + 1) * HD, :], part[rows, h // PER, :]).then_inc(q_in[h % QB], 16)

            def sequence(b, earlier, more):
                if not earlier:
                    pool.wait_ge(q_lo, PRIMED + 1)
                    stack(b, 0, False)
                    stack(b, 1, False)
                for h in range(HEADS):
                    n = HEADS * b + h
                    for r, (row, ready) in enumerate(((nmT_hi, nm_hi), (nmT_lo, nm_lo))):
                        wait_alone(pool, ready, PRIMED + n + 1)
                        pool.dma_start(q_rows[h % QB][3 * HD + r:3 * HD + r + 1, :].rearrange("o (t q) -> o t q", q=P),
                                       row[:]).then_inc(nm_in[h % QB], 16)
                    if h + 2 < HEADS:
                        if h + 2 == PER:
                            wait_alone(pool, q_lo, PRIMED + KD * b + 2)
                        stack(b, h + 2, earlier)
                    if h == 0:
                        pool.wait_ge(z_done, PRIMED + NT * b)
                        pool.wait_ge(x2_done, PRIMED + b + 1)
                        nc.gpsimd.tensor_tensor(res[:], x2[:], bp[:].unsqueeze(1).to_broadcast([P, NT, D]),
                                                ALU.add).then_inc(res_done, 1)
                    if more and h < 4:
                        if h == 0:
                            wait_alone(pool, rows_ready, PRIMED + b + 2)
                        gather(2 * h)
                        gather(2 * h + 1)
                if more:
                    wait_alone(pool, q_lo, PRIMED + KD * (b + 1) + 1)
                    stack(b + 1, 0)
                    stack(b + 1, 1)

            each_sequence(pool, sequence)
            for n in range(QB):
                pool.wait_ge(nm_in[n], 32 * of_head(batches - 1, HEADS - QB + (n - HEADS) % QB))

        @block.tensor
        def _(pe):
            def three(ps, left, right, first, last):
                (lh, ll), (rh, rl) = left, right
                nc.tensor.matmul(ps, lh, rh, start=first, stop=False)
                nc.tensor.matmul(ps, lh, rl, start=False, stop=False)
                return nc.tensor.matmul(ps, ll, rh, start=False, stop=last)

            def bank(n):
                return slice(n * BANK, (n + 1) * BANK)

            def tile(n):
                return slice(n * P, (n + 1) * P)

            def project_q(b, g):
                pe.wait_ge(t_lo, PRIMED + KD * (b + 1))
                for c in range(HALVES):
                    for k in range(KD):
                        last = three(S[g][:, bank(c)], (wq_hi[:, k, tile(g)], wq_lo[:, k, tile(g)]),
                                     (x2T_hi[:, k, bank(c)], x2T_lo[:, k, bank(c)]), k == 0, k == KD - 1)
                last.then_inc(q_ps, 1)

            def scores(b, h, i):
                n = HEADS * b + h
                if i == 0:
                    if h:
                        pe.wait_ge(nm_lo, PRIMED + n)
                    else:
                        pe.wait_ge(q_lo, PRIMED + KD * (b + 1))
                        pe.wait_ge(k_lo, PRIMED + HALVES * (b + 1))
                    pe.wait_ge(q_in[h % QB], 48 * of_head(b, h))
                elif i >= 2 or h:
                    pe.wait_ge(mx, PRIMED + NT * n + i - 1)
                s = S[i % 2]
                width = (i + 1) * P
                for c in range(0, width, BANK):
                    c1 = min(width, c + BANK)
                    nc.tensor.matmul(s[:, c:c1], q_rows[h % QB][:3 * HD, tile(i)], k_rows[:3 * HD, c:c1], start=True, stop=True)
                nc.tensor.matmul(s[:, i * P:width], ident_bf[:], mask_bf[:], start=False, stop=True,
                                 skip_group_check=True).then_inc(s_ps, 1)

            def transpose_max(b, h):
                n = HEADS * b + h
                pe.wait_ge(mx, PRIMED + NT * (n + 1))
                nc.tensor.transpose(S[0][:NT, :P], nmax[:], ident[:]).then_inc(nm_ps, 1)

            def scores_T(b, h, c):
                n = HEADS * b + h
                half, t = chunks[c]
                if c == 0:
                    pe.wait_ge(nm_in[h % QB], 32 * of_head(b, h))
                if h == 0 and c < 2:
                    pe.wait_ge(v_done, PRIMED + 2 * (b + 1))
                else:
                    pe.wait_ge(ex, PRIMED + NCH * n + c - 1)
                off = max(0, t - PER * half) * P
                last = nc.tensor.matmul(ST[c % 2][:, off:], k_rows[:, tile(t)],
                                        q_rows[h % QB][:, half * BANK + off:(half + 1) * BANK], start=True, stop=True)
                if t >= PER * half:
                    last = nc.tensor.matmul(ST[c % 2][:, off:off + P], ident_bf[:], maskT_bf[:], start=False, stop=True,
                                            skip_group_check=True)
                last.then_inc(st_ps, 1)

            def weigh(b, h, c):
                n = HEADS * b + h
                half, t = chunks[c]
                if t == 0 and h == 0:
                    pe.wait_ge(z_done, PRIMED + NT * b)
                if t == 0 and h:
                    pe.wait_ge(o_used, PRIMED + HALVES * (n - 1) + half + 1)
                pe.wait_ge(ex, PRIMED + NCH * n + c + 1)
                off = max(0, t - PER * half) * P
                nc.tensor.matmul(O[half][:2 * HD, off:], v1[:, t, :], prob[c % 3][:, off:], start=(t == 0), stop=True,
                                 skip_group_check=(t > 0)).then_inc(pv_ps, 1)

            pe.wait_ge(const_in, PRIMED + N_CONST)
            pe.wait_ge(setup, PRIMED + SETUP)
            pe.wait_ge(padded, PRIMED + PADDED)

            def transpose_rows(b, k):
                pe.wait_ge(x2_done, PRIMED + b + 1)
                for t in range(NT):
                    last = nc.tensor.transpose(S[k][:, tile(t)], x2[:, t, tile(k)], ident[:])
                last.then_inc(t_ps, 1)

            def project_out(b, i):
                if i % 2 == 0:
                    pe.wait_ge(att_done, PRIMED + 8 * b + 4 + i // 2 + 1)
                if i >= 2:
                    pe.wait_ge(z_done, PRIMED + NT * b + i - 1)
                for k in range(KD):
                    last = nc.tensor.matmul(O[i % 2][:, :D], att[:, k, tile(i)], wp_sb[:, k, :], start=(k == 0),
                                            stop=(k == KD - 1))
                last.then_inc(pr_ps, 1)

            def sequence(b, earlier, more):
                if not earlier:
                    for k in range(KD):
                        transpose_rows(b, k)
                    for g in range(KD):
                        project_q(b, g)
                pe.wait_ge(o_used, PRIMED + HALVES * HEADS * b)
                for c in range(HALVES):
                    for k in range(KD):
                        last = three(O[c][:], (wkv_hi[:, k, :], wkv_lo[:, k, :]),
                                     (x2T_hi[:, k, bank(c)], x2T_lo[:, k, bank(c)]), k == 0, k == KD - 1)
                    last.then_inc(kv_ps, 1)
                pe.wait_ge(ex, PRIMED + NCH * HEADS * b)
                for c in range(HALVES):
                    pe.wait_ge(kv_sb, PRIMED + HALVES * b + c + 1)
                    for n in range(PER):
                        last = nc.tensor.transpose(ST[c][:, tile(n)], kvT[:, tile(PER * c + n)], ident[:])
                    last.then_inc(v_ps, 1)
                for i in range(NT):
                    scores(b, 0, i)
                    if earlier and i < OUT_EARLY:
                        project_out(b - 1, i)
                transpose_max(b, 0)
                if earlier:
                    for i in range(OUT_EARLY, NT):
                        project_out(b - 1, i)
                for h in range(HEADS):
                    scores_T(b, h, 0)
                    for c in range(NCH):
                        if c + 1 < NCH:
                            scores_T(b, h, c + 1)
                        if h + 1 < HEADS:
                            for i in SCORES_AT.get(c, ()):
                                scores(b, h + 1, i)
                            if c == MAX_AT:
                                transpose_max(b, h + 1)
                        elif more:
                            if c == 0:
                                pe.wait_ge(nm_lo, PRIMED + HEADS * (b + 1))
                            if c in ROWS_AT:
                                transpose_rows(b + 1, ROWS_AT[c])
                            if c in Q_AT:
                                project_q(b + 1, Q_AT[c])
                        weigh(b, h, c)
            each_sequence(pe, sequence)
            pe.wait_ge(o_used, PRIMED + HALVES * HEADS * batches)
            for i in range(NT):
                project_out(batches - 1, i)
            pe.wait_ge(miss_done, PRIMED + 2 * batches)
            nc.tensor.matmul(ST[0][:1, :1], misses[:], ones[:], start=True, stop=True).then_inc(total_ps, 1)

        @block.scalar
        def _(act):
            act.wait_ge(const_in, PRIMED + N_CONST)
            nc.scalar.activation(wkv_hi[:], wkv_raw[:], ACT.Copy).then_inc(setup, 1)
            nc.scalar.activation(wq_hi[:], wq_raw[:], ACT.Copy).then_inc(setup, 1)

            def copy_out(b, h, half):
                act.wait_ge(pv_ps, PRIMED + NCH * (HEADS * b + h) + PER + half * (NCH - PER))
                rows = slice(h % PER * HD, (h % PER + 1) * HD)
                cols = slice(half * BANK, (half + 1) * BANK)
                if h == 0 and half == 0:
                    act.wait_ge(pr_ps, PRIMED + NT * b)
                nc.scalar.activation(att[rows, h // PER, cols], O[half][:HD, :], ACT.Copy)
                nc.scalar.activation(sums[rows, h // PER, cols], O[half][HD:2 * HD, :], ACT.Copy).then_inc(o_used, 1)

            def rows_high(b, k):
                act.wait_ge(t_ps, PRIMED + KD * b + k + 1)
                nc.scalar.activation(x2T_hi[:, k, :], S[k][:], ACT.Copy).then_inc(t_hi, 1)

            def q_high(b, g):
                act.wait_ge(q_ps, PRIMED + KD * b + g + 1)
                nc.scalar.activation(q4_hi[:, g, :], S[g][:], ACT.Copy, scale=SCALE).then_inc(q_hi, 1)

            def check(b, h, earlier):
                n = HEADS * b + h
                act.wait_ge(check_in[h % 2], PRIMED + HEADS // 2 * 16 * b + 16 * (h // 2 + 1))
                if earlier or h >= 2:
                    act.wait_ge(compared, PRIMED + n - 1)
                nc.scalar.activation(check_round[:, h % 2], checked[:, h % 2], ACT.Copy).then_inc(check_hi, 1)

            def sequence(b, earlier, more):
                if not earlier:
                    for k in range(KD):
                        rows_high(b, k)
                    for g in range(KD):
                        q_high(b, g)
                for c in range(HALVES):
                    act.wait_ge(kv_ps, PRIMED + HALVES * b + c + 1)
                    cols = slice(c * BANK, (c + 1) * BANK)
                    nc.scalar.activation(k_rows[:3 * HD, cols], O[c][:3 * HD, :], ACT.Copy).then_inc(k_hi, 1)
                    nc.scalar.activation(kvT[:, cols], O[c][:], ACT.Copy).then_inc(kv_sb, 1)
                for h in range(HEADS):
                    n = HEADS * b + h
                    for c, (half, t) in enumerate(chunks):
                        off = max(0, t - PER * half) * P
                        act.wait_ge(st_ps, PRIMED + NCH * n + c + 1)
                        if h or c >= 3:
                            act.wait_ge(pv_ps, PRIMED + NCH * n + c - 2)
                        nc.scalar.activation(prob[c % 3][:, off:], ST[c % 2][:, off:], ACT.Exp).then_inc(ex, 1)
                        if c == 1 and h:
                            copy_out(b, h - 1, 1)
                        if c == PER + 2:
                            copy_out(b, h, 0)
                        if c == PER + 4:
                            check(b, h, earlier)
                        if more and h == HEADS - 1:
                            if c - 1 in ROWS_AT:
                                rows_high(b + 1, ROWS_AT[c - 1])
                            if c - 2 in Q_AT:
                                q_high(b + 1, Q_AT[c - 2])
                copy_out(b, HEADS - 1, 1)

            each_sequence(act, sequence)

        @block.vector
        def _(dve):
            n_link = [0]
            base = [0]

            def link(ins, alone=False):
                n_link[0] += 1
                ins.then_inc(chain, 1)
                (wait_alone if alone else lambda e, s, v: e.wait_ge(s, v))(dve, chain, PRIMED + base[0] + n_link[0])

            def normalised(dst, src, stats, mean_var, done, first=0, end=NT):
                part = slice(first, end)
                for i in range(first, end):
                    ins = nc.vector.bn_aggr(mean_var[:, i], stats[:, i])
                link(ins)
                link(nc.vector.tensor_copy(var[:, part], mean_var[:, part, 1]))
                rsqrt(nc, link, rstd[:, part], var[:, part], tmp[:, part], shifted[:, part])
                if dst is out_row:
                    dve.wait_ge(x3_st, PRIMED + 16 * seq[0])
                for i in range(first, end):
                    ins = nc.vector.tensor_scalar(dst[:, i], src[:, i], mean_var[:, i, 0:1], rstd[:, i:i + 1], ALU.subtract,
                                                  ALU.mult)
                if end == NT:
                    ins.then_inc(done, 1)

            seq = [0]

            def plan(n):
                cols = bass.ds(n * NT, NT)
                for c in range(2):
                    link(nc.vector.tensor_copy(rows_now[c][:], route["row"][c][:, cols]))
                    link(nc.vector.tensor_copy(weight_now[:, c], route["weight"][c][:, cols]))
                nc.vector.memset(unread[:], 0.0).then_inc(rows_ready, 1)

            def residual(n, t):
                dve.wait_ge(y_in[t], 32 * (n + 1))
                link(nc.vector.scalar_tensor_tensor(x2[:, t], y[0][:, t], weight_now[:, 0, t:t + 1], x1[:, t], ALU.mult, ALU.add))
                link(nc.vector.scalar_tensor_tensor(x2[:, t], y[1][:, t], weight_now[:, 1, t:t + 1], x2[:, t], ALU.mult, ALU.add))
                nc.vector.bn_stats(stA[:, t], x2[:, t]).then_inc(stA_done, 1)

            plan(0)
            nc.vector.memset(prob[0][:], 0.0).then_inc(padded, 1)
            nc.vector.memset(prob[1][:], 1.0).then_inc(padded, 1)
            dve.wait_ge(padded, PRIMED + 2)
            rows = slice(3 * HD, 4 * HD)
            for n in range(HALVES):
                cols = slice(n * BANK, (n + 1) * BANK)
                for m in range(QB):
                    nc.vector.tensor_copy(q_rows[m][rows, cols], prob[0][rows, :])
                nc.vector.tensor_copy(k_rows[rows, cols], prob[0][rows, :]).then_inc(padded, 1)
            dve.wait_ge(padded, PRIMED + 2 + HALVES)
            for n in range(HALVES):
                nc.vector.tensor_copy(k_rows[3 * HD:3 * HD + 2, n * BANK:(n + 1) * BANK],
                                      prob[1][3 * HD:3 * HD + 2, :]).then_inc(padded, 1)
            nc.vector.memset(ones[:], 1.0)
            nc.vector.memset(misses[:], 0.0)
            nc.vector.memset(v1[:], 1.0).then_inc(padded, 1)
            dve.wait_ge(const_in, PRIMED + N_CONST)
            nc.vector.tensor_copy(ident_bf[:], ident[:])
            nc.vector.tensor_copy(mask_bf[:], z[:, 0, :P])
            nc.vector.tensor_copy(maskT_bf[:], z[:, 1, :P])
            dve.wait_ge(setup, PRIMED + 2)
            nc.vector.tensor_tensor(wkv_lo[:], wkv_raw[:], wkv_hi[:], ALU.subtract).then_inc(setup, 1)
            nc.vector.tensor_tensor(wq_lo[:], wq_raw[:], wq_hi[:], ALU.subtract).then_inc(setup, 1)
            dve.wait_ge(x1_ld, PRIMED + 16)
            for first in (0, NT // 2):
                for t in range(first, first + NT // 2):
                    residual(0, t)
                dve.wait_ge(stA_done, PRIMED + first + NT // 2)
                normalised(x2, x2, stA, mvA, x2_done, first, first + NT // 2)
            first_links = n_link[0]
            dve.wait_ge(x2_done, PRIMED + 1)

            def rows_low(b, k):
                dve.wait_ge(t_hi, PRIMED + KD * b + k + 1)
                nc.vector.tensor_tensor(x2T_lo[:, k, :], S[k][:], x2T_hi[:, k, :], ALU.subtract).then_inc(t_lo, 1)

            def q_low(b, g):
                dve.wait_ge(q_hi, PRIMED + KD * b + g + 1)
                nc.vector.scalar_tensor_tensor(q4_lo[:, g, :], S[g][:], SCALE, q4_hi[:, g, :], ALU.mult,
                                               ALU.subtract).then_inc(q_lo, 1)

            def compare(b, h):
                n = HEADS * b + h
                dve.wait_ge(check_hi, PRIMED + n + 1)
                dve.wait_ge(compared, PRIMED + n)
                nc.vector.scalar_tensor_tensor(unequal[:], checked[:, h % 2], 1.0, check_round[:, h % 2], ALU.mult,
                                               ALU.not_equal, accum_out=miss[:, h:h + 1]).then_inc(compared, 1)

            def output(b, i):
                dve.wait_ge(pr_ps, PRIMED + NT * b + i + 1)
                if i == 0:
                    dve.wait_ge(res_done, PRIMED + b + 1)
                    dve.wait_ge(x3_done, PRIMED + b)
                nc.vector.tensor_tensor(z[:, i], O[i % 2][:, :D], res[:, i], ALU.add).then_inc(z_done, 1)

            def output_stats(b, i):
                dve.wait_ge(z_done, PRIMED + NT * b + i + 1)
                nc.vector.bn_stats(st[:, i], z[:, i]).then_inc(st_done, 1)

            def sum_misses(b):
                dve.wait_ge(compared, PRIMED + HEADS * (b + 1))
                nc.vector.reduce_sum(missed[:], miss[:], X).then_inc(miss_done, 1)
                dve.wait_ge(miss_done, PRIMED + 2 * b + 1)
                nc.vector.tensor_tensor(misses[:], misses[:], missed[:], ALU.add).then_inc(miss_done, 1)
                dve.wait_ge(miss_done, PRIMED + 2 * b + 2)

            def row_max(b, h, i):
                dve.wait_ge(s_ps, PRIMED + NT * (HEADS * b + h) + i + 1)
                nc.vector.tensor_reduce(nmax[:, i:i + 1], S[i % 2][:, :(i + 1) * P], X, ALU.max, negate=True).then_inc(mx, 1)

            def max_rows(b, h):
                n = HEADS * b + h
                dve.wait_ge(nm_ps, PRIMED + n + 1)
                if h:
                    dve.wait_ge(nm_in[(h - 1) % QB], 32 * of_head(b, h - 1))
                nc.vector.tensor_copy(nmT_hi[:], S[0][:NT, :P]).then_inc(nm_hi, 1)
                dve.wait_ge(nm_hi, PRIMED + n + 1)
                nc.vector.tensor_tensor(nmT_lo[:], S[0][:NT, :P], nmT_hi[:], ALU.subtract).then_inc(nm_lo, 1)

            def normalise(b, group, piece):
                if piece % 2 == 0:
                    dve.wait_ge(o_used, PRIMED + HALVES * (HEADS * b + PER * group + PER - 1) + piece // 2 + 1)
                cols = slice(piece * PIECE, (piece + 1) * PIECE)
                link(nc.vector.reciprocal(sums[:, group, cols], sums[:, group, cols]))
                nc.vector.tensor_tensor(att[:, group, cols], att[:, group, cols], sums[:, group, cols],
                                        ALU.mult).then_inc(att_done, 1)

            def sequence(b, earlier, more):
                n_link[0] = 0
                base[0] = first_links + FIRST + LINKS * (b - 1) if earlier else first_links
                seq[0] = b - 1
                if not earlier:
                    for k in range(KD):
                        rows_low(b, k)
                    for g in range(KD):
                        q_low(b, g)
                part = slice(HD, 2 * HD)
                for c in range(HALVES):
                    cols = slice(c * BANK, (c + 1) * BANK)
                    dve.wait_ge(k_hi, PRIMED + HALVES * b + c + 1)
                    dve.wait_ge(kv_sb, PRIMED + HALVES * b + c + 1)
                    nc.vector.tensor_tensor(k_rows[part, cols], O[c][part, :], k_rows[part, cols],
                                            ALU.subtract).then_inc(k_lo, 1)
                if earlier:
                    normalise(b - 1, 1, 2)
                for c in range(HALVES):
                    dve.wait_ge(v_ps, PRIMED + HALVES * b + c + 1)
                    nc.vector.tensor_copy(v1[:, PER * c:PER * (c + 1), :HD],
                                          ST[c][:].rearrange("p (t s) -> p t s", s=P)[:, :, 3 * HD:]).then_inc(v_done, 1)
                for i in range(NT):
                    row_max(b, 0, i)
                    if earlier and i < OUT_EARLY:
                        output(b - 1, i)
                max_rows(b, 0)
                if earlier:
                    normalise(b - 1, 1, 3)
                    for i in range(OUT_EARLY, NT):
                        output(b - 1, i)
                if more:
                    plan(b + 1)
                for h in range(HEADS):
                    following = h + 1 < HEADS
                    if following:
                        for i in range(NT):
                            row_max(b, h + 1, i)
                        max_rows(b, h + 1)
                    if earlier and h == 0:
                        for i in range(NT):
                            output_stats(b - 1, i)
                        wait_alone(dve, st_done, PRIMED + NT * b)
                        normalised(out_row, z, st, mv, x3_done)
                    if more and h in TILES_AT:
                        if h == min(TILES_AT):
                            dve.wait_ge(x1_ld, PRIMED + 16 * (b + 2))
                            dve.wait_ge(res_done, PRIMED + b + 1)
                        for t in TILES_AT[h]:
                            residual(b + 1, t)
                    if more and h == NORMALISE_AT:
                        wait_alone(dve, stA_done, PRIMED + NT * (b + 2))
                        normalised(x2, x2, stA, mvA, x2_done)
                        dve.wait_ge(x2_done, PRIMED + b + 2)
                    if more and h == HEADS - 1:
                        for k in range(KD):
                            rows_low(b + 1, k)
                    if PER <= h < 2 * PER:
                        normalise(b, 0, h - PER)
                    if more and h == HEADS - 1:
                        for g in range(KD):
                            q_low(b + 1, g)
                    if h == HEADS - 1:
                        normalise(b, 1, 0)
                        normalise(b, 1, 1)
                    compare(b, h)
                sum_misses(b)
                assert n_link[0] == (LINKS if more and earlier else FIRST if more else LAST), n_link[0]

            LINKS = 4 + 2 * NT + 8 + 2 * (2 + RSQRT_LINKS)
            FIRST = LINKS - 2 - (2 + RSQRT_LINKS)
            LAST = LINKS - (4 + 2 * NT + 2 + RSQRT_LINKS)
            each_sequence(dve, sequence)
            n_link[0] = 0
            base[0] = first_links + FIRST + (batches - 2) * LINKS + LAST
            b = batches - 1
            for piece in range(2, 4):
                normalise(b, 1, piece)
            for i in range(NT):
                output(b, i)
                output_stats(b, i)
            dve.wait_ge(st_done, PRIMED + NT * batches)
            seq[0] = b
            normalised(out_row, z, st, mv, x3_done)
            dve.wait_ge(total_ps, PRIMED + 1)
            nc.vector.tensor_scalar(flag[0:1, 0:1], ST[0][:1, :1], 0.0, None, ALU.is_gt).then_inc(flag_done, 1)
            dve.wait_ge(flag_done, PRIMED + 1)


def model_program(nc, t, out):
    T, D = t["x"].shape
    batches = t["xT"].shape[0]
    experts = t["expert_weights"].shape[0]
    tiles = T // P
    capacity = T + UNIT
    most_units = (2 * T) // UNIT + experts - 1
    x1, x3 = (nc.dram_tensor(n, [T, D], F32, kind="Internal").ap() for n in ("x1_dram", "x3_dram"))
    slots = nc.dram_tensor("slots_dram", [experts * capacity, D], F32, kind="Internal").ap()
    results = nc.dram_tensor("results_dram", [(most_units + 1) * UNIT, D], F32, kind="Internal").ap()
    with ExitStack() as ctx:
        def sb(n, s, d=F32):
            return ctx.enter_context(nc.sbuf_tensor(n, s, d))

        weights_inexact = sb("weights_inexact", [1, 1], I32)
        with ExitStack() as routing:
            def rsb(n, s, d=F32):
                return routing.enter_context(nc.sbuf_tensor(n, s, d))

            units = rsb("units", [1, experts + 2], I32)
            route = dict(weight=[rsb(f"weight{c}", [P, tiles]) for c in range(2)],
                         row=[rsb(f"row{c}", [P, tiles], I32) for c in range(2)])
            with ExitStack() as first:
                columns = t["expert_weights"].shape[2]
                first_expert = [first.enter_context(nc.sbuf_tensor(f"first_expert{n}", [P, columns], d))
                                for n, d in enumerate((F32, F32R, F32R))]
                with ExitStack() as counting:
                    def csb(n, s):
                        return counting.enter_context(nc.sbuf_tensor(n, s, F32))

                    route.update(rank=[csb(f"rank{c}", [P, tiles]) for c in range(2)],
                                 onehot=[csb(f"onehot{c}", [P, tiles, experts]) for c in range(2)],
                                 count=csb("count", [P, experts]))
                    attend_and_route_phase(nc, t["x"], t["xT"], t["wqT"], t["wkT"], t["wvT"], t["wo"], t["w_router"],
                                           t["b_router"], t, route, x1, slots, batches, capacity, units, t["unit_starts"],
                                           results, first_expert, t["expert_weights"])
                moe_phase(nc, units, first_expert, slots, t["expert_weights"], t["expert_biases"], results, t["ident"],
                          capacity, T)
            heads_phase(nc, x1, results, route, t["wkv"], t["wq"], t["wp"], t["bp"], t["ident"], t["mask"], t["maskT"], x3,
                        batches, t["ffn_weights"], weights_inexact)
        for split in (True, False):
            ffn_phase(nc, weights_inexact, x3, t["ffn_weights"], t["ffn_scales"], t["w3_scales"], out,
                      t["ident"], split)


def kernel(**inputs):
    import numpy as np
    import concourse.bacc as bacc
    from concourse.bass_utils import run_bass_kernel_spmd

    a = {n: np.asarray(v) for n, v in inputs.items()}
    f32 = np.float32
    B, S, D = a["L0_attn_x"].shape
    E, _, F = a["L0_ffn_W1"].shape

    def rows(w):
        return w.reshape(-1, P, *w.shape[1:]).swapaxes(0, 1)

    def on_all(v):
        return np.broadcast_to(v, (P, v.shape[0]))

    def by_block(v):
        return v.reshape(-1, P).T

    square = np.ones((P, P), f32)
    Wk, Wv, Wq = a["L1_attn_Wk"], a["L1_attn_Wv"], a["L1_attn_Wq"]
    data = {
        "x": a["L0_attn_x"].reshape(B * S, D),
        "xT": a["L0_attn_x"].reshape(B, S, D // P, P).transpose(0, 3, 2, 1),
        "wqT": rows(a["L0_attn_Wq"].T), "wkT": rows(a["L0_attn_Wk"].T), "wvT": rows(a["L0_attn_Wv"].T),
        "wo": rows(a["L0_attn_Wo"]),
        "w_router": rows(a["L0_ffn_W_router"]), "b_router": on_all(a["L0_ffn_b_router"]),
        "expert_weights": np.concatenate([
            a["L0_ffn_W1"].reshape(E, D // P, P, F).transpose(0, 2, 1, 3).reshape(E, P, -1),
            a["L0_ffn_W2"].reshape(E, F // P, P, D).transpose(0, 2, 1, 3).reshape(E, P, -1)], 2),
        "expert_biases": np.concatenate([
            a["L0_ffn_b1"].reshape(E, F // P, P).transpose(0, 2, 1),
            np.broadcast_to(a["L0_ffn_b2"][:, None], (E, P, D))], 2),
        "wkv": rows(np.concatenate([Wk, Wk, Wk, Wv], 1)),
        "wq": rows(Wq.transpose(1, 0, 2).reshape(D, -1)),
        "wp": rows(a["L1_attn_Wp"]), "bp": on_all(a["L1_attn_bp"]),
        "ffn_weights": np.concatenate([rows(a[f"L1_ffn_{n}_w"].T).reshape(P, -1) for n in ("w1", "w2", "h1", "h2", "w3")], 1),
        "ffn_scales": np.stack([by_block(a[f"L1_ffn_{n}_s"]) for n in ("w1", "w2", "h1", "h2")], 1),
        "w3_scales": on_all(a["L1_ffn_w3_s"]),
        "ident": np.eye(P, dtype=f32), "mask": np.triu(square, 1) * f32(-1e30), "maskT": np.tril(square, -1) * f32(-1e30),
        "before_me": np.triu(square, 1), "all_ones": square, "iota_e": on_all(np.arange(E, dtype=f32)),
        "unit_starts": on_all(np.arange(0, B * S, UNIT, dtype=f32)),
    }
    nc = bacc.Bacc("TRN2", target_bir_lowering=False, num_devices=1)
    arrays = {n + "_dram": np.ascontiguousarray(v) for n, v in data.items()}
    t = {n[:-5]: nc.dram_tensor(n, v.shape, mybir.dt.from_np(v.dtype), kind="ExternalInput").ap()
         for n, v in arrays.items()}
    out = nc.dram_tensor("out_dram", [B * S, D], F32, kind="ExternalOutput").ap()
    model_program(nc, t, out)
    result = run_bass_kernel_spmd(nc, [arrays], core_ids=[0])
    return result.results[0]["out_dram"].reshape(B, S, D)
```
